# Optimizing a Trainium2 kernel written in Bass

```python
import numpy as np
import jax
import jax.numpy as jnp

def _softmax(x, axis=-1):
    return jax.nn.softmax(x, axis=axis)

def _gelu(x):
    return jax.nn.gelu(x, approximate=True)

def _silu(x):
    return jax.nn.silu(x)

def _sigmoid(x):
    return jax.nn.sigmoid(x)

def _layernorm(x, axis=-1, eps=1e-05):
    m = jnp.mean(x, axis=axis, keepdims=True)
    v = jnp.var(x, axis=axis, keepdims=True)
    return (x - m) / jnp.sqrt(v + eps)

def _scatter_add(tgt, idx, src, axis=0):
    return tgt.at[idx].add(src)

def _segment_sum(src, seg, n):
    return jax.ops.segment_sum(src, seg, n)
kernel_name = 'mk_vit_tower_cls_d1_tok_img512_r4_df463e'

def setup_inputs(seed: int=0):
    np.random.seed(seed)
    _w = jnp.asarray

    def _rec_inputs():
        import jax
        import jax.numpy as jnp
        _rk = jax.random.key(seed)
        x = -0.000392918 + 0.999932 * jax.random.normal(jax.random.fold_in(_rk, 1), (16, 1, 128, 128), jnp.float32)
        cls_tok = 0.02 * jax.random.normal(jax.random.fold_in(_rk, 5), (1, 1, 128), jnp.float32)
        return (x, cls_tok)
    x, cls_tok = _rec_inputs()

    def _L0_tok_setup():
        import math
        import jax, jax.numpy as jnp
        import numpy as np
        PW = PH = 16
        EMB = 128
        HID = 128
        B, H, W = (64, 128, 128)
        L = H // PW * (W // PH)
        SIGMA_ZERO = 0.1

        def _f_noise(x):
            return jnp.sign(x) * jnp.sqrt(jnp.abs(x))

        def _noisy_linear(x, w, b, sw, sb, eps_in, eps_out):
            ei = _f_noise(eps_in)
            eo = _f_noise(eps_out)
            w_n = w + sw * (eo[:, None] * ei[None, :])
            b_n = b + sb * eo
            return x @ w_n.T + b_n

        def _unfold_patches(x):
            b = x.shape[0]
            p = x.reshape(b, H // PW, PW, W // PH, PH)
            p = p.transpose(0, 1, 3, 2, 4)
            return p.reshape(b, L, PW * PH)

        def _pos_encoding(x):
            pos = jnp.arange(L, dtype=jnp.float32)[:, None]
            div = jnp.exp(jnp.arange(0, EMB, 2, dtype=jnp.float32) * (-math.log(10000.0) / EMB))
            ang = pos * div
            pe = jnp.stack([jnp.sin(ang), jnp.cos(ang)], axis=-1).reshape(L, EMB)
            return x + pe[None, :, :]
        key = jax.random.key(seed)
        ks = jax.random.split(key, 12)
        in_f = PW * PH
        sig = SIGMA_ZERO / math.sqrt(in_f)
        bnd1 = 1.0 / math.sqrt(in_f)
        bnd3 = 1.0 / math.sqrt(HID)
        u = lambda k, shape, bnd: jax.random.uniform(k, shape, jnp.float32, -bnd, bnd)
        return {'inputs': jax.random.normal(ks[0], (B, 1, H, W), jnp.float32), 'W1_w': u(ks[1], (HID, in_f), bnd1), 'W1_b': u(ks[2], (HID,), bnd1), 'W1_sw': jnp.full((HID, in_f), sig, jnp.float32), 'W1_sb': jnp.full((HID,), sig, jnp.float32), 'W2_w': u(ks[3], (HID, in_f), bnd1), 'W2_b': u(ks[4], (HID,), bnd1), 'W2_sw': jnp.full((HID, in_f), sig, jnp.float32), 'W2_sb': jnp.full((HID,), sig, jnp.float32), 'W3_w': u(ks[5], (EMB, HID), bnd3), 'W3_b': u(ks[6], (EMB,), bnd3), 'eps_in1': jax.random.normal(ks[7], (in_f,), jnp.float32), 'eps_out1': jax.random.normal(ks[8], (HID,), jnp.float32), 'eps_in2': jax.random.normal(ks[9], (in_f,), jnp.float32), 'eps_out2': jax.random.normal(ks[10], (HID,), jnp.float32)}
    _L0_tok_all = _L0_tok_setup()
    _L0_tok_in = {k: v for k, v in _L0_tok_all.items() if k in ('W1_w', 'W1_b', 'W1_sw', 'W1_sb', 'W2_w', 'W2_b', 'W2_sw', 'W2_sb', 'W3_w', 'W3_b', 'eps_in1', 'eps_out1', 'eps_in2', 'eps_out2')}
    del _L0_tok_all

    def _L0_attn_setup():
        import jax, jax.numpy as jnp
        import numpy as np
        EPS = 1e-08

        def _cum_mean(t):
            n = t.shape[-1]
            denom = jnp.arange(1, n + 1, dtype=t.dtype)
            return jnp.cumsum(t, axis=-1) / denom
        key = jax.random.key(seed)
        ks = jax.random.split(key, 4)
        b, n, dim, h = (2, 512, 128, 8)
        x = jax.random.normal(ks[0], (b, n, dim), dtype=jnp.float32)
        w_qkv = jax.random.normal(ks[1], (dim, 3 * dim), dtype=jnp.float32) * dim ** (-0.5)
        w_out = jax.random.normal(ks[2], (dim, dim), dtype=jnp.float32) * dim ** (-0.5)
        b_out = jnp.zeros((dim,), dtype=jnp.float32)
        norm_g = jnp.ones((1, h, 1, 1), dtype=jnp.float32)
        norm_b = jnp.zeros((1, h, 1, 1), dtype=jnp.float32)
        return {'x': x, 'w_qkv': w_qkv, 'w_out': w_out, 'b_out': b_out, 'norm_g': norm_g, 'norm_b': norm_b}
    _L0_attn_all = _L0_attn_setup()
    _L0_attn_in = {k: v for k, v in _L0_attn_all.items() if k in ('w_qkv', 'w_out', 'b_out', 'norm_g', 'norm_b')}
    del _L0_attn_all

    def _L0_ffn_setup():
        import jax, jax.numpy as jnp
        import numpy as np
        K = 2
        EPS = 1e-06

        def _layernorm(x, gamma, beta):
            mu = jnp.mean(x, axis=-1, keepdims=True)
            var = jnp.mean(jnp.square(x - mu), axis=-1, keepdims=True)
            return (x - mu) * jax.lax.rsqrt(var + EPS) * gamma + beta
        key = jax.random.key(seed)
        ks = jax.random.split(key, 5)
        B, S, D, F, E = (8, 512, 128, 512, 8)
        x = jax.random.normal(ks[0], (B, S, D), dtype=jnp.float32)
        router_w = jax.random.normal(ks[1], (D, E), dtype=jnp.float32) * 0.02
        w1 = jax.random.normal(ks[2], (E, D, F), dtype=jnp.float32) * 0.02
        b1 = jnp.zeros((E, F), dtype=jnp.float32)
        w2 = jax.random.normal(ks[3], (E, F, D), dtype=jnp.float32) * 0.02
        b2 = jnp.zeros((E, D), dtype=jnp.float32)
        gamma = jnp.ones((E, D), dtype=jnp.float32)
        beta = jnp.zeros((E, D), dtype=jnp.float32)
        return {'x': x, 'router_w': router_w, 'w1': w1, 'b1': b1, 'w2': w2, 'b2': b2, 'gamma': gamma, 'beta': beta}
    _L0_ffn_all = _L0_ffn_setup()
    _L0_ffn_in = {k: v for k, v in _L0_ffn_all.items() if k in ('router_w', 'w1', 'b1', 'w2', 'b2', 'gamma', 'beta')}
    del _L0_ffn_all
    return {'x': x, 'cls_tok': cls_tok, 'L0_tok_W1_w': _L0_tok_in['W1_w'], 'L0_tok_W1_b': _L0_tok_in['W1_b'], 'L0_tok_W1_sw': _L0_tok_in['W1_sw'], 'L0_tok_W1_sb': _L0_tok_in['W1_sb'], 'L0_tok_W2_w': _L0_tok_in['W2_w'], 'L0_tok_W2_b': _L0_tok_in['W2_b'], 'L0_tok_W2_sw': _L0_tok_in['W2_sw'], 'L0_tok_W2_sb': _L0_tok_in['W2_sb'], 'L0_tok_W3_w': _L0_tok_in['W3_w'], 'L0_tok_W3_b': _L0_tok_in['W3_b'], 'L0_tok_eps_in1': _L0_tok_in['eps_in1'], 'L0_tok_eps_out1': _L0_tok_in['eps_out1'], 'L0_tok_eps_in2': _L0_tok_in['eps_in2'], 'L0_tok_eps_out2': _L0_tok_in['eps_out2'], 'L0_attn_w_qkv': _L0_attn_in['w_qkv'], 'L0_attn_w_out': _L0_attn_in['w_out'], 'L0_attn_b_out': _L0_attn_in['b_out'], 'L0_attn_norm_g': _L0_attn_in['norm_g'], 'L0_attn_norm_b': _L0_attn_in['norm_b'], 'L0_ffn_router_w': _L0_ffn_in['router_w'], 'L0_ffn_w1': _L0_ffn_in['w1'], 'L0_ffn_b1': _L0_ffn_in['b1'], 'L0_ffn_w2': _L0_ffn_in['w2'], 'L0_ffn_b2': _L0_ffn_in['b2'], 'L0_ffn_gamma': _L0_ffn_in['gamma'], 'L0_ffn_beta': _L0_ffn_in['beta']}

def reference(x, cls_tok, L0_tok_W1_w, L0_tok_W1_b, L0_tok_W1_sw, L0_tok_W1_sb, L0_tok_W2_w, L0_tok_W2_b, L0_tok_W2_sw, L0_tok_W2_sb, L0_tok_W3_w, L0_tok_W3_b, L0_tok_eps_in1, L0_tok_eps_out1, L0_tok_eps_in2, L0_tok_eps_out2, L0_attn_w_qkv, L0_attn_w_out, L0_attn_b_out, L0_attn_norm_g, L0_attn_norm_b, L0_ffn_router_w, L0_ffn_w1, L0_ffn_b1, L0_ffn_w2, L0_ffn_b2, L0_ffn_gamma, L0_ffn_beta):
    import jax
    import jax.numpy as jnp

    def _L0_tok_ref(inputs, W1_w, W1_b, W1_sw, W1_sb, W2_w, W2_b, W2_sw, W2_sb, W3_w, W3_b, eps_in1, eps_out1, eps_in2, eps_out2):
        import math
        import jax, jax.numpy as jnp
        import numpy as np
        PW = PH = 16
        EMB = 128
        HID = 128
        B, H, W = (64, 128, 128)
        L = H // PW * (W // PH)
        SIGMA_ZERO = 0.1

        def _f_noise(x):
            return jnp.sign(x) * jnp.sqrt(jnp.abs(x))

        def _noisy_linear(x, w, b, sw, sb, eps_in, eps_out):
            ei = _f_noise(eps_in)
            eo = _f_noise(eps_out)
            w_n = w + sw * (eo[:, None] * ei[None, :])
            b_n = b + sb * eo
            return x @ w_n.T + b_n

        def _unfold_patches(x):
            b = x.shape[0]
            p = x.reshape(b, H // PW, PW, W // PH, PH)
            p = p.transpose(0, 1, 3, 2, 4)
            return p.reshape(b, L, PW * PH)

        def _pos_encoding(x):
            pos = jnp.arange(L, dtype=jnp.float32)[:, None]
            div = jnp.exp(jnp.arange(0, EMB, 2, dtype=jnp.float32) * (-math.log(10000.0) / EMB))
            ang = pos * div
            pe = jnp.stack([jnp.sin(ang), jnp.cos(ang)], axis=-1).reshape(L, EMB)
            return x + pe[None, :, :]
        x = _unfold_patches(inputs)
        g = _noisy_linear(x, W1_w, W1_b, W1_sw, W1_sb, eps_in1, eps_out1)
        x_gate = g * jnp.tanh(jax.nn.softplus(g))
        x_inner = _noisy_linear(x, W2_w, W2_b, W2_sw, W2_sb, eps_in2, eps_out2)
        x = x_gate * x_inner
        x = x @ W3_w.T + W3_b
        return _pos_encoding(x)

    def _L0_attn_ref(x, w_qkv, w_out, b_out, norm_g, norm_b):
        import jax, jax.numpy as jnp
        import numpy as np
        EPS = 1e-08

        def _cum_mean(t):
            n = t.shape[-1]
            denom = jnp.arange(1, n + 1, dtype=t.dtype)
            return jnp.cumsum(t, axis=-1) / denom
        b, n, dim = x.shape
        h = norm_g.shape[1]
        d = dim // h
        scale = dim ** (-0.5)
        qkv = (x @ w_qkv).reshape(b, n, 3, h, d).transpose(2, 0, 3, 1, 4)
        q, k, v = (qkv[0], qkv[1], qkv[2])
        dots = jnp.einsum('bhid,bhjd->bhij', q, k) * scale
        causal_mask = jnp.triu(jnp.ones((n, n), dtype=bool), k=1)
        dots = jnp.where(causal_mask, 0.0, dots)
        mu = jnp.diagonal(_cum_mean(dots), axis1=-2, axis2=-1)[..., None]
        t = dots - mu
        s = jnp.diagonal(_cum_mean(t * t), axis1=-2, axis2=-1)[..., None]
        normed = t * jax.lax.rsqrt(s + EPS)
        attn = normed * norm_g + norm_b
        attn = jnp.where(causal_mask, 0.0, attn)
        out = jnp.einsum('bhij,bhjd->bhid', attn, v)
        out = out.transpose(0, 2, 1, 3).reshape(b, n, dim)
        return out @ w_out + b_out

    def _L0_ffn_ref(x, router_w, w1, b1, w2, b2, gamma, beta):
        import jax, jax.numpy as jnp
        import numpy as np
        K = 2
        EPS = 1e-06

        def _layernorm(x, gamma, beta):
            mu = jnp.mean(x, axis=-1, keepdims=True)
            var = jnp.mean(jnp.square(x - mu), axis=-1, keepdims=True)
            return (x - mu) * jax.lax.rsqrt(var + EPS) * gamma + beta
        B, S, D = x.shape
        E = w1.shape[0]
        xf = x.reshape(-1, D)
        logits = xf @ router_w
        gate_vals, idx = jax.lax.top_k(logits, K)
        gates = jax.nn.softmax(gate_vals, axis=-1)
        out = jnp.zeros_like(xf)
        for e in range(E):
            h = jax.nn.relu(xf @ w1[e] + b1[e]) @ w2[e] + b2[e]
            y = _layernorm(xf + h, gamma[e], beta[e])
            w = jnp.sum(jnp.where(idx == e, gates, 0.0), axis=-1)
            out = out + w[:, None] * y
        return out.reshape(B, S, D)
    h = _L0_tok_ref(x, L0_tok_W1_w, L0_tok_W1_b, L0_tok_W1_sw, L0_tok_W1_sb, L0_tok_W2_w, L0_tok_W2_b, L0_tok_W2_sw, L0_tok_W2_sb, L0_tok_W3_w, L0_tok_W3_b, L0_tok_eps_in1, L0_tok_eps_out1, L0_tok_eps_in2, L0_tok_eps_out2)
    h = jnp.concatenate([jnp.broadcast_to(cls_tok, (h.shape[0], 1, h.shape[2])), h], axis=1)
    h = h + _L0_attn_ref(_layernorm(h, axis=-1), L0_attn_w_qkv, L0_attn_w_out, L0_attn_b_out, L0_attn_norm_g, L0_attn_norm_b)
    h = h + _L0_ffn_ref(_layernorm(h, axis=-1), L0_ffn_router_w, L0_ffn_w1, L0_ffn_b1, L0_ffn_w2, L0_ffn_b2, L0_ffn_gamma, L0_ffn_beta)
    return h

_drawn_inputs = setup_inputs


def setup_inputs(seed=0):
    import zlib

    import numpy as np

    out = dict(_drawn_inputs(seed))
    spreads = {'L0_tok_W1_sw': (0.0062500000931322575, 0.6),
     'L0_tok_W1_sb': (0.0062500000931322575, 0.6),
     'L0_tok_W2_sw': (0.0062500000931322575, 0.6),
     'L0_tok_W2_sb': (0.0062500000931322575, 0.6),
     'L0_attn_b_out': (0.0, 0.471),
     'L0_attn_norm_g': (1.0, 0.2),
     'L0_attn_norm_b': (0.0, 0.1),
     'L0_ffn_b1': (0.0, 0.8),
     'L0_ffn_b2': (0.0, 2.0),
     'L0_ffn_gamma': (1.0, 0.6),
     'L0_ffn_beta': (0.0, 0.8)}
    factors = {'L0_tok_W1_b': 2.892,
     'L0_tok_W2_b': 2.876,
     'L0_ffn_router_w': 3.45,
     'L0_ffn_w1': 8.0,
     'L0_ffn_w2': 8.0}
    for name, (base, spread) in spreads.items():
        noise = np.random.default_rng([zlib.crc32(name.encode()), seed]).standard_normal(out[name].shape)
        drawn = base * np.exp(spread * noise) if base else spread * noise
        out[name] = jnp.asarray(drawn.astype(out[name].dtype))
    for name, factor in factors.items():
        out[name] = (out[name] * factor).astype(out[name].dtype)
    return out
```

```python
from contextlib import ExitStack

import numpy as np
import concourse.bass as bass
from concourse import mybir

F32 = mybir.dt.float32
F32R = mybir.dt.float32r
U32 = mybir.dt.uint32
ALU = mybir.AluOpType
ACT = mybir.ActivationFunctionType
AX = mybir.AxisListType

P = 128
IMAGES, SIDE, PATCH = 16, 128, 16
GRID = SIDE // PATCH
PATCHES = GRID * GRID
TOKENS = IMAGES * PATCHES
FEATURES = PATCH * PATCH
HALVES = FEATURES // P
TILES = TOKENS // P
CLS = TILES
BANK = 512
CHUNKS = TOKENS // BANK
CT = TILES // CHUNKS
HEADS, HD = 8, 16
HP = HEADS // 2
KEYS = PATCHES + 1
GROUPS = 4
GI = IMAGES // GROUPS
EXPERTS, HIDDEN = 8, 512
FT = HIDDEN // P
LN1_EPS, LN2_EPS, ATT_EPS, MOE_EPS = 1e-5, 1e-5, 1e-8, 1e-6
EXP_CAP = 16384.0

NOISE_COLS = [("w", 4 * P), ("sw", 4 * P), ("ei", 4), ("eo_row", 2 * P), ("eo_col", 2), ("b", 2), ("sb", 2)]
BODY_COLS = [("w3T", P), ("b3", P), ("pos", P), ("ident", P), ("cls", P), ("wq", P), ("wk", P), ("wv", P),
             ("wout", P), ("bout", P), ("beta", P), ("router", EXPERTS), ("mask", KEYS), ("inv_n", 1),
             ("par_scaled", 2), ("par", 2), ("iota", EXPERTS), ("g_tab", HP), ("b_tab", HP), ("b_col", 1)]


def columns(spec):
    at, found = 0, {}
    for name, width in spec:
        found[name] = (at, at + width)
        at += width
    return found, at


NOISE_AT, NOISE_W = columns(NOISE_COLS)
BODY_AT, BODY_W = columns(BODY_COLS)


def vit_tower(nc, patches, noise, body, w1b1, w2, gb2, out):
    ctx = ExitStack()
    with ctx:
        def sb(name, shape, dtype=F32):
            return ctx.enter_context(nc.sbuf_tensor(name, shape, dtype))

        def sem(name):
            return ctx.enter_context(nc.semaphore(name))

        xT = sb("xT", [P, CHUNKS, HALVES, BANK])
        noise_sb = sb("noise_sb", [P, NOISE_W])
        body_sb = sb("body_sb", [P, BODY_W])
        NF0, NF1 = NOISE_AT["ei"][0], NOISE_AT["eo_col"][1]
        NFW = NF1 - NF0
        f_abs = sb("f_abs", [P, NFW])
        f_root = sb("f_root", [P, NFW])
        f_sign = sb("f_sign", [P, NFW])
        f_noise = sb("f_noise", [P, NFW])
        sw_eo = sb("sw_eo", [P, 4, P])
        w_noisy = sb("w_noisy", [P, 4, P])
        b_noisy = sb("b_noisy", [P, 2])
        posb = sb("posb", [P, P])
        S = sb("S", [P, GROUPS, HP, GI, KEYS])
        SQ = sb("SQ", [P, GROUPS, HP * GI * KEYS])
        parts = SQ[:, :, :].rearrange("p g n -> p (g n)")
        g_sb = parts[:, 0 * TOKENS:1 * TOKENS]
        n_sb = parts[:, 1 * TOKENS:2 * TOKENS]
        e_sb = parts[:, 2 * TOKENS:3 * TOKENS]
        m_sb = parts[:, 3 * TOKENS:4 * TOKENS]
        r_sb = sb("r_sb", [P, TOKENS])
        gn_sb = sb("gn_sb", [P, TOKENS])
        gT = sb("gT", [P, TOKENS])
        h = sb("h", [P, TILES + 1, P])
        hb = sb("hb", [P, TILES + 1, P])
        st = sb("st", [P, TILES + 1, 6])
        mv = sb("mv", [P, TILES + 1, 2])
        ve = sb("ve", [P, TILES + 1])
        rstd = sb("rstd", [P, TILES + 1])
        minus_half = sb("minus_half", [P, TILES + 1])
        xn = sb("xn", [P, TILES + 1, P])
        xnT = sb("xnT", [P, TOKENS + 1])
        qTm = sb("qTm", [P, IMAGES, 2, PATCHES])
        kT = sb("kT", [P, IMAGES, KEYS])
        v = sb("v", [KEYS, IMAGES, P])
        v_cls_b = sb("v_cls_b", [P, 1])
        NS = GROUPS * HP * GI
        ssum = sb("ssum", [P, NS])
        mu = sb("mu", [P, NS])
        qsum = sb("qsum", [P, NS])
        var = sb("var", [P, NS])
        sd = sb("sd", [P, NS])
        rs = sb("rs", [P, NS])
        rg = sb("rg", [P, NS])
        bmask = sb("bmask", [P, HP, KEYS])
        attnT = sb("attnT", [P, IMAGES, HP * P])
        oT = sb("oT", [P, 2, IMAGES, PATCHES])
        wout_par = sb("wout_par", [P, 2, P])
        acc = sb("acc", [P, TILES + 1, P])
        x2 = sb("x2", [P, TILES + 1, P])
        x2T = sb("x2T", [P, TOKENS + 2])
        x2T_hi = sb("x2T_hi", [P, TOKENS + 2], F32R)
        x2T_lo = sb("x2T_lo", [P, TOKENS + 2], F32R)
        lg = sb("lg", [P, TILES + 1, EXPERTS])
        top = sb("top", [P, TILES + 1, 8])
        top_at = sb("top_at", [P, TILES + 1, 8], U32)
        top_atf = sb("top_atf", [P, TILES + 1, 2])
        dlt = sb("dlt", [P, TILES + 1])
        ex = sb("ex", [P, TILES + 1])
        den = sb("den", [P, TILES + 1])
        g1 = sb("g1", [P, TILES + 1])
        g2 = sb("g2", [P, TILES + 1])
        sel = sb("sel", [P, 2, TILES + 1, EXPERTS])
        gate = sb("gate", [P, TILES + 1, EXPERTS])
        gateT = sb("gateT", [EXPERTS, TILES + 1, P])
        w1_in = [sb(f"w1_in{b}", [P, HIDDEN + FT]) for b in range(2)]
        w1_hi = [sb(f"w1_hi{b}", [P, HIDDEN], F32R) for b in range(2)]
        w1_lo = [sb(f"w1_lo{b}", [P, HIDDEN], F32R) for b in range(2)]
        w2_in = [sb(f"w2_in{b}", [P, FT, P]) for b in range(2)]
        gb2_in = [sb(f"gb2_in{b}", [P, 2, P]) for b in range(2)]
        CW = [BANK, BANK, 2]
        CN = [CT, CT, 1]
        CR = [P, P, 1]
        C0 = [0, CT, CLS]
        hid = [attnT[:, FT * c:FT * (c + 1), :] for c in range(CHUNKS)] + [sb("hid_cls", [P, FT, 2])]
        S_flat = S[:, :, :, :, :].rearrange("p g h i k -> p (g h i k)")

        def over_S(n):
            return S_flat[:, n * BANK:(n + 1) * BANK].rearrange("p (t d) -> p t d", d=P)

        x2b = [over_S(c) for c in range(CHUNKS)] + [sb("x2b_cls", [P, 1, P])]
        y = [over_S(2 + c) for c in range(CHUNKS)] + [sb("y_cls", [P, 1, P])]
        u = [over_S(4 + c) for c in range(CHUNKS)] + [sb("u_cls", [P, 1, P])]
        yst = [sb(f"yst{c}", [P, CN[c], 6]) for c in range(3)]
        ymv = [sb(f"ymv{c}", [P, CN[c], 2]) for c in range(3)]
        yd = [sb(f"yd{c}", [P, CN[c]]) for c in range(3)]
        ymean = [sb(f"ymean{c}", [P, CN[c]]) for c in range(3)]
        yve = [sb(f"yve{c}", [P, CN[c]]) for c in range(3)]
        yrs = [sb(f"yrs{c}", [P, CN[c]]) for c in range(3)]
        ya = [sb(f"ya{c}", [P, CN[c]]) for c in range(3)]

        ps = ctx.enter_context(nc.psum_tensor("ps", [P, 8, BANK], F32))

        def nz(name):
            a, b = NOISE_AT[name]
            return noise_sb[:, a:b]

        def bd(name, rows=P):
            a, b = BODY_AT[name]
            return body_sb[0:rows, a:b]

        def fz(name):
            a, b = NOISE_AT[name]
            return f_noise[:, a - NF0:b - NF0]

        ident = bd("ident")

        noise_in, body_in, patches_in = sem("noise_in"), sem("body_in"), [sem("patches_in0"), sem("patches_in1")]
        w1_loaded = [sem("w1_loaded0"), sem("w1_loaded1")]
        w2_loaded = [sem("w2_loaded0"), sem("w2_loaded1")]
        gb2_loaded = [sem("gb2_loaded0"), sem("gb2_loaded1")]
        f_parts, f_done, w_done, b_done = sem("f_parts"), sem("f_done"), sem("w_done"), sem("b_done")
        consts_set, pow_const = sem("consts_set"), sem("pow_const")
        gate_ps, inner_ps = sem("gate_ps"), sem("inner_ps")
        gate_read, exp_done, mish_dve, gn_done, gT_done = (
            sem("gate_read"), sem("exp_done"), sem("mish_dve"), sem("gn_done"), sem("gT_done"))
        h_ps, h_done, hb_done = sem("h_ps"), sem("h_done"), sem("hb_done")
        ln_stats, ln_ve, ln_rstd = sem("ln_stats"), sem("ln_ve"), sem("ln_rstd")
        xn_done, xnT_ps, xnT_done = sem("xn_done"), sem("xnT_ps"), sem("xnT_done")
        q_ps, k_ps, v_ps, cls_ps = sem("q_ps"), sem("k_ps"), sem("v_ps"), sem("cls_ps")
        q_done, k_done, v_done, cls_done = sem("q_done"), sem("k_done"), sem("v_done"), sem("cls_done")
        cls_o_done = sem("cls_o_done")
        scores_ps, S_masked, S_sum, mu_done, S_centred = (
            sem("scores_ps"), sem("S_masked"), sem("S_sum"), sem("mu_done"), sem("S_centred"))
        T_masked, squared, var_done, sd_done, rs_done, rg_done = (
            sem("T_masked"), sem("squared"), sem("var_done"), sem("sd_done"), sem("rs_done"), sem("rg_done"))
        S_scaled, attn_done = sem("S_scaled"), sem("attn_done")
        attnT_ps, attnT_act, attnT_dve = sem("attnT_ps"), sem("attnT_act"), sem("attnT_dve")
        o_ps, o_done, proj_ps, acc_done = sem("o_ps"), sem("o_done"), sem("proj_ps"), sem("acc_done")
        ln2_stats, ln2_ve, ln2_rstd, x2_done = sem("ln2_stats"), sem("ln2_ve"), sem("ln2_rstd"), sem("x2_done")
        x2T_ps, x2T_done, x2T_hi_done, x2T_lo_done = (
            sem("x2T_ps"), sem("x2T_done"), sem("x2T_hi_done"), sem("x2T_lo_done"))
        logits_ps, routing, exp_gate, gates_done = sem("logits_ps"), sem("routing"), sem("exp_gate"), sem("gates_done")
        w1_hi_done, w1_lo_done = sem("w1_hi_done"), sem("w1_lo_done")
        hid_ps, hid_done = sem("hid_ps"), sem("hid_done")
        cls_hid_ps, cls_hid_sum, cls_hid_done = sem("cls_hid_ps"), sem("cls_hid_sum"), sem("cls_hid_done")
        y_ps, y_read = sem("y_ps"), sem("y_read")
        x2b_done, y_stats, y_parts, y_var, y_ve, y_rs, y_a, u_done, moe_acc = (
            sem("x2b_done"), sem("y_stats"), sem("y_parts"), sem("y_var"), sem("y_ve"), sem("y_rs"), sem("y_a"), sem("u_done"),
            sem("moe_acc"))
        gateT_ps, gateT_done, beta_ps, final_done, stored = (
            sem("gateT_ps"), sem("gateT_done"), sem("beta_ps"), sem("final_done"), sem("stored"))

        bn1_done, bn2_done, topped = sem("bn1_done"), sem("bn2_done"), sem("topped")

        block = ctx.enter_context(nc.Block())

        @block.sync
        def _(sp):
            sp.dma_start(noise_sb[:, :], noise).then_inc(noise_in, 16)
            for c in range(CHUNKS):
                sp.dma_start(xT[:, c, :, :], patches[:, c, :, :]).then_inc(patches_in[c], 16)
            sp.dma_start(body_sb[:, :], body).then_inc(body_in, 16)

            def load_expert(e, b):
                sp.dma_start(w1_in[b][:, :], w1b1[bass.ds(e, 1), :, :].rearrange("a p n -> (a p) n")
                             ).then_inc(w1_loaded[b], 16)
                sp.dma_start(w2_in[b][:, :, :], w2[bass.ds(e, 1), :, :, :].rearrange("a p t n -> (a p) t n")
                             ).then_inc(w2_loaded[b], 16)
                sp.dma_start(gb2_in[b][:, :, :], gb2[bass.ds(e, 1), :, :].to_broadcast([P, 2, P])
                             ).then_inc(gb2_loaded[b], 16)

            for b in range(2):
                load_expert(b, b)
            with sp.Fori(0, EXPERTS // 2 - 1) as it:
                for b in range(2):
                    sp.wait_ge(y_ps, 3 * (2 * it + b + 1))
                    sp.wait_ge(moe_acc, 3 * (2 * it + b + 1))
                    load_expert(2 * it + b + 2, b)

            for c in range(CHUNKS):
                sp.wait_ge(final_done, c + 1)
                for b in range(2):
                    rows = acc[PATCHES * b:PATCHES * (b + 1), CT * c:CT * (c + 1), :]
                    dst = out[2 * CT * c + b:2 * CT * (c + 1):2, 1:KEYS, :].rearrange("t r d -> r t d")
                    sp.dma_start(dst, rows).then_inc(stored, 16)
            sp.wait_ge(final_done, CHUNKS + 1)
            sp.dma_start(out[:, 0:1, :].rearrange("t r d -> r t d"),
                         acc[0:1, CLS:CLS + 1, :].to_broadcast([1, IMAGES, P])).then_inc(stored, 16)
            sp.wait_ge(stored, 16 * (2 * CHUNKS + 1))

        @block.gpsimd
        def _(pool):
            nc.gpsimd.memset(minus_half[:, :], -0.5).then_inc(pow_const, 1)
            pool.wait_ge(pow_const, 1)
            for c in range(CHUNKS):
                sl = slice(c * BANK, (c + 1) * BANK)
                pool.wait_ge(mish_dve, 3 * c + 2)
                pool.wait_ge(gate_read, c + 1)
                nc.gpsimd.tensor_tensor(gn_sb[:, sl], g_sb[:, sl], n_sb[:, sl], ALU.mult).then_inc(gn_done, 1)

            def ln_power(stats, ve_sem, out_sem, eps, c):
                a, b = (CT * c, CT * (c + 1)) if c < CHUNKS else (CLS, CLS + 1)
                pool.wait_ge(stats, c + 1)
                nc.gpsimd.tensor_scalar(ve[:, a:b], mv[:, a:b, 1], eps, None, ALU.add).then_inc(ve_sem, 1)
                pool.wait_ge(ve_sem, c + 1)
                nc.gpsimd.tensor_tensor(rstd[:, a:b], ve[:, a:b], minus_half[:, a:b], ALU.pow).then_inc(out_sem, 1)

            for c in range(CHUNKS + 1):
                ln_power(ln_stats, ln_ve, ln_rstd, LN1_EPS, c)
            pool.wait_ge(h_done, CHUNKS)
            pool.wait_ge(consts_set, 8)
            pool.wait_ge(body_in, 16)
            nc.gpsimd.tensor_tensor(hb[:, :, :], h[:, :, :],
                                    bd("bout").unsqueeze(1).to_broadcast([P, TILES + 1, P]), ALU.add
                                    ).then_inc(hb_done, 1)
            for g in range(GROUPS):
                pool.wait_ge(S_centred, g + 1)
                t = S[:, g, :, :, :].rearrange("p h i k -> p (h i) k")
                nc.gpsimd.tensor_tensor(t, t, bd("mask").unsqueeze(1).to_broadcast([P, HP * GI, KEYS]), ALU.mult
                                        ).then_inc(T_masked, 1)
            for g in range(GROUPS):
                pool.wait_ge(rg_done, 1)
                pool.wait_ge(squared, g + 1)
                t = S[:, g, :, :, :].rearrange("p h i k -> p (h i) k")
                r = rg[:, g * HP * GI:(g + 1) * HP * GI].unsqueeze(2).to_broadcast([P, HP * GI, KEYS])
                nc.gpsimd.tensor_tensor(t, t, r, ALU.mult).then_inc(S_scaled, 1)
            for c in range(CHUNKS + 1):
                ln_power(ln2_stats, ln2_ve, ln2_rstd, LN2_EPS, c)

            def w1_low(e, b):
                pool.wait_ge(w1_hi_done, e + 1)
                nc.gpsimd.tensor_tensor(w1_lo[b][:, :], w1_in[b][:, 0:HIDDEN], w1_hi[b][:, :].bitcast(F32),
                                        ALU.subtract).then_inc(w1_lo_done, 1)

            w1_low(0, 0)
            for c in range(CHUNKS + 1):
                sl = slice(c * BANK, c * BANK + CW[c])
                pool.wait_ge(x2T_hi_done, c + 1)
                nc.gpsimd.tensor_tensor(x2T_lo[:, sl], x2T[:, sl], x2T_hi[:, sl].bitcast(F32), ALU.subtract
                                        ).then_inc(x2T_lo_done, 1)

            def expert(it, b, split_next):
                e = 2 * it + b
                pool.wait_ge(gb2_loaded[b], 16 * (it + 1))
                for c in range(3):
                    pool.wait_ge(y_read, 3 * e + c + 1)
                    r = CR[c]
                    nc.gpsimd.tensor_tensor(x2b[c][0:r, :, :], x2[0:r, C0[c]:C0[c] + CN[c], :],
                                            gb2_in[b][0:r, 1:2, :].to_broadcast([r, CN[c], P]), ALU.add
                                            ).then_inc(x2b_done, 1)
                if split_next:
                    w1_low(e + 1, 1 - b)
                for c in range(3):
                    n = 3 * e + c + 1
                    r = CR[c]
                    pool.wait_ge(y_ve, n)
                    nc.gpsimd.tensor_tensor(yrs[c][0:r, :], yve[c][0:r, :], minus_half[0:r, 0:CN[c]], ALU.pow
                                            ).then_inc(y_rs, 1)
                    pool.wait_ge(y_rs, n)
                    nc.gpsimd.tensor_tensor(ya[c][0:r, :].unsqueeze(2), yrs[c][0:r, :].unsqueeze(2),
                                            gate[0:r, C0[c]:C0[c] + CN[c], bass.ds(e, 1)], ALU.mult).then_inc(y_a, 1)

            pool.wait_ge(gates_done, 1)
            with pool.Fori(0, EXPERTS // 2 - 1) as it:
                for b in range(2):
                    expert(it, b, True)
            expert(EXPERTS // 2 - 1, 0, True)
            expert(EXPERTS // 2 - 1, 1, False)

        @block.scalar
        def _(act):
            act.wait_ge(noise_in, 16)
            raw = noise_sb[:, NF0:NF1]
            nc.scalar.activation(f_abs[:, :], raw, ACT.Abs).then_inc(f_parts, 1)
            act.wait_ge(f_parts, 1)
            nc.scalar.activation(f_root[:, :], f_abs[:, :], ACT.Sqrt).then_inc(f_parts, 1)
            nc.scalar.activation(f_sign[:, :], raw, ACT.Sign).then_inc(f_parts, 1)
            act.wait_ge(b_done, 1)
            for c in range(CHUNKS):
                sl = slice(c * BANK, (c + 1) * BANK)
                act.wait_ge(gate_ps, c + 1)
                nc.scalar.activation(e_sb[:, sl], ps[:, 2 * c, :], ACT.Exp, bias=b_noisy[:, 0:1]).then_inc(exp_done, 1)
                nc.scalar.activation(g_sb[:, sl], ps[:, 2 * c, :], ACT.Identity, bias=b_noisy[:, 0:1]
                                     ).then_inc(gate_read, 1)
            for c in range(CHUNKS):
                act.wait_ge(xnT_ps, c + 1)
                nc.scalar.copy(xnT[:, c * BANK:(c + 1) * BANK], ps[:, 6 + c, :]).then_inc(xnT_done, 1)
            act.wait_ge(xnT_ps, CHUNKS + 1)
            nc.scalar.copy(xnT[:, TOKENS:TOKENS + 1], ps[:, 2, 0:1]).then_inc(xnT_done, 1)
            for c in range(CHUNKS):
                act.wait_ge(q_ps, c + 1)
                for a in range(2):
                    nc.scalar.activation(qTm[:, c * 8:(c + 1) * 8, a, :],
                                         ps[:, c, :].rearrange("p (i r) -> p i r", r=PATCHES), ACT.Copy,
                                         scale=bd("par_scaled")[:, a:a + 1]).then_inc(q_done, 1)
            act.wait_ge(cls_ps, 1)
            nc.scalar.activation(v_cls_b[:, :], ps[:, 2, 1:2], ACT.Copy, scale=bd("b_col")).then_inc(cls_o_done, 1)
            nc.scalar.copy(kT[:, :, PATCHES:KEYS], ps[:, 2, 0:1].unsqueeze(1).to_broadcast([P, IMAGES, 1])
                           ).then_inc(cls_done, 1)
            nc.scalar.copy(v[PATCHES:KEYS, :, :],
                           ps[PATCHES:KEYS, 2, P:2 * P].unsqueeze(1).to_broadcast([1, IMAGES, P])
                           ).then_inc(cls_done, 1)
            for g in range(GROUPS):
                act.wait_ge(v_ps, g + 1)
                nc.scalar.copy(v[0:PATCHES, g * GI:(g + 1) * GI, :],
                               ps[0:PATCHES, [3, 6, 7, 2][g], :].rearrange("p (i d) -> p i d", d=P)
                               ).then_inc(v_done, 1)
            act.wait_ge(w1_loaded[0], 16)
            nc.scalar.copy(w1_hi[0][:, :], w1_in[0][:, 0:HIDDEN]).then_inc(w1_hi_done, 1)
            for g in range(GROUPS):
                act.wait_ge(T_masked, g + 1)
                nc.scalar.activation(SQ[:, g, :], S[:, g, :, :, :].rearrange("p h i k -> p (h i k)"), ACT.Square
                                     ).then_inc(squared, 1)
            act.wait_ge(var_done, 1)
            nc.scalar.activation(sd[:, :], var[:, :], ACT.Sqrt).then_inc(sd_done, 1)
            for i in range(0, IMAGES, 2):
                act.wait_ge(attnT_ps, i + 1)
                nc.scalar.copy(attnT[0:KEYS, i, :], ps[0:KEYS, i % 4, :]).then_inc(attnT_act, 1)
            for g in range(GROUPS):
                act.wait_ge(o_ps, g + 1)
                nc.scalar.copy(oT[:, :, g * GI:(g + 1) * GI, :].rearrange("p a i r -> p i a r"),
                               ps[:, 4 + g, :].rearrange("p (i a r) -> p i a r", a=2, r=PATCHES)).then_inc(o_done, 1)
            for c in range(CHUNKS + 1):
                sl = slice(c * BANK, c * BANK + CW[c])
                n = CW[c] if c < CHUNKS else 1
                act.wait_ge(x2T_ps, c + 1)
                nc.scalar.copy(x2T[:, c * BANK:c * BANK + n], ps[:, 4 + c, 0:n]).then_inc(x2T_done, 1)
                act.wait_ge(x2T_done, c + 1)
                act.wait_ge(consts_set, 8)
                last = nc.scalar.copy(x2T_hi[:, sl], x2T[:, sl]).then_inc(x2T_hi_done, 1)
            act.wait_ge(routing, 4)
            nc.scalar.activation(ex[:, :], dlt[:, :], ACT.Exp).then_inc(exp_gate, 1)

            def expert(it, b, first):
                e = 2 * it + b
                if not first or b == 1:
                    act.wait_ge(w1_loaded[b], 16 * (it + 1))
                    if not first:
                        act.wait_ge(cls_hid_ps, e - 1)
                    nc.scalar.copy(w1_hi[b][:, :], w1_in[b][:, 0:HIDDEN]).then_inc(w1_hi_done, 1)
                for c in range(CHUNKS):
                    if not first or b == 1:
                        act.wait_ge(y_ps, 3 * (e - 1) + c + 1)
                    for f in range(FT):
                        act.wait_ge(hid_ps, (2 * e + c) * FT + f + 1)
                        nc.scalar.activation(hid[c][:, f, :], ps[:, f, :], ACT.Relu,
                                             bias=w1_in[b][:, HIDDEN + f:HIDDEN + f + 1]).then_inc(hid_done, 1)

            for b in range(2):
                expert(0, b, True)
            with act.Fori(1, EXPERTS // 2) as it:
                for b in range(2):
                    expert(it, b, False)
            act.wait_ge(gateT_ps, 3)
            nc.scalar.copy(gateT[:, 0:CT, :].rearrange("e t p -> e (t p)"), ps[0:EXPERTS, 0, :]).then_inc(gateT_done, 1)
            nc.scalar.copy(gateT[:, CT:2 * CT, :].rearrange("e t p -> e (t p)"), ps[0:EXPERTS, 1, :]
                           ).then_inc(gateT_done, 1)
            nc.scalar.copy(gateT[:, CLS, :], ps[0:EXPERTS, 2, 0:P]).then_inc(gateT_done, 1)

        @block.vector
        def _(dve):
            nc.vector.memset(h[:, CLS, :], 0.0).then_inc(consts_set, 1)
            nc.vector.memset(acc[:, CLS, :], 0.0).then_inc(consts_set, 1)
            nc.vector.memset(x2T[:, TOKENS:TOKENS + 2], 0.0).then_inc(consts_set, 1)
            dve.wait_ge(consts_set, 3)
            dve.wait_ge(f_parts, 3)
            nc.vector.tensor_tensor(f_noise[:, :], f_root[:, :], f_sign[:, :], ALU.mult).then_inc(f_done, 1)
            dve.wait_ge(f_done, 1)
            for k in range(2):
                nc.vector.tensor_tensor(
                    sw_eo[:, 2 * k:2 * k + 2, :], nz("sw").rearrange("p (k n) -> p k n", n=P)[:, 2 * k:2 * k + 2, :],
                    fz("eo_row")[:, k * P:(k + 1) * P].unsqueeze(1).to_broadcast([P, 2, P]), ALU.mult
                ).then_inc(f_done, 1)
            dve.wait_ge(f_done, 3)
            for k in range(4):
                nc.vector.scalar_tensor_tensor(out=w_noisy[:, k, :], in0=sw_eo[:, k, :], scalar=fz("ei")[:, k:k + 1],
                                               in1=nz("w")[:, k * P:(k + 1) * P], op0=ALU.mult, op1=ALU.add
                                               ).then_inc(w_done, 1)
            nc.vector.tensor_tensor(b_noisy[:, :], nz("sb"), fz("eo_col"), ALU.mult).then_inc(f_done, 1)
            dve.wait_ge(f_done, 4)
            nc.vector.tensor_tensor(b_noisy[:, :], b_noisy[:, :], nz("b"), ALU.add).then_inc(b_done, 1)
            dve.wait_ge(body_in, 16)
            nc.vector.tensor_tensor(posb[:, :], bd("pos"), bd("b3"), ALU.add).then_inc(consts_set, 1)
            nc.vector.tensor_tensor(bmask[:, :, :], bd("b_tab").unsqueeze(2).to_broadcast([P, HP, KEYS]),
                                    bd("mask").unsqueeze(1).to_broadcast([P, HP, KEYS]), ALU.mult
                                    ).then_inc(consts_set, 1)
            for a in range(2):
                nc.vector.tensor_scalar(wout_par[:, a, :], bd("wout"), bd("par")[:, a:a + 1], None, ALU.mult
                                        ).then_inc(consts_set, 1)
            nc.vector.tensor_copy(h[0:1, CLS, :], bd("cls", 1)).then_inc(consts_set, 1)
            dve.wait_ge(consts_set, 8)

            for c in range(CHUNKS):
                sl = slice(c * BANK, (c + 1) * BANK)
                dve.wait_ge(exp_done, c + 1)
                nc.vector.tensor_scalar(e_sb[:, sl], e_sb[:, sl], EXP_CAP, None, ALU.min).then_inc(mish_dve, 1)
                dve.wait_ge(mish_dve, 3 * c + 1)
                nc.vector.scalar_tensor_tensor(out=n_sb[:, sl], in0=e_sb[:, sl], scalar=2.0, in1=e_sb[:, sl],
                                               op0=ALU.add, op1=ALU.mult).then_inc(mish_dve, 1)
                dve.wait_ge(mish_dve, 3 * c + 2)
                nc.vector.tensor_scalar(m_sb[:, sl], n_sb[:, sl], 2.0, None, ALU.add).then_inc(mish_dve, 1)
                dve.wait_ge(mish_dve, 3 * c + 3)
                nc.vector.reciprocal(r_sb[:, sl], m_sb[:, sl]).then_inc(gT_done, 1)
                dve.wait_ge(gT_done, 3 * c + 1)
                dve.wait_ge(gn_done, c + 1)
                nc.vector.tensor_tensor(gn_sb[:, sl], gn_sb[:, sl], r_sb[:, sl], ALU.mult).then_inc(gT_done, 1)
                dve.wait_ge(gT_done, 3 * c + 2)
                dve.wait_ge(inner_ps, c + 1)
                nc.vector.scalar_tensor_tensor(out=gT[:, sl], in0=ps[:, 2 * c + 1, :], scalar=b_noisy[:, 1:2],
                                               in1=gn_sb[:, sl], op0=ALU.add, op1=ALU.mult).then_inc(gT_done, 1)

            def stats(src, sem_done, t0, t1):
                for t in range(t0, t1):
                    nc.vector.bn_stats(st[:, t, :], src[:, t, :]).then_inc(sem_done[0], 1)
                dve.wait_ge(sem_done[0], t1)
                for t in range(t0, t1):
                    last = nc.vector.bn_aggr(mv[:, t, :], st[:, t, :])
                last.then_inc(sem_done[1], 1)

            tile_ranges = [(0, CT), (CT, 2 * CT), (CLS, CLS + 1)]
            for c in range(CHUNKS):
                dve.wait_ge(h_ps, c + 1)
                nc.vector.tensor_tensor(h[:, CT * c:CT * (c + 1), :],
                                        ps[:, 4 + c, :].rearrange("p (t d) -> p t d", d=P),
                                        posb[:, :].unsqueeze(1).to_broadcast([P, CT, P]), ALU.add).then_inc(h_done, 1)
                dve.wait_ge(h_done, c + 1)
                stats(h, (bn1_done, ln_stats), *tile_ranges[c])
            stats(h, (bn1_done, ln_stats), *tile_ranges[2])
            for c in range(CHUNKS + 1):
                dve.wait_ge(ln_rstd, c + 1)
                for t in range(*tile_ranges[c]):
                    nc.vector.tensor_scalar(xn[:, t, :], h[:, t, :], mv[:, t, 0:1], rstd[:, t:t + 1],
                                            ALU.subtract, ALU.mult).then_inc(xn_done, 1)
            for c in range(CHUNKS):
                dve.wait_ge(k_ps, c + 1)
                nc.vector.tensor_copy(kT[:, 8 * c:8 * (c + 1), 0:PATCHES],
                                      ps[:, 4 + c, :].rearrange("p (i r) -> p i r", r=PATCHES)).then_inc(k_done, 1)

            for g in range(GROUPS):
                dve.wait_ge(scores_ps, g + 1)
                src = ps[:, 4 * (g % 2):4 * (g % 2) + HP, 0:GI * KEYS].rearrange("p h (i k) -> p h i k", k=KEYS)
                nc.vector.tensor_tensor(
                    S[:, g, :, :, :], src,
                    bd("mask").unsqueeze(1).unsqueeze(1).to_broadcast([P, HP, GI, KEYS]), ALU.mult
                ).then_inc(S_masked, 1)
            GS = HP * GI

            def rows(g):
                return S[:, g, :, :, :].rearrange("p h i k -> p (h i) k")

            for g in range(GROUPS):
                dve.wait_ge(S_masked, g + 1)
                nc.vector.tensor_reduce(ssum[:, g * GS:(g + 1) * GS], rows(g), AX.X, ALU.add).then_inc(S_sum, 1)
                dve.wait_ge(S_sum, g + 1)
                nc.vector.tensor_scalar(mu[:, g * GS:(g + 1) * GS], ssum[:, g * GS:(g + 1) * GS], bd("inv_n"), None,
                                        ALU.mult).then_inc(mu_done, 1)
                dve.wait_ge(mu_done, g + 1)
                nc.vector.tensor_tensor(rows(g), rows(g),
                                        mu[:, g * GS:(g + 1) * GS].unsqueeze(2).to_broadcast([P, GS, KEYS]),
                                        ALU.subtract).then_inc(S_centred, 1)
            for g in range(GROUPS):
                dve.wait_ge(squared, g + 1)
                nc.vector.tensor_reduce(qsum[:, g * GS:(g + 1) * GS], SQ[:, g, :].rearrange("p (n k) -> p n k", k=KEYS),
                                        AX.X, ALU.add).then_inc(S_sum, 1)
            dve.wait_ge(S_sum, 2 * GROUPS)
            nc.vector.tensor_scalar(var[:, :], qsum[:, :], bd("inv_n"), ATT_EPS, ALU.mult, ALU.add
                                    ).then_inc(var_done, 1)
            dve.wait_ge(sd_done, 1)
            nc.vector.reciprocal(rs[:, :], sd[:, :]).then_inc(rs_done, 1)
            dve.wait_ge(rs_done, 1)
            nc.vector.tensor_tensor(
                rg[:, :].rearrange("p (g h i) -> p g h i", g=GROUPS, h=HP),
                rs[:, :].rearrange("p (g h i) -> p g h i", g=GROUPS, h=HP),
                bd("g_tab").unsqueeze(1).unsqueeze(3).to_broadcast([P, GROUPS, HP, GI]), ALU.mult
            ).then_inc(rg_done, 1)
            for g in range(GROUPS):
                dve.wait_ge(S_scaled, g + 1)
                nc.vector.tensor_tensor(S[:, g, :, :, :], S[:, g, :, :, :],
                                        bmask[:, :, :].unsqueeze(2).to_broadcast([P, HP, GI, KEYS]), ALU.add
                                        ).then_inc(attn_done, 1)
            for i in range(1, IMAGES, 2):
                dve.wait_ge(attnT_ps, i + 1)
                nc.vector.tensor_copy(attnT[0:KEYS, i, :], ps[0:KEYS, i % 4, :]).then_inc(attnT_dve, 1)

            dve.wait_ge(hb_done, 1)
            for c in range(CHUNKS):
                dve.wait_ge(proj_ps, c + 1)
                nc.vector.tensor_tensor(acc[:, CT * c:CT * (c + 1), :],
                                        ps[:, c, :].rearrange("p (t d) -> p t d", d=P),
                                        hb[:, CT * c:CT * (c + 1), :], ALU.add).then_inc(acc_done, 1)
            dve.wait_ge(proj_ps, CHUNKS + 1)
            nc.vector.tensor_tensor(acc[0:1, CLS, :], ps[0:1, 2, 0:P], hb[0:1, CLS, :], ALU.add).then_inc(acc_done, 1)
            dve.wait_ge(xn_done, TILES + 1)
            for c in range(CHUNKS + 1):
                dve.wait_ge(acc_done, c + 1)
                stats(acc, (bn2_done, ln2_stats), *tile_ranges[c])
            for c in range(CHUNKS + 1):
                dve.wait_ge(ln2_rstd, c + 1)
                for t in range(*tile_ranges[c]):
                    nc.vector.tensor_scalar(x2[:, t, :], acc[:, t, :], mv[:, t, 0:1], rstd[:, t:t + 1],
                                            ALU.subtract, ALU.mult).then_inc(x2_done, 1)

            dve.wait_ge(logits_ps, 1)
            nc.vector.tensor_copy(lg[:, 0:TILES, :], ps[:, 7, 0:TILES * EXPERTS].rearrange("p (t e) -> p t e", e=EXPERTS)
                                  ).then_inc(routing, 1)
            nc.vector.tensor_copy(lg[:, CLS, :], bd("iota")).then_inc(routing, 1)
            dve.wait_ge(routing, 2)
            nc.vector.tensor_copy(lg[0:1, CLS, :], ps[0:1, 7, TILES * EXPERTS:(TILES + 1) * EXPERTS]
                                  ).then_inc(routing, 1)
            dve.wait_ge(routing, 3)
            for t in range(TILES + 1):
                nc.vector.max(top[:, t, :], lg[:, t, :]).then_inc(topped, 1)
            dve.wait_ge(topped, TILES + 1)
            nc.vector.tensor_tensor(dlt[:, :], top[:, :, 1], top[:, :, 0], ALU.subtract).then_inc(routing, 1)
            for t in range(TILES + 1):
                nc.vector.max_index(top_at[:, t, :], top[:, t, :], lg[:, t, :]).then_inc(topped, 1)
            dve.wait_ge(topped, 2 * (TILES + 1))
            nc.vector.tensor_copy(top_atf[:, :, :], top_at[:, :, 0:2]).then_inc(topped, 1)
            dve.wait_ge(exp_gate, 1)
            nc.vector.tensor_scalar(den[:, :], ex[:, :], 1.0, None, ALU.add).then_inc(topped, 1)
            dve.wait_ge(topped, 2 * (TILES + 1) + 2)
            nc.vector.reciprocal(g1[:, :], den[:, :]).then_inc(topped, 1)
            dve.wait_ge(topped, 2 * (TILES + 1) + 3)
            nc.vector.tensor_tensor(g2[:, :], ex[:, :], g1[:, :], ALU.mult).then_inc(topped, 1)
            iota = bd("iota").unsqueeze(1).to_broadcast([P, TILES + 1, EXPERTS])
            for k in range(2):
                nc.vector.tensor_tensor(sel[:, k, :, :], iota,
                                        top_atf[:, :, k:k + 1].to_broadcast([P, TILES + 1, EXPERTS]), ALU.is_equal
                                        ).then_inc(topped, 1)
            dve.wait_ge(topped, 2 * (TILES + 1) + 6)
            for k, gk in ((0, g1), (1, g2)):
                nc.vector.tensor_tensor(sel[:, k, :, :], sel[:, k, :, :],
                                        gk[:, :].unsqueeze(2).to_broadcast([P, TILES + 1, EXPERTS]), ALU.mult
                                        ).then_inc(topped, 1)
            dve.wait_ge(topped, 2 * (TILES + 1) + 8)
            nc.vector.tensor_tensor(gate[:, :, :], sel[:, 0, :, :], sel[:, 1, :, :], ALU.add).then_inc(gates_done, 1)

            dve.wait_ge(gates_done, 1)
            nc.vector.memset(u[2][:, :, :], 0.0).then_inc(y_read, 3)

            def expert(it, b):
                e = 2 * it + b
                dve.wait_ge(cls_hid_ps, e + 1)
                nc.vector.tensor_tensor(hid[2][:, :, :], ps[:, 6, 0:2 * FT].rearrange("p (f n) -> p f n", n=2),
                                        w1_in[b][:, HIDDEN:HIDDEN + FT].unsqueeze(2).to_broadcast([P, FT, 2]), ALU.add
                                        ).then_inc(cls_hid_sum, 1)
                dve.wait_ge(cls_hid_sum, e + 1)
                nc.vector.tensor_scalar(hid[2][:, :, :], hid[2][:, :, :], 0.0, None, ALU.max
                                        ).then_inc(cls_hid_done, 1)
                for c in range(3):
                    n = 3 * e + c + 1
                    r, k = CR[c], CN[c]
                    dve.wait_ge(y_ps, n)
                    dve.wait_ge(x2b_done, n)
                    yb = ps[0:r, [4, 5, 7][c], 0:k * P].rearrange("p (t d) -> p t d", d=P)
                    nc.vector.tensor_tensor(y[c][0:r, :, :], yb, x2b[c][0:r, :, :], ALU.add).then_inc(y_read, 1)
                    dve.wait_ge(y_read, n + 3)
                    for t in range(k):
                        last = nc.vector.bn_stats(yst[c][0:r, t, :], y[c][0:r, t, :])
                    last.then_inc(y_stats, 1)
                    dve.wait_ge(y_stats, n)
                    nc.vector.tensor_tensor(ymv[c][0:r, :, :], yst[c][0:r, :, 1:3], yst[c][0:r, :, 4:6], ALU.add
                                            ).then_inc(y_parts, 1)
                    nc.vector.tensor_tensor(yd[c][0:r, :], yst[c][0:r, :, 1], yst[c][0:r, :, 4], ALU.subtract
                                            ).then_inc(y_parts, 1)
                    dve.wait_ge(y_parts, 4 * n - 2)
                    nc.vector.tensor_scalar(ymean[c][0:r, :], ymv[c][0:r, :, 0], 0.5, None, ALU.mult
                                            ).then_inc(y_parts, 1)
                    nc.vector.scalar_tensor_tensor(out=yd[c][0:r, :], in0=yd[c][0:r, :], scalar=P / 4.0,
                                                   in1=yd[c][0:r, :], op0=ALU.mult, op1=ALU.mult
                                                   ).then_inc(y_parts, 1)
                    dve.wait_ge(y_parts, 4 * n)
                    nc.vector.tensor_tensor(yd[c][0:r, :], yd[c][0:r, :], ymv[c][0:r, :, 1], ALU.add
                                            ).then_inc(y_var, 1)
                    dve.wait_ge(y_var, n)
                    nc.vector.tensor_scalar(yve[c][0:r, :], yd[c][0:r, :], 1.0 / P, MOE_EPS, ALU.mult, ALU.add
                                            ).then_inc(y_ve, 1)
                    for t in range(k):
                        last = nc.vector.scalar_tensor_tensor(
                            out=u[c][0:r, t, :], in0=y[c][0:r, t, :], scalar=ymean[c][0:r, t:t + 1],
                            in1=gb2_in[b][0:r, 0, :], op0=ALU.subtract, op1=ALU.mult)
                    last.then_inc(u_done, 1)
                    dve.wait_ge(u_done, n)
                    dve.wait_ge(y_a, n)
                    for t in range(k):
                        at = acc[0:r, C0[c] + t, :]
                        last = nc.vector.scalar_tensor_tensor(out=at, in0=u[c][0:r, t, :], scalar=ya[c][0:r, t:t + 1],
                                                              in1=at, op0=ALU.mult, op1=ALU.add)
                    last.then_inc(moe_acc, 1)

            with dve.Fori(0, EXPERTS // 2) as it:
                for b in range(2):
                    dve.wait_ge(gb2_loaded[b], 16 * (it + 1))
                    expert(it, b)
            dve.wait_ge(moe_acc, 3 * EXPERTS)
            for c in range(CHUNKS):
                dve.wait_ge(beta_ps, c + 1)
                nc.vector.tensor_tensor(acc[:, CT * c:CT * (c + 1), :], acc[:, CT * c:CT * (c + 1), :],
                                        ps[:, 3 - c, :].rearrange("p (t d) -> p t d", d=P), ALU.add
                                        ).then_inc(final_done, 1)
            dve.wait_ge(beta_ps, CHUNKS + 1)
            nc.vector.tensor_tensor(acc[0:1, CLS, :], acc[0:1, CLS, :], ps[0:1, 6, 0:P], ALU.add
                                    ).then_inc(final_done, 1)

        @block.tensor
        def _(pe):
            mm = nc.tensor.matmul

            pe.wait_ge(w_done, 4)
            for c in range(CHUNKS):
                pe.wait_ge(patches_in[c], 16)
                for k, done in ((0, gate_ps), (1, inner_ps)):
                    for half in range(HALVES):
                        last = mm(ps[:, 2 * c + k, :], w_noisy[:, 2 * k + half, :], xT[:, c, half, :],
                                  start=(half == 0), stop=(half == HALVES - 1))
                    last.then_inc(done, 1)
            pe.wait_ge(body_in, 16)
            for c in range(CHUNKS):
                pe.wait_ge(gT_done, 3 * (c + 1))
                for t in range(CT * c, CT * (c + 1)):
                    last = mm(ps[:, 4 + c, (t % CT) * P:(t % CT + 1) * P], gT[:, t * P:(t + 1) * P], bd("w3T"),
                              start=True, stop=True)
                last.then_inc(h_ps, 1)
            for c in range(CHUNKS):
                for t in range(CT * c, CT * (c + 1)):
                    pe.wait_ge(xn_done, t + 1)
                    last = nc.tensor.transpose(ps[:, 6 + c, (t % CT) * P:(t % CT + 1) * P], xn[:, t, :], ident)
                last.then_inc(xnT_ps, 1)
            pe.wait_ge(xn_done, TILES + 1)
            pe.wait_ge(gate_read, 2)
            nc.tensor.transpose(ps[:, 2, 0:1], xn[0:1, CLS, :], ident[0:1, 0:1]).then_inc(xnT_ps, 1)
            for c in range(CHUNKS):
                pe.wait_ge(xnT_done, c + 1)
                pe.wait_ge(h_done, c + 1)
                cols = xnT[:, c * BANK:(c + 1) * BANK]
                mm(ps[:, c, :], bd("wq"), cols, start=True, stop=True).then_inc(q_ps, 1)
                mm(ps[:, 4 + c, :], bd("wk"), cols, start=True, stop=True).then_inc(k_ps, 1)
            pe.wait_ge(xnT_done, CHUNKS + 1)
            col = xnT[:, TOKENS:TOKENS + 1]
            mm(ps[:, 2, 0:1], bd("wk"), col, start=True, stop=True)
            mm(ps[:, 2, 1:2], bd("wv"), col, start=True, stop=True)
            mm(ps[PATCHES:KEYS, 2, P:2 * P], col, bd("wv"), start=True, stop=True).then_inc(cls_ps, 1)
            for g in range(GROUPS):
                if g == 3:
                    pe.wait_ge(cls_o_done, 1)
                    pe.wait_ge(cls_done, 2)
                for i in range(GI):
                    n = GI * g + i
                    last = mm(ps[0:PATCHES, [3, 6, 7, 2][g], i * P:(i + 1) * P],
                              xnT[:, n * PATCHES:(n + 1) * PATCHES], bd("wv"), start=True, stop=True)
                last.then_inc(v_ps, 1)
            pe.wait_ge(q_done, 4)
            pe.wait_ge(k_done, 2)
            pe.wait_ge(v_done, GROUPS)
            for g in range(GROUPS):
                if g >= 2:
                    pe.wait_ge(S_masked, g - 1)
                for i in range(GI):
                    n = GI * g + i
                    for h_ in range(HP):
                        rows = slice(32 * h_, 32 * (h_ + 1))
                        last = mm(ps[:, 4 * (g % 2) + h_, i * KEYS:(i + 1) * KEYS],
                                  qTm[rows, n, :, :], kT[rows, n, :], start=True, stop=True)
                last.then_inc(scores_ps, 1)

            def turn(n):
                g, i = n // GI, n % GI
                if i == 0:
                    pe.wait_ge(attn_done, g + 1)
                if n >= 4:
                    if n % 2 == 0:
                        pe.wait_ge(attnT_act, n // 2 - 1)
                    else:
                        pe.wait_ge(attnT_dve, (n - 1) // 2 - 1)
                for h_ in range(HP):
                    last = nc.tensor.transpose(ps[0:KEYS, n % 4, h_ * P:(h_ + 1) * P], S[:, g, h_, i, :], ident)
                last.then_inc(attnT_ps, 1)

            def weigh(n):
                g, i = n // GI, n % GI
                pe.wait_ge(attnT_dve if n % 2 else attnT_act, n // 2 + 1)
                for h_ in range(HP):
                    last = mm(ps[32 * h_:32 * (h_ + 1), 4 + g, i * P:(i + 1) * P],
                              v[:, n, 32 * h_:32 * (h_ + 1)], attnT[0:KEYS, n, h_ * P:(h_ + 1) * P],
                              start=True, stop=True)
                if i == GI - 1:
                    last.then_inc(o_ps, 1)

            AHEAD = 3
            for n in range(IMAGES + AHEAD):
                if n < IMAGES:
                    turn(n)
                if n >= AHEAD:
                    weigh(n - AHEAD)
            for c in range(CHUNKS):
                pe.wait_ge(o_done, 2 * (c + 1))
                if c == 0:
                    pe.wait_ge(attnT_act, IMAGES // 2)
                    pe.wait_ge(attnT_dve, IMAGES // 2)
                for t in range(CT * c, CT * (c + 1)):
                    for a in range(2):
                        last = mm(ps[:, c, (t % CT) * P:(t % CT + 1) * P], oT[:, a, 2 * t:2 * t + 2, :].rearrange("p i r -> p (i r)"),
                                  wout_par[:, a, :], start=(a == 0), stop=(a == 1))
                last.then_inc(proj_ps, 1)
            mm(ps[0:1, 2, 0:P], v_cls_b[:, 0:1], bd("wout"), start=True, stop=True).then_inc(proj_ps, 1)
            for c in range(CHUNKS + 1):
                a, b = [(0, CT), (CT, 2 * CT), (CLS, CLS + 1)][c]
                for t in range(a, b):
                    pe.wait_ge(x2_done, t + 1)
                    if c < CHUNKS:
                        last = nc.tensor.transpose(ps[:, 4 + c, (t % CT) * P:(t % CT + 1) * P], x2[:, t, :], ident)
                    else:
                        last = nc.tensor.transpose(ps[:, 6, 0:1], x2[0:1, t, :], ident[0:1, 0:1])
                last.then_inc(x2T_ps, 1)
            for t in range(TILES):
                pe.wait_ge(x2T_done, t // CT + 1)
                mm(ps[:, 7, t * EXPERTS:(t + 1) * EXPERTS], x2T[:, t * P:(t + 1) * P], bd("router"),
                   start=True, stop=True)
            pe.wait_ge(x2T_done, CHUNKS + 1)
            mm(ps[0:1, 7, TILES * EXPERTS:(TILES + 1) * EXPERTS], x2T[:, TOKENS:TOKENS + 1], bd("router"),
               start=True, stop=True).then_inc(logits_ps, 1)

            def expert(it, b):
                e = 2 * it + b
                pe.wait_ge(w1_lo_done, e + 1)
                for c in range(3):
                    cols = slice(c * BANK, c * BANK + CW[c])
                    pe.wait_ge(x2T_lo_done, c + 1)
                    for f in range(FT):
                        w = slice(f * P, (f + 1) * P)
                        if c < CHUNKS:
                            o = ps[:, f, :]
                            if c > 0:
                                pe.wait_ge(hid_done, (2 * e + c - 1) * FT + f + 1)
                        else:
                            o = ps[:, 6, 2 * f:2 * f + 2]
                        mm(o, w1_hi[b][:, w], x2T_lo[:, cols], start=True, stop=False)
                        mm(o, w1_lo[b][:, w], x2T_hi[:, cols], start=False, stop=False)
                        last = mm(o, w1_hi[b][:, w], x2T_hi[:, cols], start=False, stop=True)
                        if c < CHUNKS:
                            last.then_inc(hid_ps, 1)
                last.then_inc(cls_hid_ps, 1)
                pe.wait_ge(w2_loaded[b], 16 * (it + 1))
                for c in range(3):
                    if c < CHUNKS:
                        pe.wait_ge(hid_done, (2 * e + c + 1) * FT)
                    else:
                        pe.wait_ge(cls_hid_done, e + 1)
                    pe.wait_ge(y_read, 3 * e + c + 1)
                    r = CR[c]
                    for t in range(CN[c]):
                        for f in range(FT):
                            last = mm(ps[0:r, [4, 5, 7][c], t * P:(t + 1) * P], hid[c][:, f, t * P:t * P + r],
                                      w2_in[b][:, f, :], start=(f == 0), stop=(f == FT - 1))
                    last.then_inc(y_ps, 1)

            with pe.Fori(0, EXPERTS // 2) as it:
                for b in range(2):
                    expert(it, b)
            pe.wait_ge(gates_done, 1)
            for c in range(CHUNKS + 1):
                a, b = [(0, CT), (CT, 2 * CT), (CLS, CLS + 1)][c]
                for t in range(a, b):
                    last = nc.tensor.transpose(ps[0:EXPERTS, c, (t - a) * P:(t - a + 1) * P], gate[:, t, :], ident)
                last.then_inc(gateT_ps, 1)
            pe.wait_ge(gateT_done, 3)
            for c in range(CHUNKS + 1):
                a, b = [(0, CT), (CT, 2 * CT), (CLS, CLS + 1)][c]
                bank = [3, 2, 6][c]
                r = CR[c]
                for t in range(a, b):
                    last = mm(ps[0:r, bank, (t - a) * P:(t - a + 1) * P], gateT[:, t, 0:r], bd("beta", EXPERTS),
                              start=True, stop=True)
                last.then_inc(beta_ps, 1)


def constants():
    pos = np.arange(PATCHES, dtype=np.float32)[:, None]
    div = np.exp(np.arange(0, P, 2, dtype=np.float32) * np.float32(-np.log(10000.0) / P))
    ang = pos * div
    pe = np.stack([np.sin(ang), np.cos(ang)], axis=-1).reshape(PATCHES, P).astype(np.float32)
    row = np.arange(P) % PATCHES
    mask = np.concatenate([np.arange(PATCHES)[None, :] <= row[:, None], np.ones((P, 1), bool)], 1)
    par = (np.arange(P)[:, None] // HD % 2) == np.arange(2)[None, :]
    f = np.float32
    return {"pos": np.tile(pe, (2, 1)), "ident": np.eye(P, dtype=f), "mask": mask.astype(f),
            "inv_n": (1.0 / (row + 2.0))[:, None].astype(f), "par_scaled": (par * float(P) ** -0.5).astype(f),
            "par": par.astype(f), "iota": np.tile(np.arange(EXPERTS, dtype=f), (P, 1))}


def pack(spec, parts):
    cols = []
    for name, width in spec:
        a = parts[name]
        assert a.shape[1] == width and a.dtype == np.float32, name
        cols.append(np.concatenate([a, np.zeros((P - a.shape[0], width), np.float32)], 0))
    return np.ascontiguousarray(np.concatenate(cols, 1))


def kernel(**inputs):
    import concourse.bacc as bacc
    from concourse.bass_utils import run_bass_kernel_spmd

    a = {k: np.asarray(v) for k, v in inputs.items()}

    def rows(vec):
        return np.broadcast_to(vec.reshape(1, -1), (P, vec.size))

    def by_feature(m):
        return m.T.reshape(HALVES, P, P).transpose(1, 0, 2).reshape(P, HALVES * P)

    t = {k[7:]: v for k, v in a.items() if k.startswith("L0_tok_")}
    noise = pack(NOISE_COLS, {
        "w": np.concatenate([by_feature(t["W1_w"]), by_feature(t["W2_w"])], 1),
        "sw": np.concatenate([by_feature(t["W1_sw"]), by_feature(t["W2_sw"])], 1),
        "ei": np.concatenate([t["eps_in1"].reshape(HALVES, P).T, t["eps_in2"].reshape(HALVES, P).T], 1),
        "eo_row": np.concatenate([rows(t["eps_out1"]), rows(t["eps_out2"])], 1),
        "eo_col": np.stack([t["eps_out1"], t["eps_out2"]], 1),
        "b": np.stack([t["W1_b"], t["W2_b"]], 1),
        "sb": np.stack([t["W1_sb"], t["W2_sb"]], 1)})
    norm_g, norm_b = a["L0_attn_norm_g"].reshape(HEADS), a["L0_attn_norm_b"].reshape(HEADS)

    def head_table(vec):
        return np.repeat(vec.reshape(HP, 2).T, PATCHES, axis=0)

    body = pack(BODY_COLS, dict(
        constants(), w3T=t["W3_w"].T, b3=rows(t["W3_b"]), cls=a["cls_tok"].reshape(1, P),
        wq=a["L0_attn_w_qkv"][:, 0:P], wk=a["L0_attn_w_qkv"][:, P:2 * P], wv=a["L0_attn_w_qkv"][:, 2 * P:3 * P],
        wout=a["L0_attn_w_out"], bout=rows(a["L0_attn_b_out"]), beta=a["L0_ffn_beta"],
        router=a["L0_ffn_router_w"], g_tab=head_table(norm_g), b_tab=head_table(norm_b),
        b_col=np.repeat(norm_b, HD)[:, None]))
    px = a["x"].reshape(IMAGES, GRID, HALVES, PATCH // HALVES, GRID, PATCH)
    px = px.transpose(3, 5, 2, 0, 1, 4).reshape(P, HALVES, CHUNKS, BANK).transpose(0, 2, 1, 3)
    w1b1 = np.concatenate([a["L0_ffn_w1"], a["L0_ffn_b1"].reshape(EXPERTS, FT, P).transpose(0, 2, 1)], 2)
    arrays = {
        "patches": px, "noise": noise, "body": body, "w1b1": w1b1,
        "w2": a["L0_ffn_w2"].reshape(EXPERTS, FT, P, P).transpose(0, 2, 1, 3),
        "gb2": np.stack([a["L0_ffn_gamma"], a["L0_ffn_b2"]], 1)}
    arrays = {k: np.ascontiguousarray(v) for k, v in arrays.items()}

    nc = bacc.Bacc("TRN2", target_bir_lowering=False, num_devices=1)
    args = [nc.dram_tensor(k, v.shape, mybir.dt.from_np(v.dtype), kind="ExternalInput").ap()
            for k, v in arrays.items()]
    out = nc.dram_tensor("out", (IMAGES, KEYS, P), F32, kind="ExternalOutput").ap()
    vit_tower(nc, *args, out)
    r = run_bass_kernel_spmd(nc, [arrays], core_ids=[0])
    return r.results[0]["out"]
```

```python
from contextlib import ExitStack

import numpy as np
import concourse.bass as bass
from concourse import mybir

F32 = mybir.dt.float32
F32R = mybir.dt.float32r
U32 = mybir.dt.uint32
ALU = mybir.AluOpType
ACT = mybir.ActivationFunctionType
AX = mybir.AxisListType

P = 128
IMAGES, SIDE, PATCH = 16, 128, 16
GRID = SIDE // PATCH
PATCHES = GRID * GRID
TOKENS = IMAGES * PATCHES
FEATURES = PATCH * PATCH
HALVES = FEATURES // P
TILES = TOKENS // P
CLS = TILES
BANK = 512
CHUNKS = TOKENS // BANK
CT = TILES // CHUNKS
HEADS, HD = 8, 16
HP = HEADS // 2
KEYS = PATCHES + 1
GROUPS = 4
GI = IMAGES // GROUPS
EXPERTS, HIDDEN = 8, 512
FT = HIDDEN // P
LN1_EPS, LN2_EPS, ATT_EPS, MOE_EPS = 1e-5, 1e-5, 1e-8, 1e-6
EXP_CAP = 16384.0

NOISE_COLS = [("w", 4 * P), ("sw", 4 * P), ("ei", 4), ("eo_row", 2 * P), ("eo_col", 2), ("b", 2), ("sb", 2)]
BODY_COLS = [("w3T", P), ("b3", P), ("pos", P), ("ident", P), ("cls", P), ("wq", P), ("wk", P), ("wv", P),
             ("wout", P), ("bout", P), ("beta_rep", P), ("gamma_rows", P), ("b2T", EXPERTS),
             ("sel", TILES + 1), ("router", EXPERTS), ("mask", KEYS), ("inv_n", 1),
             ("par_scaled", 2), ("par", 2), ("iota", EXPERTS), ("g_tab", HP), ("b_tab", HP), ("b_col", 1)]


def columns(spec):
    at, found = 0, {}
    for name, width in spec:
        found[name] = (at, at + width)
        at += width
    return found, at


NOISE_AT, NOISE_W = columns(NOISE_COLS)
BODY_AT, BODY_W = columns(BODY_COLS)


def vit_tower(nc, patches, noise, body, w1b1, w2, gb2, out):
    ctx = ExitStack()
    with ctx:
        def sb(name, shape, dtype=F32):
            return ctx.enter_context(nc.sbuf_tensor(name, shape, dtype))

        def sem(name):
            return ctx.enter_context(nc.semaphore(name))

        xT_oT = sb("xT_oT", [P, CHUNKS * HALVES * BANK])
        xT = xT_oT[:, :].rearrange("p (c h n) -> p c h n", c=CHUNKS, h=HALVES)
        noise_sb = sb("noise_sb", [P, NOISE_W])
        body_sb = sb("body_sb", [P, BODY_W])
        NF0, NF1 = NOISE_AT["ei"][0], NOISE_AT["eo_col"][1]
        NFW = NF1 - NF0
        f_abs = sb("f_abs", [P, NFW])
        f_root = sb("f_root", [P, NFW])
        f_sign = sb("f_sign", [P, NFW])
        f_noise = sb("f_noise", [P, NFW])
        sw_eo = sb("sw_eo", [P, 4, P])
        w_noisy = sb("w_noisy", [P, 4, P])
        b_noisy = sb("b_noisy", [P, 2])
        posb = sb("posb", [P, P])
        S = sb("S", [P, GROUPS, HP, GI, KEYS])
        SQ = sb("SQ", [P, GROUPS, HP * GI * KEYS])
        parts = SQ[:, :, :].rearrange("p g n -> p (g n)")
        g_sb = parts[:, 0 * TOKENS:1 * TOKENS]
        n_sb = parts[:, 1 * TOKENS:2 * TOKENS]
        e_sb = parts[:, 2 * TOKENS:3 * TOKENS]
        m_sb = parts[:, 3 * TOKENS:4 * TOKENS]
        pairs = sb("pairs", [P, BANK])
        inv_pair = sb("inv_pair", [P, BANK // 2])
        attnT = sb("attnT", [P, CHUNKS * FT, HP * P])
        last_parts = attnT[:, :, :].rearrange("p n m -> p (n m)")
        r_sb = last_parts[:, 0:TOKENS]
        gn_sb = last_parts[:, TOKENS:2 * TOKENS]
        gT = sb("gT", [P, TOKENS])
        table_scrap = sb("table_scrap", [P, 2])
        zeros = sb("zeros", [P, P])
        h = sb("h", [P, TILES + 1, P])
        hb = sb("hb", [P, TILES + 1, P])
        st = sb("st", [P, TILES + 1, 6])
        mv = sb("mv", [P, TILES + 1, 2])
        ve = sb("ve", [P, TILES + 1])
        rstd = sb("rstd", [P, TILES + 1])
        minus_half = sb("minus_half", [P, TILES + 1])
        xn = sb("xn", [P, TILES + 1, P])
        xnT = sb("xnT", [P, IMAGES, KEYS])
        qTm = sb("qTm", [P, IMAGES, 2, PATCHES])
        kT = sb("kT", [P, IMAGES, KEYS])
        v = sb("v", [KEYS, IMAGES, P])
        xnT_cls = xnT[:, 0, PATCHES:KEYS]
        v_cls_b = sb("v_cls_b", [P, 1])
        NS = GROUPS * HP * GI
        ssum = sb("ssum", [P, NS])
        mu = sb("mu", [P, NS])
        qsum = sb("qsum", [P, NS])
        var = sb("var", [P, NS])
        sd = sb("sd", [P, NS])
        rs = sb("rs", [P, NS])
        rg = sb("rg", [P, NS])
        bmask = sb("bmask", [P, HP, KEYS])
        oT = xT_oT[:, :].rearrange("p (a i r) -> p a i r", a=2, i=IMAGES)
        wout_par = sb("wout_par", [P, 2, P])
        acc = sb("acc", [P, TILES + 1, P])
        x2 = sb("x2", [P, TILES + 1, P])
        x2T = sb("x2T", [P, TOKENS])
        x2T_hi = sb("x2T_hi", [P, TOKENS], F32R)
        x2T_lo = sb("x2T_lo", [P, TOKENS], F32R)
        x2T_cls = sb("x2T_cls", [P, 1])
        cls_hid = sb("cls_hid", [P, EXPERTS, FT])
        cls_yT = sb("cls_yT", [P, EXPERTS])
        E0, E1 = TILES * EXPERTS, (TILES + 1) * EXPERTS
        cls_st = sb("cls_st", [P, 6])
        cls_mv = sb("cls_mv", [P, 2])
        cls_ve = sb("cls_ve", [P, 1])
        cls_rs = sb("cls_rs", [P, 1])
        cls_rows = sb("cls_rows", [P, P])
        beta_sel = sb("beta_sel", [P, TILES, P])
        lg = sb("lg", [P, TILES + 1, EXPERTS])
        top = sb("top", [P, TILES + 1, 8])
        top_at = sb("top_at", [P, TILES + 1, 8], U32)
        top_atf = sb("top_atf", [P, TILES + 1, 2])
        dlt = sb("dlt", [P, TILES + 1])
        ex = sb("ex", [P, TILES + 1])
        den = sb("den", [P, TILES + 1])
        g1 = sb("g1", [P, TILES + 1])
        g2 = sb("g2", [P, TILES + 1])
        sel = sb("sel", [P, 2, TILES + 1, EXPERTS])
        gate = sb("gate", [P, TILES + 1, EXPERTS])
        gateT = sb("gateT", [P, P])
        w1_all = sb("w1_all", [P, EXPERTS, HIDDEN + FT])
        w1_in = [sb(f"w1_in{b}", [P, HIDDEN + FT]) for b in range(2)]
        w2_all = sb("w2_all", [P, EXPERTS, FT, P])
        w1_hi = [sb(f"w1_hi{b}", [P, HIDDEN], F32R) for b in range(2)]
        w1_lo = [sb(f"w1_lo{b}", [P, HIDDEN], F32R) for b in range(2)]
        gb2_in = [sb(f"gb2_in{b}", [P, 2, P]) for b in range(2)]
        V_BANK = [4, 5, 6, 4]
        WARM = 16
        LN_TILES = [(CLS, CLS + 1), (0, CT), (CT, 2 * CT)]
        hid = [attnT[:, FT * c:FT * (c + 1), :] for c in range(CHUNKS)]

        S_flat = S[:, :, :, :, :].rearrange("p g h i k -> p (g h i k)")

        def over_S(n):
            return S_flat[:, n * BANK:(n + 1) * BANK].rearrange("p (t d) -> p t d", d=P)

        x2b = [over_S(c) for c in range(CHUNKS)]
        y = [over_S(2 + c) for c in range(CHUNKS)]
        u = [over_S(4 + c) for c in range(CHUNKS)]
        yst = [sb(f"yst{c}", [P, CT, 6]) for c in range(CHUNKS)]
        ymv = [sb(f"ymv{c}", [P, CT, 2]) for c in range(CHUNKS)]
        yd = [sb(f"yd{c}", [P, CT]) for c in range(CHUNKS)]
        ymean = [sb(f"ymean{c}", [P, CT]) for c in range(CHUNKS)]
        yve = [sb(f"yve{c}", [P, CT]) for c in range(CHUNKS)]
        yrs = [sb(f"yrs{c}", [P, CT]) for c in range(CHUNKS)]
        ya = [sb(f"ya{c}", [P, CT]) for c in range(CHUNKS)]

        ps = ctx.enter_context(nc.psum_tensor("ps", [P, 8, BANK], F32))

        def nz(name):
            a, b = NOISE_AT[name]
            return noise_sb[:, a:b]

        def bd(name, rows=P):
            a, b = BODY_AT[name]
            return body_sb[0:rows, a:b]

        def fz(name):
            a, b = NOISE_AT[name]
            return f_noise[:, a - NF0:b - NF0]

        ident = bd("ident")

        noise_in, body_in, patches_in = sem("noise_in"), sem("body_in"), [sem("patches_in0"), sem("patches_in1")]
        w1_loaded, w2_loaded = sem("w1_loaded"), sem("w2_loaded")
        w1_in_loaded = [sem("w1_in_loaded0"), sem("w1_in_loaded1")]
        gb2_loaded = [sem("gb2_loaded0"), sem("gb2_loaded1")]
        f_parts, f_done, w_done, b_done = sem("f_parts"), sem("f_done"), sem("w_done"), sem("b_done")
        f_abs_done = sem("f_abs_done")
        consts_set, pow_const = sem("consts_set"), sem("pow_const")
        gate_ps, inner_ps = sem("gate_ps"), sem("inner_ps")
        gate_read, exp_done, mish_dve, gn_done, gT_done = (
            sem("gate_read"), sem("exp_done"), sem("mish_dve"), sem("gn_done"), sem("gT_done"))
        recip_steps = sem("recip_steps")
        h_ps, h_done, hb_done = sem("h_ps"), sem("h_done"), sem("hb_done")
        ln_stats, ln_ve, ln_rstd = sem("ln_stats"), sem("ln_ve"), sem("ln_rstd")
        xn_done, xnT_ps, xnT_done = sem("xn_done"), sem("xnT_ps"), sem("xnT_done")
        q_ps, k_ps, v_ps, cls_ps = sem("q_ps"), sem("k_ps"), sem("v_ps"), sem("cls_ps")
        q_done, k_done, v_done, cls_done = sem("q_done"), sem("k_done"), sem("v_done"), sem("cls_done")
        scores_ps, S_masked, S_sum, mu_done, S_centred = (
            sem("scores_ps"), sem("S_masked"), sem("S_sum"), sem("mu_done"), sem("S_centred"))
        T_masked, squared, var_done, sd_done, rs_done, rg_done = (
            sem("T_masked"), sem("squared"), sem("var_done"), sem("sd_done"), sem("rs_done"), sem("rg_done"))
        S_scaled, attn_done = sem("S_scaled"), sem("attn_done")
        sq_sum = sem("sq_sum")
        attnT_ps, attnT_done = sem("attnT_ps"), sem("attnT_done")
        o_ps, o_done, proj_ps, acc_done = sem("o_ps"), sem("o_done"), sem("proj_ps"), sem("acc_done")
        ln2_stats, ln2_ve, ln2_rstd, x2_done = sem("ln2_stats"), sem("ln2_ve"), sem("ln2_rstd"), sem("x2_done")
        x2T_ps, x2T_done, x2T_hi_done, x2T_lo_done = (
            sem("x2T_ps"), sem("x2T_done"), sem("x2T_hi_done"), sem("x2T_lo_done"))
        logits_ps, routing, exp_gate, gates_done = sem("logits_ps"), sem("routing"), sem("exp_gate"), sem("gates_done")
        w1_hi_done, w1_lo_done = sem("w1_hi_done"), sem("w1_lo_done")
        hid_ps, hid_done = sem("hid_ps"), sem("hid_done")
        x2T_cls_done, cls_hid_ps, cls_hid_done = sem("x2T_cls_done"), sem("cls_hid_ps"), sem("cls_hid_done")
        cls_yT_ps, cls_yT_done, cls_y_ps, cls_row_done, cls_ve_done, cls_rs_done = (
            sem("cls_yT_ps"), sem("cls_yT_done"), sem("cls_y_ps"), sem("cls_row_done"), sem("cls_ve_done"),
            sem("cls_rs_done"))
        zeros_set = sem("zeros_set")
        beta_sel_done = sem("beta_sel_done")
        y_ps, y_read = sem("y_ps"), sem("y_read")
        x2b_done, y_stats, y_parts, y_var, y_ve, y_rs, y_a, u_done, moe_acc = (
            sem("x2b_done"), sem("y_stats"), sem("y_parts"), sem("y_var"), sem("y_ve"), sem("y_rs"), sem("y_a"), sem("u_done"),
            sem("moe_acc"))
        gateT_ps, gateT_done, beta_ps, final_done, stored = (
            sem("gateT_ps"), sem("gateT_done"), sem("beta_ps"), sem("final_done"), sem("stored"))

        bn1_done, bn2_done, topped = sem("bn1_done"), sem("bn2_done"), sem("topped")

        block = ctx.enter_context(nc.Block())

        @block.sync
        def _(sp):
            sp.dma_start(noise_sb[:, :], noise).then_inc(noise_in, 16)
            for c in range(CHUNKS):
                sp.dma_start(xT[:, c, :, :], patches[:, c, :, :]).then_inc(patches_in[c], 16)
            sp.dma_start(body_sb[:, :], body).then_inc(body_in, 16)

            sp.dma_start(w1_all[:, :, :], w1b1).then_inc(w1_loaded, 16)
            sp.dma_start(w2_all[:, :, :, :], w2).then_inc(w2_loaded, 16)

            def load_expert(e, b):
                sp.dma_start(w1_in[b][:, :], w1b1[:, bass.ds(e, 1), :].rearrange("p a n -> p (a n)")
                             ).then_inc(w1_in_loaded[b], 16)
                sp.dma_start(gb2_in[b][:, :, :], gb2[bass.ds(e, 1), :, :].to_broadcast([P, 2, P])
                             ).then_inc(gb2_loaded[b], 16)

            for b in range(2):
                load_expert(b, b)
            with sp.Fori(0, EXPERTS // 2 - 1) as it:
                for b in range(2):
                    sp.wait_ge(moe_acc, 2 * (2 * it + b + 1))
                    load_expert(2 * it + b + 2, b)

            sp.wait_ge(final_done, CHUNKS + 1)
            sp.dma_start(out[:, 0:1, :].rearrange("t r d -> r t d"),
                         acc[0:1, CLS:CLS + 1, :].to_broadcast([1, IMAGES, P])).then_inc(stored, 16)
            for c in range(CHUNKS):
                sp.wait_ge(moe_acc, 2 * (EXPERTS - 1) + c + 1)
                for b in range(2):
                    rows = acc[PATCHES * b:PATCHES * (b + 1), CT * c:CT * (c + 1), :]
                    dst = out[2 * CT * c + b:2 * CT * (c + 1):2, 1:KEYS, :].rearrange("t r d -> r t d")
                    sp.dma_start(dst, rows).then_inc(stored, 16)
            sp.wait_ge(stored, 16 * (2 * CHUNKS + 1))

        @block.gpsimd
        def _(pool):
            nc.gpsimd.memset(minus_half[:, :], -0.5).then_inc(pow_const, 1)
            pool.wait_ge(pow_const, 1)

            def ln_power(stats, ve_sem, out_sem, eps, n):
                a, b = LN_TILES[n]
                pool.wait_ge(stats, n + 1)
                nc.gpsimd.tensor_scalar(ve[:, a:b], mv[:, a:b, 1], eps, None, ALU.add).then_inc(ve_sem, 1)
                pool.wait_ge(ve_sem, n + 1)
                nc.gpsimd.tensor_tensor(rstd[:, a:b], ve[:, a:b], minus_half[:, a:b], ALU.pow).then_inc(out_sem, 1)

            ln_power(ln_stats, ln_ve, ln_rstd, LN1_EPS, 0)
            for c in range(CHUNKS):
                sl = slice(c * BANK, (c + 1) * BANK)
                pool.wait_ge(mish_dve, 3 * c + 2)
                pool.wait_ge(gate_read, c + 1)
                nc.gpsimd.tensor_tensor(gn_sb[:, sl], g_sb[:, sl], n_sb[:, sl], ALU.mult).then_inc(gn_done, 1)
                if c == 0:
                    pool.wait_ge(xn_done, 1)
                    ln_power(ln2_stats, ln2_ve, ln2_rstd, LN2_EPS, 0)

            for n in (1, 2):
                ln_power(ln_stats, ln_ve, ln_rstd, LN1_EPS, n)

            def centre_masked(g):
                pool.wait_ge(S_centred, g + 1)
                t = S[:, g, :, :, :].rearrange("p h i k -> p (h i) k")
                nc.gpsimd.tensor_tensor(t, t, bd("mask").unsqueeze(1).to_broadcast([P, HP * GI, KEYS]), ALU.mult
                                        ).then_inc(T_masked, 1)

            def scale(g):
                pool.wait_ge(rg_done, g + 1)
                t = S[:, g, :, :, :].rearrange("p h i k -> p (h i) k")
                r = rg[:, g * HP * GI:(g + 1) * HP * GI].unsqueeze(2).to_broadcast([P, HP * GI, KEYS])
                nc.gpsimd.tensor_tensor(t, t, r, ALU.mult).then_inc(S_scaled, 1)

            centre_masked(0)
            pool.wait_ge(h_done, CHUNKS)
            pool.wait_ge(body_in, 16)
            nc.gpsimd.tensor_tensor(hb[:, 0:TILES, :], h[:, 0:TILES, :],
                                    bd("bout").unsqueeze(1).to_broadcast([P, TILES, P]), ALU.add
                                    ).then_inc(hb_done, 1)
            nc.gpsimd.tensor_tensor(beta_sel[0:E0, :, :], bd("beta_rep", E0).unsqueeze(1).to_broadcast([E0, TILES, P]),
                                    bd("sel", E0)[:, 0:TILES].unsqueeze(2).to_broadcast([E0, TILES, P]), ALU.mult
                                    ).then_inc(beta_sel_done, 1)
            for g in range(1, GROUPS):
                centre_masked(g)
                scale(g - 1)
            scale(GROUPS - 1)
            for n in (1, 2):
                ln_power(ln2_stats, ln2_ve, ln2_rstd, LN2_EPS, n)

            def w1_low(e, b):
                pool.wait_ge(w1_hi_done, e + 1)
                nc.gpsimd.tensor_tensor(w1_lo[b][:, :], w1_in[b][:, 0:HIDDEN], w1_hi[b][:, :].bitcast(F32),
                                        ALU.subtract).then_inc(w1_lo_done, 1)

            pool.wait_ge(w1_in_loaded[0], 16)
            w1_low(0, 0)
            for c in range(CHUNKS):
                sl = slice(c * BANK, (c + 1) * BANK)
                pool.wait_ge(x2T_hi_done, c + 1)
                nc.gpsimd.tensor_tensor(x2T_lo[:, sl], x2T[:, sl], x2T_hi[:, sl].bitcast(F32), ALU.subtract
                                        ).then_inc(x2T_lo_done, 1)

            def expert(it, b, split_next, first=False):
                e = 2 * it + b
                pool.wait_ge(gb2_loaded[b], 16 * (it + 1))
                for c in range(CHUNKS):
                    pool.wait_ge(y_read, 2 * e + c + 1)
                    nc.gpsimd.tensor_tensor(x2b[c], x2[:, CT * c:CT * (c + 1), :],
                                            gb2_in[b][:, 1:2, :].to_broadcast([P, CT, P]), ALU.add
                                            ).then_inc(x2b_done, 1)
                if split_next:
                    w1_low(e + 1, 1 - b)
                if first:
                    pool.wait_ge(cls_ve_done, 1)
                    pool.wait_ge(w1_lo_done, 2)
                    nc.gpsimd.tensor_tensor(cls_rs[E0:E1, :], cls_ve[E0:E1, :], minus_half[E0:E1, 0:1], ALU.pow
                                            ).then_inc(cls_rs_done, 1)
                    pool.wait_ge(cls_rs_done, 1)
                for c in range(CHUNKS):
                    n = 2 * e + c + 1
                    pool.wait_ge(y_ve, n)
                    nc.gpsimd.tensor_tensor(yrs[c][:, :], yve[c][:, :], minus_half[:, 0:CT], ALU.pow
                                            ).then_inc(y_rs, 1)
                    pool.wait_ge(y_rs, n)
                    nc.gpsimd.tensor_tensor(ya[c][:, :].unsqueeze(2), yrs[c][:, :].unsqueeze(2),
                                            gate[:, CT * c:CT * (c + 1), bass.ds(e, 1)], ALU.mult).then_inc(y_a, 1)

            pool.wait_ge(gates_done, 1)
            expert(0, 0, True, first=True)
            expert(0, 1, True)
            with pool.Fori(1, EXPERTS // 2 - 1) as it:
                for b in range(2):
                    expert(it, b, True)
            expert(EXPERTS // 2 - 1, 0, True)
            expert(EXPERTS // 2 - 1, 1, False)

        @block.scalar
        def _(act):
            act.wait_ge(noise_in, 16)
            nc.scalar.activation(f_sign[:, :], noise_sb[:, NF0:NF1], ACT.Sign).then_inc(f_parts, 1)
            act.wait_ge(f_abs_done, 1)
            nc.scalar.activation(f_root[:, :], f_abs[:, :], ACT.Sqrt).then_inc(f_parts, 1)

            act.wait_ge(zeros_set, 1)
            nc.scalar.activation(table_scrap[:, 0:1], zeros[:, 0:1], ACT.Exp)

            def gate_parts(c):
                sl = slice(c * BANK, (c + 1) * BANK)
                act.wait_ge(gate_ps, c + 1)
                nc.scalar.activation(e_sb[:, sl], ps[:, 2 * c, :], ACT.Exp, bias=b_noisy[:, 0:1]).then_inc(exp_done, 1)
                nc.scalar.activation(g_sb[:, sl], ps[:, 2 * c, :], ACT.Identity, bias=b_noisy[:, 0:1]
                                     ).then_inc(gate_read, 1)

            act.wait_ge(b_done, 1)
            gate_parts(0)
            act.wait_ge(xnT_ps, 1)
            nc.scalar.copy(xnT[:, :, PATCHES:KEYS], ps[:, 7, 0:1].unsqueeze(1).to_broadcast([P, IMAGES, 1])
                           ).then_inc(xnT_done, 1)
            act.wait_ge(cls_ps, 1)
            nc.scalar.activation(v_cls_b[:, :], ps[:, 7, 2:3], ACT.Copy, scale=bd("b_col")).then_inc(cls_done, 1)
            nc.scalar.copy(kT[:, :, PATCHES:KEYS], ps[:, 7, 1:2].unsqueeze(1).to_broadcast([P, IMAGES, 1])
                           ).then_inc(cls_done, 1)
            gate_parts(1)
            act.wait_ge(x2T_ps, 1)
            nc.scalar.copy(x2T_cls[:, :], ps[:, 7, 3:4]).then_inc(x2T_cls_done, 1)

            for c in range(CHUNKS):
                act.wait_ge(xnT_ps, c + 2)
                nc.scalar.copy(xnT[:, 8 * c:8 * (c + 1), 0:PATCHES],
                               ps[:, 6, :].rearrange("p (i r) -> p i r", r=PATCHES)).then_inc(xnT_done, 1)
                act.wait_ge(q_ps, c + 1)
                for a in range(2):
                    nc.scalar.activation(qTm[:, c * 8:(c + 1) * 8, a, :],
                                         ps[:, [2, 6][c], :].rearrange("p (i r) -> p i r", r=PATCHES), ACT.Copy,
                                         scale=bd("par_scaled")[:, a:a + 1]).then_inc(q_done, 1)

            def copy_v(g):
                act.wait_ge(v_ps, g + 1)
                nc.scalar.copy(v[:, g * GI:(g + 1) * GI, :],
                               ps[0:KEYS, V_BANK[g], :].rearrange("p (i d) -> p i d", d=P)).then_inc(v_done, 1)

            def square(g):
                act.wait_ge(T_masked, g + 1)
                nc.scalar.activation(SQ[:, g, :], S[:, g, :, :, :].rearrange("p h i k -> p (h i k)"), ACT.Square
                                     ).then_inc(squared, 1)

            def root(g):
                cols = slice(g * HP * GI, (g + 1) * HP * GI)
                act.wait_ge(var_done, g + 1)
                nc.scalar.activation(sd[:, cols], var[:, cols], ACT.Sqrt).then_inc(sd_done, 1)

            def copy_attnT(n):
                act.wait_ge(attnT_ps, n + 1)
                if n >= 8:
                    act.wait_ge(o_ps, (n - 8) // GI + 1)
                nc.scalar.copy(attnT[0:KEYS, n % 8, :], ps[0:KEYS, 4 + n % 2, :]).then_inc(attnT_done, 1)

            def copy_o(g):
                act.wait_ge(o_ps, g + 1)
                nc.scalar.copy(oT[:, :, g * GI:(g + 1) * GI, :].rearrange("p a i r -> p i a r"),
                               ps[:, 6 + g % 2, :].rearrange("p (i a r) -> p i a r", a=2, r=PATCHES)
                               ).then_inc(o_done, 1)

            nc.scalar.activation(table_scrap[:, 1:2], zeros[:, 0:1], ACT.Sqrt)
            copy_v(0)
            copy_v(1)
            square(0)
            copy_v(2)
            copy_v(3)
            root(0)
            square(1)
            act.wait_ge(w1_in_loaded[0], 16)
            nc.scalar.copy(w1_hi[0][:, :], w1_in[0][:, 0:HIDDEN]).then_inc(w1_hi_done, 1)
            root(1)
            square(2)
            for i in range(GI):
                copy_attnT(i)
            root(2)
            square(3)
            copy_attnT(GI)
            copy_o(0)
            root(3)
            for n in range(GI + 1, IMAGES):
                copy_attnT(n)
                if n % GI == 1 and n > 2 * GI:
                    copy_o(n // GI - 1)
            copy_o(GROUPS - 1)
            for c in range(CHUNKS):
                sl = slice(c * BANK, (c + 1) * BANK)
                act.wait_ge(x2T_ps, c + 2)
                nc.scalar.copy(x2T[:, sl], ps[:, 4 + c, :]).then_inc(x2T_done, 1)
                act.wait_ge(x2T_done, c + 1)
                nc.scalar.copy(x2T_hi[:, sl], x2T[:, sl]).then_inc(x2T_hi_done, 1)
            act.wait_ge(routing, 4)
            nc.scalar.activation(ex[:, :], dlt[:, :], ACT.Exp).then_inc(exp_gate, 1)

            def expert(it, b, first):
                e = 2 * it + b
                if not first or b == 1:
                    act.wait_ge(w1_in_loaded[b], 16 * (it + 1))
                    if not first:
                        act.wait_ge(hid_ps, (2 * e - 2) * FT)
                    nc.scalar.copy(w1_hi[b][:, :], w1_in[b][:, 0:HIDDEN]).then_inc(w1_hi_done, 1)
                for c in range(CHUNKS):
                    if not first or b == 1:
                        act.wait_ge(y_ps, 2 * (e - 1) + c + 1)
                    for f in range(FT):
                        act.wait_ge(hid_ps, (2 * e + c) * FT + f + 1)
                        nc.scalar.activation(hid[c][:, f, :], ps[:, f, :], ACT.Relu,
                                             bias=w1_in[b][:, HIDDEN + f:HIDDEN + f + 1]).then_inc(hid_done, 1)

            expert(0, 0, True)
            act.wait_ge(gateT_ps, 1)
            nc.scalar.copy(gateT[0:E1, :], ps[0:E1, 6, 0:P]).then_inc(gateT_done, 1)
            expert(0, 1, True)
            with act.Fori(1, EXPERTS // 2) as it:
                for b in range(2):
                    expert(it, b, False)

        @block.vector
        def _(dve):
            nc.vector.memset(zeros[:, :], 0.0).then_inc(zeros_set, 1)
            nc.vector.memset(h[:, CLS, :], 0.0).then_inc(consts_set, 1)
            nc.vector.memset(acc[:, CLS, :], 0.0).then_inc(consts_set, 1)
            dve.wait_ge(noise_in, 16)
            raw = noise_sb[:, NF0:NF1]
            nc.vector.scalar_tensor_tensor(out=f_abs[:, :], in0=raw, scalar=-1.0, in1=raw, op0=ALU.mult, op1=ALU.max
                                           ).then_inc(f_abs_done, 1)
            dve.wait_ge(f_parts, 2)
            nc.vector.tensor_tensor(f_noise[:, :], f_root[:, :], f_sign[:, :], ALU.mult).then_inc(f_done, 1)
            dve.wait_ge(f_done, 1)
            for k in range(2):
                nc.vector.tensor_tensor(
                    sw_eo[:, 2 * k:2 * k + 2, :], nz("sw").rearrange("p (k n) -> p k n", n=P)[:, 2 * k:2 * k + 2, :],
                    fz("eo_row")[:, k * P:(k + 1) * P].unsqueeze(1).to_broadcast([P, 2, P]), ALU.mult
                ).then_inc(f_done, 1)
            dve.wait_ge(f_done, 3)
            for k in range(4):
                nc.vector.scalar_tensor_tensor(out=w_noisy[:, k, :], in0=sw_eo[:, k, :], scalar=fz("ei")[:, k:k + 1],
                                               in1=nz("w")[:, k * P:(k + 1) * P], op0=ALU.mult, op1=ALU.add
                                               ).then_inc(w_done, 1)
            nc.vector.tensor_tensor(b_noisy[:, :], nz("sb"), fz("eo_col"), ALU.mult).then_inc(f_done, 1)
            dve.wait_ge(f_done, 4)
            nc.vector.tensor_tensor(b_noisy[:, :], b_noisy[:, :], nz("b"), ALU.add).then_inc(b_done, 1)
            dve.wait_ge(body_in, 16)
            nc.vector.tensor_tensor(posb[:, :], bd("pos"), bd("b3"), ALU.add).then_inc(consts_set, 1)
            nc.vector.tensor_tensor(bmask[:, :, :], bd("b_tab").unsqueeze(2).to_broadcast([P, HP, KEYS]),
                                    bd("mask").unsqueeze(1).to_broadcast([P, HP, KEYS]), ALU.mult
                                    ).then_inc(consts_set, 1)
            for a in range(2):
                nc.vector.tensor_scalar(wout_par[:, a, :], bd("wout"), bd("par")[:, a:a + 1], None, ALU.mult
                                        ).then_inc(consts_set, 1)
            dve.wait_ge(consts_set, 2)
            nc.vector.tensor_copy(h[0:1, CLS, :], bd("cls", 1)).then_inc(consts_set, 1)
            nc.vector.tensor_tensor(hb[0:1, CLS, :], bd("cls", 1), bd("bout", 1), ALU.add).then_inc(consts_set, 1)
            dve.wait_ge(consts_set, 8)

            def stats(src, sem_done, n):
                a, b = LN_TILES[n]
                for t in range(a, b):
                    nc.vector.bn_stats(st[:, t, :], src[:, t, :]).then_inc(sem_done[0], 1)
                dve.wait_ge(sem_done[0], [1, CT + 1, 2 * CT + 1][n])
                for t in range(a, b):
                    last = nc.vector.bn_aggr(mv[:, t, :], st[:, t, :])
                last.then_inc(sem_done[1], 1)

            def normalise(dst, src, rstd_sem, out_sem, n):
                dve.wait_ge(rstd_sem, n + 1)
                for t in range(*LN_TILES[n]):
                    nc.vector.tensor_scalar(dst[:, t, :], src[:, t, :], mv[:, t, 0:1], rstd[:, t:t + 1],
                                            ALU.subtract, ALU.mult).then_inc(out_sem, 1)

            stats(h, (bn1_done, ln_stats), 0)
            normalise(xn, h, ln_rstd, xn_done, 0)

            Q = BANK // 4

            def recip_of(c):
                m, r = m_sb[:, c * BANK:(c + 1) * BANK], r_sb[:, c * BANK:(c + 1) * BANK]
                pair = pairs[:, :]

                def step(out, a, b_, n):
                    nc.vector.tensor_tensor(out, a, b_, ALU.mult).then_inc(recip_steps, 1)
                    dve.wait_ge(recip_steps, 7 * c + n)

                step(pair[:, 0:2 * Q], m[:, 0:2 * Q], m[:, 2 * Q:4 * Q], 1)
                step(pair[:, 2 * Q:3 * Q], pair[:, 0:Q], pair[:, Q:2 * Q], 2)
                nc.vector.reciprocal(pair[:, 3 * Q:4 * Q], pair[:, 2 * Q:3 * Q]).then_inc(recip_steps, 1)
                dve.wait_ge(recip_steps, 7 * c + 3)
                nc.vector.tensor_tensor(inv_pair[:, 0:Q], pair[:, 3 * Q:4 * Q], pair[:, Q:2 * Q], ALU.mult
                                        ).then_inc(recip_steps, 1)
                nc.vector.tensor_tensor(inv_pair[:, Q:2 * Q], pair[:, 3 * Q:4 * Q], pair[:, 0:Q], ALU.mult
                                        ).then_inc(recip_steps, 1)
                dve.wait_ge(recip_steps, 7 * c + 5)
                nc.vector.tensor_tensor(r[:, 0:2 * Q], inv_pair[:, :], m[:, 2 * Q:4 * Q], ALU.mult
                                        ).then_inc(recip_steps, 1)
                nc.vector.tensor_tensor(r[:, 2 * Q:4 * Q], inv_pair[:, :], m[:, 0:2 * Q], ALU.mult
                                        ).then_inc(recip_steps, 1)
                dve.wait_ge(recip_steps, 7 * c + 7)

            def mish_start(c):
                sl = slice(c * BANK, (c + 1) * BANK)
                dve.wait_ge(exp_done, c + 1)
                nc.vector.tensor_scalar(e_sb[:, sl], e_sb[:, sl], EXP_CAP, None, ALU.min).then_inc(mish_dve, 1)
                dve.wait_ge(mish_dve, 3 * c + 1)
                nc.vector.scalar_tensor_tensor(out=n_sb[:, sl], in0=e_sb[:, sl], scalar=2.0, in1=e_sb[:, sl],
                                               op0=ALU.add, op1=ALU.mult).then_inc(mish_dve, 1)
                dve.wait_ge(mish_dve, 3 * c + 2)
                nc.vector.tensor_scalar(m_sb[:, sl], n_sb[:, sl], 2.0, None, ALU.add).then_inc(mish_dve, 1)
                dve.wait_ge(mish_dve, 3 * c + 3)

            def mish_end(c):
                sl = slice(c * BANK, (c + 1) * BANK)
                dve.wait_ge(gn_done, c + 1)
                nc.vector.tensor_tensor(gn_sb[:, sl], gn_sb[:, sl], r_sb[:, sl], ALU.mult).then_inc(gT_done, 1)
                dve.wait_ge(gT_done, 2 * c + 1)
                dve.wait_ge(inner_ps, c + 1)
                nc.vector.scalar_tensor_tensor(out=gT[:, sl], in0=ps[:, 2 * c + 1, :], scalar=b_noisy[:, 1:2],
                                               in1=gn_sb[:, sl], op0=ALU.add, op1=ALU.mult).then_inc(gT_done, 1)

            def embed(c):
                dve.wait_ge(h_ps, c + 1)
                nc.vector.tensor_tensor(h[:, CT * c:CT * (c + 1), :],
                                        ps[:, 4 + c, :].rearrange("p (t d) -> p t d", d=P),
                                        posb[:, :].unsqueeze(1).to_broadcast([P, CT, P]), ALU.add).then_inc(h_done, 1)
                dve.wait_ge(h_done, c + 1)
                stats(h, (bn1_done, ln_stats), c + 1)

            def copy_k(c):
                dve.wait_ge(k_ps, c + 1)
                nc.vector.tensor_copy(kT[:, 8 * c:8 * (c + 1), 0:PATCHES],
                                      ps[:, 4 + c, :].rearrange("p (i r) -> p i r", r=PATCHES)).then_inc(k_done, 1)

            GS = HP * GI

            def rows(g):
                return S[:, g, :, :, :].rearrange("p h i k -> p (h i) k")

            def centre(g):
                dve.wait_ge(scores_ps, g + 1)
                src = ps[:, 0:HP, 0:GI * KEYS].rearrange("p h (i k) -> p h i k", k=KEYS)
                nc.vector.tensor_tensor(
                    S[:, g, :, :, :], src,
                    bd("mask").unsqueeze(1).unsqueeze(1).to_broadcast([P, HP, GI, KEYS]), ALU.mult
                ).then_inc(S_masked, 1)
                dve.wait_ge(S_masked, g + 1)
                cols = slice(g * GS, (g + 1) * GS)
                nc.vector.tensor_reduce(ssum[:, cols], rows(g), AX.X, ALU.add).then_inc(S_sum, 1)
                dve.wait_ge(S_sum, g + 1)
                nc.vector.tensor_scalar(mu[:, cols], ssum[:, cols], bd("inv_n"), None, ALU.mult).then_inc(mu_done, 1)
                dve.wait_ge(mu_done, g + 1)
                nc.vector.tensor_tensor(rows(g), rows(g), mu[:, cols].unsqueeze(2).to_broadcast([P, GS, KEYS]),
                                        ALU.subtract).then_inc(S_centred, 1)

            def variance(g):
                cols = slice(g * GS, (g + 1) * GS)
                dve.wait_ge(squared, g + 1)
                nc.vector.tensor_reduce(qsum[:, cols], SQ[:, g, :].rearrange("p (n k) -> p n k", k=KEYS),
                                        AX.X, ALU.add).then_inc(sq_sum, 1)
                dve.wait_ge(sq_sum, g + 1)
                nc.vector.tensor_scalar(var[:, cols], qsum[:, cols], bd("inv_n"), ATT_EPS, ALU.mult, ALU.add
                                        ).then_inc(var_done, 1)

            def gain(g):
                cols = slice(g * GS, (g + 1) * GS)
                dve.wait_ge(sd_done, g + 1)
                nc.vector.reciprocal(rs[:, cols], sd[:, cols]).then_inc(rs_done, 1)
                dve.wait_ge(rs_done, g + 1)
                nc.vector.tensor_tensor(
                    rg[:, cols].rearrange("p (h i) -> p h i", h=HP), rs[:, cols].rearrange("p (h i) -> p h i", h=HP),
                    bd("g_tab").unsqueeze(2).to_broadcast([P, HP, GI]), ALU.mult).then_inc(rg_done, 1)

            def add_bias(g):
                dve.wait_ge(S_scaled, g + 1)
                nc.vector.tensor_tensor(S[:, g, :, :, :], S[:, g, :, :, :],
                                        bmask[:, :, :].unsqueeze(2).to_broadcast([P, HP, GI, KEYS]), ALU.add
                                        ).then_inc(attn_done, 1)

            mish_start(0)
            recip_of(0)
            mish_end(0)
            dve.wait_ge(proj_ps, 1)
            nc.vector.tensor_tensor(acc[0:1, CLS, :], ps[0:1, 7, P:2 * P], hb[0:1, CLS, :], ALU.add).then_inc(acc_done, 1)
            dve.wait_ge(acc_done, 1)
            stats(acc, (bn2_done, ln2_stats), 0)
            mish_start(1)
            normalise(x2, acc, ln2_rstd, x2_done, 0)
            embed(0)
            recip_of(1)
            normalise(xn, h, ln_rstd, xn_done, 1)
            mish_end(1)
            copy_k(0)
            embed(1)
            centre(0)
            normalise(xn, h, ln_rstd, xn_done, 2)
            copy_k(1)
            centre(1)
            variance(0)
            dve.wait_ge(cls_hid_ps, 1)
            nc.vector.tensor_tensor(cls_hid[:, :, :], ps[:, 7, 256:256 + EXPERTS * FT].rearrange("p (e f) -> p e f", f=FT),
                                    w1_all[:, :, HIDDEN:HIDDEN + FT], ALU.add).then_inc(cls_hid_done, 1)
            dve.wait_ge(cls_hid_done, 1)
            nc.vector.tensor_scalar(cls_hid[:, :, :], cls_hid[:, :, :], 0.0, None, ALU.max).then_inc(cls_hid_done, 1)
            gain(0)
            for g in range(2, GROUPS + 2):
                if g < GROUPS:
                    centre(g)
                if g <= GROUPS:
                    variance(g - 1)
                add_bias(g - 2)
                if g <= GROUPS:
                    gain(g - 1)

            def cls_rows_T():
                dve.wait_ge(cls_yT_ps, 1)
                nc.vector.scalar_tensor_tensor(out=cls_yT[:, :], in0=ps[:, 7, 300:300 + EXPERTS], scalar=x2T_cls[:, 0:1],
                                               in1=bd("b2T"), op0=ALU.add, op1=ALU.add).then_inc(cls_yT_done, 1)

            def cls_norm():
                dve.wait_ge(cls_y_ps, 1)
                nc.vector.tensor_copy(cls_rows[E0:E1, :], ps[E0:E1, 7, 0:P]).then_inc(cls_row_done, 1)
                dve.wait_ge(cls_row_done, 1)
                nc.vector.bn_stats(cls_st[E0:E1, :], cls_rows[E0:E1, :]).then_inc(cls_row_done, 1)
                dve.wait_ge(cls_row_done, 2)
                nc.vector.bn_aggr(cls_mv[E0:E1, :], cls_st[E0:E1, :]).then_inc(cls_row_done, 1)
                dve.wait_ge(cls_row_done, 3)
                nc.vector.tensor_scalar(cls_ve[E0:E1, :], cls_mv[E0:E1, 1:2], MOE_EPS, None, ALU.add
                                        ).then_inc(cls_ve_done, 1)

            def cls_affine():
                dve.wait_ge(cls_rs_done, 1)
                nc.vector.tensor_scalar(cls_rows[E0:E1, :], cls_rows[E0:E1, :], cls_mv[E0:E1, 0:1], cls_rs[E0:E1, 0:1],
                                        ALU.subtract, ALU.mult).then_inc(cls_row_done, 1)
                dve.wait_ge(cls_row_done, 4)
                nc.vector.tensor_tensor(cls_rows[E0:E1, :], cls_rows[E0:E1, :], body_rows("gamma_rows"), ALU.mult
                                        ).then_inc(cls_row_done, 1)
                dve.wait_ge(cls_row_done, 5)
                nc.vector.tensor_tensor(cls_rows[E0:E1, :], cls_rows[E0:E1, :], body_rows("beta_rep"), ALU.add
                                        ).then_inc(cls_row_done, 1)

            def body_rows(name):
                return bd(name)[E0:E1, :]

            dve.wait_ge(hb_done, 1)
            dve.wait_ge(xn_done, TILES + 1)
            for c in range(CHUNKS):
                dve.wait_ge(proj_ps, c + 2)
                nc.vector.tensor_tensor(acc[:, CT * c:CT * (c + 1), :],
                                        ps[:, c, :].rearrange("p (t d) -> p t d", d=P),
                                        hb[:, CT * c:CT * (c + 1), :], ALU.add).then_inc(acc_done, 1)
                dve.wait_ge(acc_done, c + 2)
                stats(acc, (bn2_done, ln2_stats), c + 1)
            for n in (1, 2):
                normalise(x2, acc, ln2_rstd, x2_done, n)

            cls_rows_T()
            dve.wait_ge(logits_ps, 1)
            nc.vector.tensor_copy(lg[:, 0:TILES, :], ps[:, 6, 0:TILES * EXPERTS].rearrange("p (t e) -> p t e", e=EXPERTS)
                                  ).then_inc(routing, 1)
            nc.vector.tensor_copy(lg[:, CLS, :], bd("iota")).then_inc(routing, 1)
            dve.wait_ge(routing, 2)
            nc.vector.tensor_copy(lg[0:1, CLS, :], ps[0:1, 6, TILES * EXPERTS:(TILES + 1) * EXPERTS]
                                  ).then_inc(routing, 1)
            dve.wait_ge(routing, 3)
            for t in range(TILES + 1):
                nc.vector.max(top[:, t, :], lg[:, t, :]).then_inc(topped, 1)
            dve.wait_ge(topped, TILES + 1)
            nc.vector.tensor_tensor(dlt[:, :], top[:, :, 1], top[:, :, 0], ALU.subtract).then_inc(routing, 1)
            for t in range(TILES + 1):
                nc.vector.max_index(top_at[:, t, :], top[:, t, :], lg[:, t, :]).then_inc(topped, 1)
            dve.wait_ge(topped, 2 * (TILES + 1))
            nc.vector.tensor_copy(top_atf[:, :, :], top_at[:, :, 0:2]).then_inc(topped, 1)
            dve.wait_ge(exp_gate, 1)
            nc.vector.tensor_scalar(den[:, :], ex[:, :], 1.0, None, ALU.add).then_inc(topped, 1)
            dve.wait_ge(topped, 2 * (TILES + 1) + 2)
            nc.vector.reciprocal(g1[:, :], den[:, :]).then_inc(topped, 1)
            dve.wait_ge(topped, 2 * (TILES + 1) + 3)
            nc.vector.tensor_tensor(g2[:, :], ex[:, :], g1[:, :], ALU.mult).then_inc(topped, 1)
            iota = bd("iota").unsqueeze(1).to_broadcast([P, TILES + 1, EXPERTS])
            for k in range(2):
                nc.vector.tensor_tensor(sel[:, k, :, :], iota,
                                        top_atf[:, :, k:k + 1].to_broadcast([P, TILES + 1, EXPERTS]), ALU.is_equal
                                        ).then_inc(topped, 1)
            dve.wait_ge(topped, 2 * (TILES + 1) + 6)
            for k, gk in ((0, g1), (1, g2)):
                nc.vector.tensor_tensor(sel[:, k, :, :], sel[:, k, :, :],
                                        gk[:, :].unsqueeze(2).to_broadcast([P, TILES + 1, EXPERTS]), ALU.mult
                                        ).then_inc(topped, 1)
            dve.wait_ge(topped, 2 * (TILES + 1) + 8)
            nc.vector.tensor_tensor(gate[:, :, :], sel[:, 0, :, :], sel[:, 1, :, :], ALU.add).then_inc(gates_done, 1)

            dve.wait_ge(gates_done, 1)
            nc.vector.memset(u[0][:, 0, 0:1], 0.0).then_inc(y_read, 2)

            def expert(it, b):
                e = 2 * it + b
                dve.wait_ge(gb2_loaded[b], 16 * (it + 1))
                for c in range(CHUNKS):
                    n = 2 * e + c + 1
                    dve.wait_ge(y_ps, n)
                    dve.wait_ge(x2b_done, n)
                    nc.vector.tensor_tensor(y[c], ps[:, 4 + c, :].rearrange("p (t d) -> p t d", d=P), x2b[c], ALU.add
                                            ).then_inc(y_read, 1)
                    dve.wait_ge(y_read, n + 2)
                    for t in range(CT):
                        last = nc.vector.bn_stats(yst[c][:, t, :], y[c][:, t, :])
                    last.then_inc(y_stats, 1)
                    dve.wait_ge(y_stats, n)
                    nc.vector.tensor_tensor(ymv[c][:, :, :], yst[c][:, :, 1:3], yst[c][:, :, 4:6], ALU.add
                                            ).then_inc(y_parts, 1)
                    nc.vector.tensor_tensor(yd[c][:, :], yst[c][:, :, 1], yst[c][:, :, 4], ALU.subtract
                                            ).then_inc(y_parts, 1)
                    dve.wait_ge(y_parts, 4 * n - 2)
                    nc.vector.tensor_scalar(ymean[c][:, :], ymv[c][:, :, 0], 0.5, None, ALU.mult
                                            ).then_inc(y_parts, 1)
                    nc.vector.scalar_tensor_tensor(out=yd[c][:, :], in0=yd[c][:, :], scalar=P / 4.0,
                                                   in1=yd[c][:, :], op0=ALU.mult, op1=ALU.mult
                                                   ).then_inc(y_parts, 1)
                    dve.wait_ge(y_parts, 4 * n)
                    nc.vector.tensor_tensor(yd[c][:, :], yd[c][:, :], ymv[c][:, :, 1], ALU.add
                                            ).then_inc(y_var, 1)
                    dve.wait_ge(y_var, n)
                    nc.vector.tensor_scalar(yve[c][:, :], yd[c][:, :], 1.0 / P, MOE_EPS, ALU.mult, ALU.add
                                            ).then_inc(y_ve, 1)
                    for t in range(CT):
                        last = nc.vector.scalar_tensor_tensor(
                            out=u[c][:, t, :], in0=y[c][:, t, :], scalar=ymean[c][:, t:t + 1],
                            in1=gb2_in[b][:, 0, :], op0=ALU.subtract, op1=ALU.mult)
                    last.then_inc(u_done, 1)
                    dve.wait_ge(u_done, n)
                    dve.wait_ge(y_a, n)
                    for t in range(CT):
                        at = acc[:, CT * c + t, :]
                        last = nc.vector.scalar_tensor_tensor(out=at, in0=u[c][:, t, :], scalar=ya[c][:, t:t + 1],
                                                              in1=at, op0=ALU.mult, op1=ALU.add)
                    last.then_inc(moe_acc, 1)

            cls_norm()
            expert(0, 0)
            cls_affine()
            dve.wait_ge(moe_acc, 2)
            for c in range(CHUNKS):
                dve.wait_ge(beta_ps, c + 1)
                nc.vector.tensor_tensor(acc[:, CT * c:CT * (c + 1), :], acc[:, CT * c:CT * (c + 1), :],
                                        ps[:, [7, 6][c], :].rearrange("p (t d) -> p t d", d=P), ALU.add
                                        ).then_inc(final_done, 1)
            dve.wait_ge(final_done, CHUNKS)
            expert(0, 1)
            dve.wait_ge(beta_ps, CHUNKS + 1)
            nc.vector.tensor_tensor(acc[0:1, CLS, :], acc[0:1, CLS, :], ps[0:1, 7, 0:P], ALU.add
                                    ).then_inc(final_done, 1)
            with dve.Fori(1, EXPERTS // 2) as it:
                for b in range(2):
                    expert(it, b)

        @block.tensor
        def _(pe):
            mm = nc.tensor.matmul

            def project(c, k, done):
                for half in range(HALVES):
                    last = mm(ps[:, 2 * c + k, :], w_noisy[:, 2 * k + half, :], xT[:, c, half, :],
                              start=(half == 0), stop=(half == HALVES - 1))
                last.then_inc(done, 1)

            pe.wait_ge(zeros_set, 1)
            for n in range(WARM):
                mm(ps[:, 6, 0:P], zeros[:, :], zeros[:, :], start=True, stop=True)
            pe.wait_ge(w_done, 2)
            pe.wait_ge(patches_in[0], 16)
            project(0, 0, gate_ps)
            pe.wait_ge(w_done, 4)
            project(0, 1, inner_ps)
            pe.wait_ge(body_in, 16)
            pe.wait_ge(xn_done, 1)
            nc.tensor.transpose(ps[:, 7, 0:1], xn[0:1, CLS, :], ident[0:1, 0:1]).then_inc(xnT_ps, 1)
            pe.wait_ge(patches_in[1], 16)
            project(1, 0, gate_ps)
            pe.wait_ge(xnT_done, 1)
            mm(ps[:, 7, 1:2], bd("wk"), xnT_cls, start=True, stop=True)
            mm(ps[:, 7, 2:3], bd("wv"), xnT_cls, start=True, stop=True).then_inc(cls_ps, 1)
            project(1, 1, inner_ps)
            pe.wait_ge(cls_done, 2)
            mm(ps[0:1, 7, P:2 * P], v_cls_b[:, 0:1], bd("wout"), start=True, stop=True).then_inc(proj_ps, 1)

            def embed(c):
                pe.wait_ge(gT_done, 2 * (c + 1))
                for t in range(CT * c, CT * (c + 1)):
                    last = mm(ps[:, 4 + c, (t % CT) * P:(t % CT + 1) * P], gT[:, t * P:(t + 1) * P], bd("w3T"),
                              start=True, stop=True)
                last.then_inc(h_ps, 1)

            def cls_units(e0, e1):
                if e0 == 0:
                    pe.wait_ge(x2_done, 1)
                    nc.tensor.transpose(ps[:, 7, 3:4], x2[0:1, CLS, :], ident[0:1, 0:1]).then_inc(x2T_ps, 1)
                    pe.wait_ge(x2T_cls_done, 1)
                    pe.wait_ge(w1_loaded, 16)
                for e in range(e0, e1):
                    for f in range(FT):
                        n = 256 + e * FT + f
                        last = mm(ps[:, 7, n:n + 1], w1_all[:, e, f * P:(f + 1) * P], x2T_cls[:, :],
                                  start=True, stop=True)
                if e1 == EXPERTS:
                    last.then_inc(cls_hid_ps, 1)

            def cls_outputs(e0, e1):
                pe.wait_ge(cls_hid_done, 2)
                pe.wait_ge(w2_loaded, 16)
                for e in range(e0, e1):
                    for f in range(FT):
                        last = mm(ps[:, 7, 300 + e:301 + e], w2_all[:, e, f, :], cls_hid[:, e, f:f + 1],
                                  start=(f == 0), stop=(f == FT - 1))
                if e1 == EXPERTS:
                    last.then_inc(cls_yT_ps, 1)

            def turn_norm(c):
                for t in range(CT * c, CT * (c + 1)):
                    pe.wait_ge(xn_done, t + 2)
                    last = nc.tensor.transpose(ps[:, 6, (t % CT) * P:(t % CT + 1) * P], xn[:, t, :], ident)
                last.then_inc(xnT_ps, 1)

            def q_and_k(c):
                pe.wait_ge(xnT_done, c + 2)
                pe.wait_ge(gate_read, 2)
                pe.wait_ge(h_done, c + 1)
                cols = xnT[:, 8 * c:8 * (c + 1), 0:PATCHES]
                mm(ps[:, [2, 6][c], :], bd("wq"), cols, start=True, stop=True).then_inc(q_ps, 1)
                mm(ps[:, 4 + c, :], bd("wk"), cols, start=True, stop=True).then_inc(k_ps, 1)

            def scores(g):
                pe.wait_ge(q_done, 2 * (g // 2 + 1))
                pe.wait_ge(k_done, g // 2 + 1)
                if g > 0:
                    pe.wait_ge(S_masked, g)
                for i in range(GI):
                    n = GI * g + i
                    for h_ in range(HP):
                        rows = slice(32 * h_, 32 * (h_ + 1))
                        last = mm(ps[:, h_, i * KEYS:(i + 1) * KEYS], qTm[rows, n, :, :], kT[rows, n, :],
                                  start=True, stop=True)
                last.then_inc(scores_ps, 1)

            def values(g):
                pe.wait_ge(*[(k_done, 1), (k_done, 2), (q_done, 4), (v_done, 1)][g])
                for i in range(GI):
                    last = mm(ps[0:KEYS, V_BANK[g], i * P:(i + 1) * P], xnT[:, GI * g + i, :], bd("wv"),
                              start=True, stop=True)
                last.then_inc(v_ps, 1)

            def turn(n):
                g, i = n // GI, n % GI
                if i == 0:
                    pe.wait_ge(attn_done, g + 1)
                if n >= 2:
                    pe.wait_ge(attnT_done, n - 1)
                for h_ in range(HP):
                    last = nc.tensor.transpose(ps[0:KEYS, 4 + n % 2, h_ * P:(h_ + 1) * P], S[:, g, h_, i, :], ident)
                last.then_inc(attnT_ps, 1)

            def weigh(n):
                g, i = n // GI, n % GI
                pe.wait_ge(attnT_done, n + 1)
                if i == 0 and g >= 2:
                    pe.wait_ge(o_done, g - 1)
                for h_ in range(HP):
                    last = mm(ps[32 * h_:32 * (h_ + 1), 6 + g % 2, i * P:(i + 1) * P],
                              v[:, n, 32 * h_:32 * (h_ + 1)], attnT[0:KEYS, n % 8, h_ * P:(h_ + 1) * P],
                              start=True, stop=True)
                if i == GI - 1:
                    last.then_inc(o_ps, 1)

            def weigh_group(g):
                for n in range(GI * g, GI * (g + 1)):
                    turn(n)
                    if n >= 1:
                        weigh(n - 1)

            embed(0)
            cls_units(0, 3)
            turn_norm(0)
            q_and_k(0)
            cls_units(3, 5)
            embed(1)
            scores(0)
            cls_units(5, 7)
            turn_norm(1)
            q_and_k(1)
            values(0)
            values(1)
            scores(1)
            values(2)
            values(3)
            cls_units(7, 8)
            scores(2)
            pe.wait_ge(v_done, GROUPS)
            pe.wait_ge(cls_hid_done, 1)
            weigh_group(0)
            scores(3)
            for g in range(1, GROUPS):
                weigh_group(g)
            weigh(IMAGES - 1)
            pe.wait_ge(S_masked, GROUPS)
            for c in range(CHUNKS):
                pe.wait_ge(o_done, 2 * (c + 1))
                for t in range(CT * c, CT * (c + 1)):
                    for a in range(2):
                        last = mm(ps[:, c, (t % CT) * P:(t % CT + 1) * P], oT[:, a, 2 * t:2 * t + 2, :].rearrange("p i r -> p (i r)"),
                                  wout_par[:, a, :], start=(a == 0), stop=(a == 1))
                last.then_inc(proj_ps, 1)
            cls_outputs(0, 5)
            for c in range(CHUNKS):
                for t in range(CT * c, CT * (c + 1)):
                    pe.wait_ge(x2_done, t + 2)
                    last = nc.tensor.transpose(ps[:, 4 + c, (t % CT) * P:(t % CT + 1) * P], x2[:, t, :], ident)
                last.then_inc(x2T_ps, 1)
            cls_outputs(5, EXPERTS)
            for t in range(TILES):
                pe.wait_ge(x2T_done, t // CT + 1)
                mm(ps[:, 6, t * EXPERTS:(t + 1) * EXPERTS], x2T[:, t * P:(t + 1) * P], bd("router"),
                   start=True, stop=True)
            mm(ps[0:1, 6, TILES * EXPERTS:(TILES + 1) * EXPERTS], x2T_cls[:, :], bd("router"),
               start=True, stop=True).then_inc(logits_ps, 1)

            def expert(it, b, between=None):
                e = 2 * it + b
                pe.wait_ge(w1_lo_done, e + 1)
                for c in range(CHUNKS):
                    cols = slice(c * BANK, (c + 1) * BANK)
                    pe.wait_ge(x2T_lo_done, c + 1)
                    for f in range(FT):
                        w = slice(f * P, (f + 1) * P)
                        if c > 0:
                            pe.wait_ge(hid_done, (2 * e + c - 1) * FT + f + 1)
                        mm(ps[:, f, :], w1_hi[b][:, w], x2T_lo[:, cols], start=True, stop=False)
                        mm(ps[:, f, :], w1_lo[b][:, w], x2T_hi[:, cols], start=False, stop=False)
                        mm(ps[:, f, :], w1_hi[b][:, w], x2T_hi[:, cols], start=False, stop=True).then_inc(hid_ps, 1)
                if between:
                    between()
                for c in range(CHUNKS):
                    pe.wait_ge(hid_done, (2 * e + c + 1) * FT)
                    pe.wait_ge(y_read, 2 * e + c + 1)
                    for t in range(CT):
                        for f in range(FT):
                            last = mm(ps[:, 4 + c, t * P:(t + 1) * P], hid[c][:, f, t * P:(t + 1) * P],
                                      w2_all[:, bass.ds(e, 1), f, :].rearrange("p a n -> p (a n)"),
                                      start=(f == 0), stop=(f == FT - 1))
                    last.then_inc(y_ps, 1)

            def turn_gates():
                pe.wait_ge(cls_yT_done, 1)
                mm(ps[E0:E1, 7, 0:P], cls_yT[:, :], ident, start=True, stop=True).then_inc(cls_y_ps, 1)
                pe.wait_ge(gates_done, 1)
                nc.tensor.transpose(ps[0:E1, 6, 0:P], gate[:, :, :].rearrange("p t e -> p (t e)"), ident
                                    ).then_inc(gateT_ps, 1)

            expert(0, 0, turn_gates)
            pe.wait_ge(gateT_done, 1)
            pe.wait_ge(beta_sel_done, 1)
            pe.wait_ge(cls_row_done, 1)
            for c in range(CHUNKS):
                mm(ps[:, [7, 6][c], :], gateT[0:E0, :], beta_sel[0:E0, CT * c:CT * (c + 1), :].rearrange("p t d -> p (t d)"),
                   start=True, stop=True).then_inc(beta_ps, 1)
            expert(0, 1)
            pe.wait_ge(final_done, 1)
            pe.wait_ge(cls_row_done, 6)
            mm(ps[0:1, 7, 0:P], gateT[E0:E1, 0:1], cls_rows[E0:E1, :], start=True, stop=True).then_inc(beta_ps, 1)
            with pe.Fori(1, EXPERTS // 2) as it:
                for b in range(2):
                    expert(it, b)


def constants():
    pos = np.arange(PATCHES, dtype=np.float32)[:, None]
    div = np.exp(np.arange(0, P, 2, dtype=np.float32) * np.float32(-np.log(10000.0) / P))
    ang = pos * div
    pe = np.stack([np.sin(ang), np.cos(ang)], axis=-1).reshape(PATCHES, P).astype(np.float32)
    row = np.arange(P) % PATCHES
    mask = np.concatenate([np.arange(PATCHES)[None, :] <= row[:, None], np.ones((P, 1), bool)], 1)
    par = (np.arange(P)[:, None] // HD % 2) == np.arange(2)[None, :]
    sel = (np.arange(P)[:, None] // EXPERTS) == np.arange(TILES + 1)[None, :]
    f = np.float32
    return {"sel": sel.astype(f), "pos": np.tile(pe, (2, 1)), "ident": np.eye(P, dtype=f), "mask": mask.astype(f),
            "inv_n": (1.0 / (row + 2.0))[:, None].astype(f), "par_scaled": (par * float(P) ** -0.5).astype(f),
            "par": par.astype(f), "iota": np.tile(np.arange(EXPERTS, dtype=f), (P, 1))}


def pack(spec, parts):
    cols = []
    for name, width in spec:
        a = parts[name]
        assert a.shape[1] == width and a.dtype == np.float32, name
        cols.append(np.concatenate([a, np.zeros((P - a.shape[0], width), np.float32)], 0))
    return np.ascontiguousarray(np.concatenate(cols, 1))


def kernel(**inputs):
    import concourse.bacc as bacc
    from concourse.bass_utils import run_bass_kernel_spmd

    a = {k: np.asarray(v) for k, v in inputs.items()}

    def rows(vec):
        return np.broadcast_to(vec.reshape(1, -1), (P, vec.size))

    def by_feature(m):
        return m.T.reshape(HALVES, P, P).transpose(1, 0, 2).reshape(P, HALVES * P)

    t = {k[7:]: v for k, v in a.items() if k.startswith("L0_tok_")}
    noise = pack(NOISE_COLS, {
        "w": np.concatenate([by_feature(t["W1_w"]), by_feature(t["W2_w"])], 1),
        "sw": np.concatenate([by_feature(t["W1_sw"]), by_feature(t["W2_sw"])], 1),
        "ei": np.concatenate([t["eps_in1"].reshape(HALVES, P).T, t["eps_in2"].reshape(HALVES, P).T], 1),
        "eo_row": np.concatenate([rows(t["eps_out1"]), rows(t["eps_out2"])], 1),
        "eo_col": np.stack([t["eps_out1"], t["eps_out2"]], 1),
        "b": np.stack([t["W1_b"], t["W2_b"]], 1),
        "sb": np.stack([t["W1_sb"], t["W2_sb"]], 1)})
    norm_g, norm_b = a["L0_attn_norm_g"].reshape(HEADS), a["L0_attn_norm_b"].reshape(HEADS)

    def head_table(vec):
        return np.repeat(vec.reshape(HP, 2).T, PATCHES, axis=0)

    body = pack(BODY_COLS, dict(
        constants(), w3T=t["W3_w"].T, b3=rows(t["W3_b"]), cls=a["cls_tok"].reshape(1, P),
        wq=a["L0_attn_w_qkv"][:, 0:P], wk=a["L0_attn_w_qkv"][:, P:2 * P], wv=a["L0_attn_w_qkv"][:, 2 * P:3 * P],
        wout=a["L0_attn_w_out"], bout=rows(a["L0_attn_b_out"]), 
        beta_rep=np.tile(a["L0_ffn_beta"], (TILES + 1, 1)), gamma_rows=np.tile(a["L0_ffn_gamma"], (TILES + 1, 1)),
        b2T=a["L0_ffn_b2"].T,
        router=a["L0_ffn_router_w"], g_tab=head_table(norm_g), b_tab=head_table(norm_b),
        b_col=np.repeat(norm_b, HD)[:, None]))
    px = a["x"].reshape(IMAGES, GRID, HALVES, PATCH // HALVES, GRID, PATCH)
    px = px.transpose(3, 5, 2, 0, 1, 4).reshape(P, HALVES, CHUNKS, BANK).transpose(0, 2, 1, 3)
    w1b1 = np.concatenate([a["L0_ffn_w1"], a["L0_ffn_b1"].reshape(EXPERTS, FT, P).transpose(0, 2, 1)], 2)
    w1b1 = w1b1.transpose(1, 0, 2)
    arrays = {
        "patches": px, "noise": noise, "body": body, "w1b1": w1b1,
        "w2": a["L0_ffn_w2"].reshape(EXPERTS, FT, P, P).transpose(2, 0, 1, 3),
        "gb2": np.stack([a["L0_ffn_gamma"], a["L0_ffn_b2"]], 1)}
    arrays = {k: np.ascontiguousarray(v) for k, v in arrays.items()}

    nc = bacc.Bacc("TRN2", target_bir_lowering=False, num_devices=1)
    args = [nc.dram_tensor(k, v.shape, mybir.dt.from_np(v.dtype), kind="ExternalInput").ap()
            for k, v in arrays.items()]
    out = nc.dram_tensor("out", (IMAGES, KEYS, P), F32, kind="ExternalOutput").ap()
    vit_tower(nc, *args, out)
    r = run_bass_kernel_spmd(nc, [arrays], core_ids=[0])
    return r.results[0]["out"]
```

```python
from contextlib import ExitStack

import numpy as np
import concourse.bass as bass
from concourse import mybir

F32 = mybir.dt.float32
F32R = mybir.dt.float32r
U32 = mybir.dt.uint32
ALU = mybir.AluOpType
ACT = mybir.ActivationFunctionType
AX = mybir.AxisListType

P = 128
IMAGES, SIDE, PATCH = 16, 128, 16
GRID = SIDE // PATCH
PATCHES = GRID * GRID
TOKENS = IMAGES * PATCHES
FEATURES = PATCH * PATCH
HALVES = FEATURES // P
TILES = TOKENS // P
CLS = TILES
BANK = 512
CHUNKS = TOKENS // BANK
CT = TILES // CHUNKS
HEADS, HD = 8, 16
HP = HEADS // 2
KEYS = PATCHES + 1
GROUPS = 4
GI = IMAGES // GROUPS
EXPERTS, HIDDEN = 8, 512
FT = HIDDEN // P
LN1_EPS, LN2_EPS, ATT_EPS, MOE_EPS = 1e-5, 1e-5, 1e-8, 1e-6
EXP_CAP = 16384.0

NOISE_COLS = [("w", 4 * P), ("sw", 4 * P), ("ei", 4), ("eo_row", 2 * P), ("eo_col", 2), ("b", 2), ("sb", 2)]
BODY_COLS = [("w3T", P), ("b3", P), ("pos", P), ("ident", P), ("cls", P), ("wq", P), ("wk", P), ("wv", P),
             ("wout", P), ("bout", P), ("beta_rep", P), ("gamma_rows", P), ("b2_rows", P), ("eye", EXPERTS * EXPERTS),
             ("sel", TILES + 1), ("router", EXPERTS), ("mask", KEYS), ("inv_n", 1),
             ("par_scaled", 2), ("par", 2), ("iota", EXPERTS), ("g_tab", HP), ("b_tab", HP), ("b_col", 1)]


def columns(spec):
    at, found = 0, {}
    for name, width in spec:
        found[name] = (at, at + width)
        at += width
    return found, at


NOISE_AT, NOISE_W = columns(NOISE_COLS)
BODY_AT, BODY_W = columns(BODY_COLS)


def vit_tower(nc, patches, noise, body, b1, w1b1, w2, gb2, out):
    ctx = ExitStack()
    with ctx:
        def sb(name, shape, dtype=F32):
            return ctx.enter_context(nc.sbuf_tensor(name, shape, dtype))

        def sem(name):
            return ctx.enter_context(nc.semaphore(name))

        xT_oT = sb("xT_oT", [P, CHUNKS * HALVES * BANK])
        xT = xT_oT[:, :].rearrange("p (c h n) -> p c h n", c=CHUNKS, h=HALVES)
        noise_sb = sb("noise_sb", [P, NOISE_W])
        body_sb = sb("body_sb", [P, BODY_W])
        NF0, NF1 = NOISE_AT["ei"][0], NOISE_AT["eo_col"][1]
        NFW = NF1 - NF0
        f_abs = sb("f_abs", [P, NFW])
        f_root = sb("f_root", [P, NFW])
        f_sign = sb("f_sign", [P, NFW])
        f_noise = sb("f_noise", [P, NFW])
        sw_eo = sb("sw_eo", [P, 4, P])
        w_noisy = sb("w_noisy", [P, 4, P])
        b_noisy = sb("b_noisy", [P, 2])
        posb = sb("posb", [P, P])
        S = sb("S", [P, GROUPS, HP, GI, KEYS])
        SQ = sb("SQ", [P, GROUPS, HP * GI * KEYS])
        parts = SQ[:, :, :].rearrange("p g n -> p (g n)")
        g_sb = parts[:, 0 * TOKENS:1 * TOKENS]
        n_sb = parts[:, 1 * TOKENS:2 * TOKENS]
        e_sb = parts[:, 2 * TOKENS:3 * TOKENS]
        m_sb = parts[:, 3 * TOKENS:4 * TOKENS]
        pairs = sb("pairs", [P, BANK])
        inv_pair = sb("inv_pair", [P, BANK // 2])
        attnT = sb("attnT", [P, CHUNKS * FT, HP * P])
        last_parts = attnT[:, :, :].rearrange("p n m -> p (n m)")
        r_sb = last_parts[:, 0:TOKENS]
        gn_sb = last_parts[:, TOKENS:2 * TOKENS]
        gT = sb("gT", [P, TOKENS])
        table_scrap = sb("table_scrap", [P, 4])
        zeros = sb("zeros", [P, P])
        h = sb("h", [P, TILES + 1, P])
        hb = sb("hb", [P, TILES + 1, P])
        st = sb("st", [P, TILES + 1, 6])
        mv = sb("mv", [P, TILES + 1, 2])
        ve = sb("ve", [P, TILES + 1])
        rstd = sb("rstd", [P, TILES + 1])
        minus_half = sb("minus_half", [P, TILES + 1])
        xn = sb("xn", [P, TILES + 1, P])
        xnT = sb("xnT", [P, IMAGES, KEYS])
        qTm = sb("qTm", [P, IMAGES, 2, PATCHES])
        kT = sb("kT", [P, IMAGES, KEYS])
        v = sb("v", [KEYS, IMAGES, P])
        xnT_cls = xnT[:, 0, PATCHES:KEYS]
        v_cls_b = sb("v_cls_b", [P, 1])
        NS = GROUPS * HP * GI
        ssum = sb("ssum", [P, NS])
        mu = sb("mu", [P, NS])
        qsum = sb("qsum", [P, NS])
        var = sb("var", [P, NS])
        sd = sb("sd", [P, NS])
        rs = sb("rs", [P, NS])
        rg = sb("rg", [P, NS])
        bmask = sb("bmask", [P, HP, KEYS])
        oT = xT_oT[:, :].rearrange("p (a i r) -> p a i r", a=2, i=IMAGES)
        wout_par = sb("wout_par", [P, 2, P])
        acc = sb("acc", [P, TILES + 1, P])
        x2 = sb("x2", [P, TILES + 1, P])
        x2T = sb("x2T", [P, TOKENS])
        x2T_hi = sb("x2T_hi", [P, TOKENS], F32R)
        x2T_lo = sb("x2T_lo", [P, TOKENS], F32R)
        x2T_cls = sb("x2T_cls", [P, 1])
        b1_sb = sb("b1_sb", [EXPERTS, HIDDEN])
        x2T_each = sb("x2T_each", [P, EXPERTS, EXPERTS])
        cls_units_sb = sb("cls_units_sb", [EXPERTS, HIDDEN])
        cls_hid = sb("cls_hid", [P, FT, EXPERTS])
        cls_hid_each = sb("cls_hid_each", [P, FT, EXPERTS, EXPERTS])
        ones_row = sb("ones_row", [1, EXPERTS])
        E0, E1 = TILES * EXPERTS, (TILES + 1) * EXPERTS
        cls_st = sb("cls_st", [P, 6])
        cls_mv = sb("cls_mv", [P, 2])
        cls_ve = sb("cls_ve", [P, 1])
        cls_rs = sb("cls_rs", [P, 1])
        cls_rows = sb("cls_rows", [P, P])
        beta_sel = sb("beta_sel", [P, TILES, P])
        lg = sb("lg", [P, TILES + 1, EXPERTS])
        top = sb("top", [P, TILES + 1, 8])
        top_at = sb("top_at", [P, TILES + 1, 8], U32)
        top_atf = sb("top_atf", [P, TILES + 1, 2])
        dlt = sb("dlt", [P, TILES + 1])
        ex = sb("ex", [P, TILES + 1])
        den = sb("den", [P, TILES + 1])
        g1 = sb("g1", [P, TILES + 1])
        g2 = sb("g2", [P, TILES + 1])
        sel = sb("sel", [P, 2, TILES + 1, EXPERTS])
        gate = sb("gate", [P, TILES + 1, EXPERTS])
        gateT = sb("gateT", [P, P])
        w1_all = sb("w1_all", [P, EXPERTS, HIDDEN + FT])
        w1_in = [sb(f"w1_in{b}", [P, HIDDEN + FT]) for b in range(2)]
        w2_all = sb("w2_all", [P, EXPERTS, FT, P])
        w1_hi = [sb(f"w1_hi{b}", [P, HIDDEN], F32R) for b in range(2)]
        w1_lo = [sb(f"w1_lo{b}", [P, HIDDEN], F32R) for b in range(2)]
        gb2_in = [sb(f"gb2_in{b}", [P, 2, P]) for b in range(2)]
        V_BANK = [4, 5, 6, 4]
        WARM = 16
        LN_TILES = [(CLS, CLS + 1), (0, CT), (CT, 2 * CT)]
        hid = [attnT[:, FT * c:FT * (c + 1), :] for c in range(CHUNKS)]

        S_flat = S[:, :, :, :, :].rearrange("p g h i k -> p (g h i k)")

        def over_S(n):
            return S_flat[:, n * BANK:(n + 1) * BANK].rearrange("p (t d) -> p t d", d=P)

        x2b = [over_S(c) for c in range(CHUNKS)]
        y = [over_S(2 + c) for c in range(CHUNKS)]
        u = [over_S(4 + c) for c in range(CHUNKS)]
        u_scaled = over_S(6)
        yst = [sb(f"yst{c}", [P, CT, 6]) for c in range(CHUNKS)]
        ymv = [sb(f"ymv{c}", [P, CT, 2]) for c in range(CHUNKS)]
        yd = [sb(f"yd{c}", [P, CT]) for c in range(CHUNKS)]
        ymean = [sb(f"ymean{c}", [P, CT]) for c in range(CHUNKS)]
        yve = [sb(f"yve{c}", [P, CT]) for c in range(CHUNKS)]
        yrs = [sb(f"yrs{c}", [P, CT]) for c in range(CHUNKS)]
        ya = [sb(f"ya{c}", [P, CT]) for c in range(CHUNKS)]

        ps = ctx.enter_context(nc.psum_tensor("ps", [P, 8, BANK], F32))

        def nz(name):
            a, b = NOISE_AT[name]
            return noise_sb[:, a:b]

        def bd(name, rows=P):
            a, b = BODY_AT[name]
            return body_sb[0:rows, a:b]

        def fz(name):
            a, b = NOISE_AT[name]
            return f_noise[:, a - NF0:b - NF0]

        ident = bd("ident")

        noise_in, body_in, patches_in = sem("noise_in"), sem("body_in"), [sem("patches_in0"), sem("patches_in1")]
        w1_loaded, w2_loaded = sem("w1_loaded"), sem("w2_loaded")
        w1_in_loaded = [sem("w1_in_loaded0"), sem("w1_in_loaded1")]
        gb2_loaded = [sem("gb2_loaded0"), sem("gb2_loaded1")]
        f_parts, f_done, w_done, b_done = sem("f_parts"), sem("f_done"), sem("w_done"), sem("b_done")
        f_abs_done = sem("f_abs_done")
        consts_set, pow_const = sem("consts_set"), sem("pow_const")
        gate_ps, inner_ps = sem("gate_ps"), sem("inner_ps")
        gate_read, exp_done, mish_dve, gn_done, gT_done = (
            sem("gate_read"), sem("exp_done"), sem("mish_dve"), sem("gn_done"), sem("gT_done"))
        recip_steps = sem("recip_steps")
        h_ps, h_done, hb_done = sem("h_ps"), sem("h_done"), sem("hb_done")
        ln_stats, ln_ve, ln_rstd = sem("ln_stats"), sem("ln_ve"), sem("ln_rstd")
        xn_done, xnT_ps, xnT_done = sem("xn_done"), sem("xnT_ps"), sem("xnT_done")
        q_ps, k_ps, v_ps, cls_ps = sem("q_ps"), sem("k_ps"), sem("v_ps"), sem("cls_ps")
        q_done, k_done, v_done, cls_done = sem("q_done"), sem("k_done"), sem("v_done"), sem("cls_done")
        scores_ps, S_masked, S_sum, mu_done, S_centred = (
            sem("scores_ps"), sem("S_masked"), sem("S_sum"), sem("mu_done"), sem("S_centred"))
        T_masked, squared, var_done, sd_done, rs_done, rg_done = (
            sem("T_masked"), sem("squared"), sem("var_done"), sem("sd_done"), sem("rs_done"), sem("rg_done"))
        S_scaled, attn_done = sem("S_scaled"), sem("attn_done")
        sq_sum = sem("sq_sum")
        attnT_ps, attnT_done = sem("attnT_ps"), sem("attnT_done")
        o_ps, o_done, proj_ps, acc_done = sem("o_ps"), sem("o_done"), sem("proj_ps"), sem("acc_done")
        ln2_stats, ln2_ve, ln2_rstd, x2_done = sem("ln2_stats"), sem("ln2_ve"), sem("ln2_rstd"), sem("x2_done")
        x2T_ps, x2T_done, x2T_hi_done, x2T_lo_done = (
            sem("x2T_ps"), sem("x2T_done"), sem("x2T_hi_done"), sem("x2T_lo_done"))
        logits_ps, routing, exp_gate, gates_done = sem("logits_ps"), sem("routing"), sem("exp_gate"), sem("gates_done")
        w1_hi_done, w1_lo_done = sem("w1_hi_done"), sem("w1_lo_done")
        hid_ps, hid_done = sem("hid_ps"), sem("hid_done")
        b1_in = sem("b1_in")
        x2T_cls_done, x2T_each_done = sem("x2T_cls_done"), sem("x2T_each_done")
        cls_units_ps, cls_units_done, cls_hid_ps, cls_hid_done, cls_hid_each_done = (
            sem("cls_units_ps"), sem("cls_units_done"), sem("cls_hid_ps"), sem("cls_hid_done"),
            sem("cls_hid_each_done"))
        cls_y_ps, cls_row_done, cls_ve_done, cls_rs_done = (
            sem("cls_y_ps"), sem("cls_row_done"), sem("cls_ve_done"), sem("cls_rs_done"))
        zeros_set = sem("zeros_set")
        beta_sel_done = sem("beta_sel_done")
        y_ps, y_read = sem("y_ps"), sem("y_read")
        x2b_done, y_stats, y_parts, y_var, y_ve, y_rs, y_a, u_done, moe_acc = (
            sem("x2b_done"), sem("y_stats"), sem("y_parts"), sem("y_var"), sem("y_ve"), sem("y_rs"), sem("y_a"), sem("u_done"),
            sem("moe_acc"))
        last_scaled, last_acc = sem("last_scaled"), sem("last_acc")
        gateT_ps, gateT_done, beta_ps, final_done, stored = (
            sem("gateT_ps"), sem("gateT_done"), sem("beta_ps"), sem("final_done"), sem("stored"))

        bn1_done, bn2_done, topped = sem("bn1_done"), sem("bn2_done"), sem("topped")

        block = ctx.enter_context(nc.Block())

        @block.sync
        def _(sp):
            sp.dma_start(noise_sb[:, :], noise).then_inc(noise_in, 16)
            for c in range(CHUNKS):
                sp.dma_start(xT[:, c, :, :], patches[:, c, :, :]).then_inc(patches_in[c], 16)
            sp.dma_start(body_sb[:, :], body).then_inc(body_in, 16)

            sp.dma_start(b1_sb[:, :], b1).then_inc(b1_in, 16)
            sp.dma_start(w1_all[:, :, :], w1b1).then_inc(w1_loaded, 16)
            sp.dma_start(w2_all[:, :, :, :], w2).then_inc(w2_loaded, 16)

            def load_expert(e, b):
                sp.dma_start(w1_in[b][:, :], w1b1[:, bass.ds(e, 1), :].rearrange("p a n -> p (a n)")
                             ).then_inc(w1_in_loaded[b], 16)
                sp.dma_start(gb2_in[b][:, :, :], gb2[bass.ds(e, 1), :, :].to_broadcast([P, 2, P])
                             ).then_inc(gb2_loaded[b], 16)

            for b in range(2):
                load_expert(b, b)
            with sp.Fori(0, EXPERTS // 2 - 1) as it:
                for b in range(2):
                    sp.wait_ge(moe_acc, 2 * (2 * it + b + 1))
                    load_expert(2 * it + b + 2, b)

            sp.wait_ge(final_done, CHUNKS + 1)
            sp.dma_start(out[:, 0:1, :].rearrange("t r d -> r t d"),
                         acc[0:1, CLS:CLS + 1, :].to_broadcast([1, IMAGES, P])).then_inc(stored, 16)
            for c in range(CHUNKS):
                sp.wait_ge(*[(last_acc, 1), (moe_acc, 2 * EXPERTS - 1)][c])
                for b in range(2):
                    rows = acc[PATCHES * b:PATCHES * (b + 1), CT * c:CT * (c + 1), :]
                    dst = out[2 * CT * c + b:2 * CT * (c + 1):2, 1:KEYS, :].rearrange("t r d -> r t d")
                    sp.dma_start(dst, rows).then_inc(stored, 16)
            sp.wait_ge(stored, 16 * (2 * CHUNKS + 1))

        @block.gpsimd
        def _(pool):
            nc.gpsimd.memset(minus_half[:, :], -0.5).then_inc(pow_const, 1)
            pool.wait_ge(pow_const, 1)

            def ln_power(stats, ve_sem, out_sem, eps, n):
                a, b = LN_TILES[n]
                pool.wait_ge(stats, n + 1)
                nc.gpsimd.tensor_scalar(ve[:, a:b], mv[:, a:b, 1], eps, None, ALU.add).then_inc(ve_sem, 1)
                pool.wait_ge(ve_sem, n + 1)
                nc.gpsimd.tensor_tensor(rstd[:, a:b], ve[:, a:b], minus_half[:, a:b], ALU.pow).then_inc(out_sem, 1)

            ln_power(ln_stats, ln_ve, ln_rstd, LN1_EPS, 0)
            for c in range(CHUNKS):
                sl = slice(c * BANK, (c + 1) * BANK)
                pool.wait_ge(mish_dve, 3 * c + 2)
                pool.wait_ge(gate_read, c + 1)
                nc.gpsimd.tensor_tensor(gn_sb[:, sl], g_sb[:, sl], n_sb[:, sl], ALU.mult).then_inc(gn_done, 1)
                if c == 0:
                    pool.wait_ge(xn_done, 1)
                    ln_power(ln2_stats, ln2_ve, ln2_rstd, LN2_EPS, 0)

            for n in (1, 2):
                ln_power(ln_stats, ln_ve, ln_rstd, LN1_EPS, n)

            def centre_masked(g):
                pool.wait_ge(S_centred, g + 1)
                t = S[:, g, :, :, :].rearrange("p h i k -> p (h i) k")
                nc.gpsimd.tensor_tensor(t, t, bd("mask").unsqueeze(1).to_broadcast([P, HP * GI, KEYS]), ALU.mult
                                        ).then_inc(T_masked, 1)

            def scale(g):
                pool.wait_ge(rg_done, g + 1)
                t = S[:, g, :, :, :].rearrange("p h i k -> p (h i) k")
                r = rg[:, g * HP * GI:(g + 1) * HP * GI].unsqueeze(2).to_broadcast([P, HP * GI, KEYS])
                nc.gpsimd.tensor_tensor(t, t, r, ALU.mult).then_inc(S_scaled, 1)

            centre_masked(0)
            centre_masked(1)
            scale(0)
            pool.wait_ge(h_done, CHUNKS)
            pool.wait_ge(body_in, 16)
            nc.gpsimd.tensor_tensor(hb[:, 0:TILES, :], h[:, 0:TILES, :],
                                    bd("bout").unsqueeze(1).to_broadcast([P, TILES, P]), ALU.add
                                    ).then_inc(hb_done, 1)
            for g in range(2, GROUPS):
                centre_masked(g)
                scale(g - 1)
            scale(GROUPS - 1)
            nc.gpsimd.tensor_tensor(beta_sel[0:E0, :, :], bd("beta_rep", E0).unsqueeze(1).to_broadcast([E0, TILES, P]),
                                    bd("sel", E0)[:, 0:TILES].unsqueeze(2).to_broadcast([E0, TILES, P]), ALU.mult
                                    ).then_inc(beta_sel_done, 1)
            ln_power(ln2_stats, ln2_ve, ln2_rstd, LN2_EPS, 1)

            def w1_low(e, b):
                pool.wait_ge(w1_hi_done, e + 1)
                nc.gpsimd.tensor_tensor(w1_lo[b][:, :], w1_in[b][:, 0:HIDDEN], w1_hi[b][:, :].bitcast(F32),
                                        ALU.subtract).then_inc(w1_lo_done, 1)

            def x2_low(c):
                sl = slice(c * BANK, (c + 1) * BANK)
                pool.wait_ge(x2T_hi_done, c + 1)
                nc.gpsimd.tensor_tensor(x2T_lo[:, sl], x2T[:, sl], x2T_hi[:, sl].bitcast(F32), ALU.subtract
                                        ).then_inc(x2T_lo_done, 1)

            pool.wait_ge(w1_in_loaded[0], 16)
            w1_low(0, 0)
            x2_low(0)
            ln_power(ln2_stats, ln2_ve, ln2_rstd, LN2_EPS, 2)
            x2_low(1)

            def expert(it, b, split_next, first=False, last=False):
                e = 2 * it + b
                pool.wait_ge(gb2_loaded[b], 16 * (it + 1))
                for c in range(CHUNKS):
                    if first:
                        pool.wait_ge(attnT_ps, IMAGES)
                        pool.wait_ge(x2_done, CT * (c + 1) + 1)
                    else:
                        pool.wait_ge(y_read, 2 * e + c - 1)
                    nc.gpsimd.tensor_tensor(x2b[c], x2[:, CT * c:CT * (c + 1), :],
                                            gb2_in[b][:, 1:2, :].to_broadcast([P, CT, P]), ALU.add
                                            ).then_inc(x2b_done, 1)
                if split_next:
                    w1_low(e + 1, 1 - b)
                if first:
                    pool.wait_ge(cls_ve_done, 1)
                    pool.wait_ge(w1_lo_done, 2)
                    nc.gpsimd.tensor_tensor(cls_rs[E0:E1, :], cls_ve[E0:E1, :], minus_half[E0:E1, 0:1], ALU.pow
                                            ).then_inc(cls_rs_done, 1)
                    pool.wait_ge(cls_rs_done, 1)
                for c in range(CHUNKS):
                    n = 2 * e + c + 1
                    pool.wait_ge(y_ve, n)
                    nc.gpsimd.tensor_tensor(yrs[c][:, :], yve[c][:, :], minus_half[:, 0:CT], ALU.pow
                                            ).then_inc(y_rs, 1)
                    pool.wait_ge(y_rs, n)
                    if first:
                        pool.wait_ge(gates_done, 1)
                    nc.gpsimd.tensor_tensor(ya[c][:, :].unsqueeze(2), yrs[c][:, :].unsqueeze(2),
                                            gate[:, CT * c:CT * (c + 1), bass.ds(e, 1)], ALU.mult).then_inc(y_a, 1)
                    if last and c == 0:
                        pool.wait_ge(last_scaled, 1)
                        pool.wait_ge(moe_acc, 2 * (EXPERTS - 1))
                        nc.gpsimd.tensor_tensor(acc[:, 0:CT, :], acc[:, 0:CT, :], u_scaled, ALU.add
                                                ).then_inc(last_acc, 1)

            expert(0, 0, True, first=True)
            expert(0, 1, True)
            with pool.Fori(1, EXPERTS // 2 - 1) as it:
                for b in range(2):
                    expert(it, b, True)
            expert(EXPERTS // 2 - 1, 0, True)
            expert(EXPERTS // 2 - 1, 1, False, last=True)

        @block.scalar
        def _(act):
            act.wait_ge(zeros_set, 2)
            nc.scalar.activation(table_scrap[:, 0:1], zeros[:, 0:1], ACT.Sqrt)
            act.wait_ge(noise_in, 16)
            nc.scalar.activation(f_sign[:, :], noise_sb[:, NF0:NF1], ACT.Sign).then_inc(f_parts, 1)
            act.wait_ge(f_abs_done, 1)
            nc.scalar.activation(f_root[:, :], f_abs[:, :], ACT.Sqrt).then_inc(f_parts, 1)

            nc.scalar.activation(table_scrap[:, 1:2], zeros[:, 0:1], ACT.Exp)

            def gate_parts(c):
                sl = slice(c * BANK, (c + 1) * BANK)
                act.wait_ge(gate_ps, c + 1)
                nc.scalar.activation(e_sb[:, sl], ps[:, 2 * c, :], ACT.Exp, bias=b_noisy[:, 0:1]).then_inc(exp_done, 1)
                nc.scalar.activation(g_sb[:, sl], ps[:, 2 * c, :], ACT.Identity, bias=b_noisy[:, 0:1]
                                     ).then_inc(gate_read, 1)

            act.wait_ge(b_done, 1)
            gate_parts(0)
            act.wait_ge(xnT_ps, 1)
            nc.scalar.copy(xnT[:, :, PATCHES:KEYS], ps[:, 7, 0:1].unsqueeze(1).to_broadcast([P, IMAGES, 1])
                           ).then_inc(xnT_done, 1)
            act.wait_ge(cls_ps, 1)
            nc.scalar.activation(v_cls_b[:, :], ps[:, 7, 2:3], ACT.Copy, scale=bd("b_col")).then_inc(cls_done, 1)
            nc.scalar.copy(kT[:, :, PATCHES:KEYS], ps[:, 7, 1:2].unsqueeze(1).to_broadcast([P, IMAGES, 1])
                           ).then_inc(cls_done, 1)
            gate_parts(1)
            act.wait_ge(x2T_ps, 1)
            nc.scalar.copy(x2T_cls[:, :], ps[:, 7, 3:4]).then_inc(x2T_cls_done, 1)

            def copy_norm(c):
                act.wait_ge(xnT_ps, c + 2)
                nc.scalar.copy(xnT[:, 8 * c:8 * (c + 1), 0:PATCHES],
                               ps[:, 6, :].rearrange("p (i r) -> p i r", r=PATCHES)).then_inc(xnT_done, 1)

            def copy_q(c):
                act.wait_ge(q_ps, c + 1)
                for a in range(2):
                    nc.scalar.activation(qTm[:, c * 8:(c + 1) * 8, a, :],
                                         ps[:, [2, 6][c], :].rearrange("p (i r) -> p i r", r=PATCHES), ACT.Copy,
                                         scale=bd("par_scaled")[:, a:a + 1]).then_inc(q_done, 1)

            def copy_k(c):
                act.wait_ge(k_ps, c + 1)
                nc.scalar.copy(kT[:, 8 * c:8 * (c + 1), 0:PATCHES],
                               ps[:, 4 + c, :].rearrange("p (i r) -> p i r", r=PATCHES)).then_inc(k_done, 1)

            def copy_v(g):
                act.wait_ge(v_ps, g + 1)
                nc.scalar.copy(v[:, g * GI:(g + 1) * GI, :],
                               ps[0:KEYS, V_BANK[g], :].rearrange("p (i d) -> p i d", d=P)).then_inc(v_done, 1)

            def square(g):
                act.wait_ge(T_masked, g + 1)
                nc.scalar.activation(SQ[:, g, :], S[:, g, :, :, :].rearrange("p h i k -> p (h i k)"), ACT.Square
                                     ).then_inc(squared, 1)

            def root(g):
                cols = slice(g * HP * GI, (g + 1) * HP * GI)
                act.wait_ge(var_done, g + 1)
                nc.scalar.activation(sd[:, cols], var[:, cols], ACT.Sqrt).then_inc(sd_done, 1)

            def copy_attnT(n):
                act.wait_ge(attnT_ps, n + 1)
                if n >= 8:
                    act.wait_ge(o_ps, (n - 8) // GI + 1)
                nc.scalar.copy(attnT[0:KEYS, n % 8, :], ps[0:KEYS, 4 + n % 2, :]).then_inc(attnT_done, 1)

            def copy_o(g):
                act.wait_ge(o_ps, g + 1)
                nc.scalar.copy(oT[:, :, g * GI:(g + 1) * GI, :].rearrange("p a i r -> p i a r"),
                               ps[:, 6 + g % 2, :].rearrange("p (i a r) -> p i a r", a=2, r=PATCHES)
                               ).then_inc(o_done, 1)

            copy_norm(0)
            copy_q(0)
            copy_norm(1)
            nc.scalar.activation(table_scrap[:, 2:3], zeros[:, 0:1], ACT.Sqrt)
            copy_q(1)
            copy_k(1)
            square(0)
            copy_v(0)
            root(0)
            copy_v(1)
            square(1)
            copy_v(2)
            copy_v(3)
            act.wait_ge(w1_in_loaded[0], 16)
            nc.scalar.copy(w1_hi[0][:, :], w1_in[0][:, 0:HIDDEN]).then_inc(w1_hi_done, 1)
            root(1)
            square(2)
            for i in range(GI):
                copy_attnT(i)
            copy_attnT(4)
            root(2)
            square(3)
            copy_attnT(5)
            copy_o(0)
            copy_attnT(6)
            copy_attnT(7)
            root(3)
            copy_attnT(8)
            copy_attnT(9)
            copy_o(1)
            copy_attnT(10)
            copy_attnT(11)
            copy_attnT(12)
            copy_attnT(13)
            copy_o(2)
            copy_attnT(14)
            copy_attnT(15)

            def copy_norm2(c):
                sl = slice(c * BANK, (c + 1) * BANK)
                act.wait_ge(x2T_ps, c + 2)
                nc.scalar.copy(x2T[:, sl], ps[:, [2, 5][c], :]).then_inc(x2T_done, 1)
                act.wait_ge(x2T_done, c + 1)
                nc.scalar.copy(x2T_hi[:, sl], x2T[:, sl]).then_inc(x2T_hi_done, 1)

            def relu_units(it, b, c, first=False):
                e = 2 * it + b
                if not first:
                    act.wait_ge(y_ps, 2 * (e - 1) + c + 1)
                for f in range(FT):
                    act.wait_ge(hid_ps, (2 * e + c) * FT + f + 1)
                    nc.scalar.activation(hid[c][:, f, :], ps[:, f, :], ACT.Relu,
                                         bias=w1_in[b][:, HIDDEN + f:HIDDEN + f + 1]).then_inc(hid_done, 1)

            def split_w1(it, b):
                act.wait_ge(w1_in_loaded[b], 16 * (it + 1))
                nc.scalar.copy(w1_hi[b][:, :], w1_in[b][:, 0:HIDDEN]).then_inc(w1_hi_done, 1)

            def expert(it, b):
                e = 2 * it + b
                act.wait_ge(hid_ps, (2 * e - 2) * FT)
                split_w1(it, b)
                for c in range(CHUNKS):
                    relu_units(it, b, c)

            copy_o(3)
            copy_norm2(0)
            relu_units(0, 0, 0, True)
            copy_norm2(1)
            split_w1(0, 1)
            act.wait_ge(routing, 4)
            nc.scalar.activation(ex[:, :], dlt[:, :], ACT.Exp).then_inc(exp_gate, 1)

            relu_units(0, 0, 1, True)
            act.wait_ge(gateT_ps, 1)
            nc.scalar.copy(gateT[0:E1, :], ps[0:E1, 6, 0:P]).then_inc(gateT_done, 1)
            for c in range(CHUNKS):
                relu_units(0, 1, c)
            with act.Fori(1, EXPERTS // 2) as it:
                for b in range(2):
                    expert(it, b)
            act.wait_ge(y_a, 2 * EXPERTS - 1)
            act.wait_ge(u_done, 2 * EXPERTS - 1)
            for t in range(CT):
                last = nc.scalar.activation(u_scaled[:, t, :], u[0][:, t, :], ACT.Copy, scale=ya[0][:, t:t + 1])
            last.then_inc(last_scaled, 1)

        @block.vector
        def _(dve):
            nc.vector.memset(ones_row[:, :], 1.0).then_inc(zeros_set, 1)
            nc.vector.memset(zeros[:, :], 0.0).then_inc(zeros_set, 1)
            nc.vector.memset(h[:, CLS, :], 0.0).then_inc(consts_set, 1)
            nc.vector.memset(acc[:, CLS, :], 0.0).then_inc(consts_set, 1)
            dve.wait_ge(noise_in, 16)
            raw = noise_sb[:, NF0:NF1]
            nc.vector.scalar_tensor_tensor(out=f_abs[:, :], in0=raw, scalar=-1.0, in1=raw, op0=ALU.mult, op1=ALU.max
                                           ).then_inc(f_abs_done, 1)
            dve.wait_ge(f_parts, 2)
            nc.vector.tensor_tensor(f_noise[:, :], f_root[:, :], f_sign[:, :], ALU.mult).then_inc(f_done, 1)
            dve.wait_ge(f_done, 1)
            for k in range(2):
                nc.vector.tensor_tensor(
                    sw_eo[:, 2 * k:2 * k + 2, :], nz("sw").rearrange("p (k n) -> p k n", n=P)[:, 2 * k:2 * k + 2, :],
                    fz("eo_row")[:, k * P:(k + 1) * P].unsqueeze(1).to_broadcast([P, 2, P]), ALU.mult
                ).then_inc(f_done, 1)
            dve.wait_ge(f_done, 3)
            for k in range(4):
                nc.vector.scalar_tensor_tensor(out=w_noisy[:, k, :], in0=sw_eo[:, k, :], scalar=fz("ei")[:, k:k + 1],
                                               in1=nz("w")[:, k * P:(k + 1) * P], op0=ALU.mult, op1=ALU.add
                                               ).then_inc(w_done, 1)
            nc.vector.tensor_tensor(b_noisy[:, :], nz("sb"), fz("eo_col"), ALU.mult).then_inc(f_done, 1)
            dve.wait_ge(f_done, 4)
            nc.vector.tensor_tensor(b_noisy[:, :], b_noisy[:, :], nz("b"), ALU.add).then_inc(b_done, 1)
            dve.wait_ge(body_in, 16)
            dve.wait_ge(consts_set, 2)
            nc.vector.tensor_copy(h[0:1, CLS, :], bd("cls", 1)).then_inc(consts_set, 1)
            nc.vector.tensor_tensor(hb[0:1, CLS, :], bd("cls", 1), bd("bout", 1), ALU.add).then_inc(consts_set, 1)
            dve.wait_ge(consts_set, 4)

            def stats(src, sem_done, n):
                a, b = LN_TILES[n]
                for t in range(a, b):
                    nc.vector.bn_stats(st[:, t, :], src[:, t, :]).then_inc(sem_done[0], 1)
                dve.wait_ge(sem_done[0], [1, CT + 1, 2 * CT + 1][n])
                for t in range(a, b):
                    last = nc.vector.bn_aggr(mv[:, t, :], st[:, t, :])
                last.then_inc(sem_done[1], 1)

            def normalise(dst, src, rstd_sem, out_sem, n):
                dve.wait_ge(rstd_sem, n + 1)
                for t in range(*LN_TILES[n]):
                    nc.vector.tensor_scalar(dst[:, t, :], src[:, t, :], mv[:, t, 0:1], rstd[:, t:t + 1],
                                            ALU.subtract, ALU.mult).then_inc(out_sem, 1)

            stats(h, (bn1_done, ln_stats), 0)

            Q = BANK // 4

            def recip_of(c):
                m, r = m_sb[:, c * BANK:(c + 1) * BANK], r_sb[:, c * BANK:(c + 1) * BANK]
                pair = pairs[:, :]

                def step(out, a, b_, n):
                    nc.vector.tensor_tensor(out, a, b_, ALU.mult).then_inc(recip_steps, 1)
                    dve.wait_ge(recip_steps, 7 * c + n)

                step(pair[:, 0:2 * Q], m[:, 0:2 * Q], m[:, 2 * Q:4 * Q], 1)
                step(pair[:, 2 * Q:3 * Q], pair[:, 0:Q], pair[:, Q:2 * Q], 2)
                nc.vector.reciprocal(pair[:, 3 * Q:4 * Q], pair[:, 2 * Q:3 * Q]).then_inc(recip_steps, 1)
                dve.wait_ge(recip_steps, 7 * c + 3)
                nc.vector.tensor_tensor(inv_pair[:, 0:Q], pair[:, 3 * Q:4 * Q], pair[:, Q:2 * Q], ALU.mult
                                        ).then_inc(recip_steps, 1)
                nc.vector.tensor_tensor(inv_pair[:, Q:2 * Q], pair[:, 3 * Q:4 * Q], pair[:, 0:Q], ALU.mult
                                        ).then_inc(recip_steps, 1)
                dve.wait_ge(recip_steps, 7 * c + 5)
                nc.vector.tensor_tensor(r[:, 0:2 * Q], inv_pair[:, :], m[:, 2 * Q:4 * Q], ALU.mult
                                        ).then_inc(recip_steps, 1)
                nc.vector.tensor_tensor(r[:, 2 * Q:4 * Q], inv_pair[:, :], m[:, 0:2 * Q], ALU.mult
                                        ).then_inc(recip_steps, 1)
                dve.wait_ge(recip_steps, 7 * c + 7)

            def mish_start(c):
                sl = slice(c * BANK, (c + 1) * BANK)
                dve.wait_ge(exp_done, c + 1)
                nc.vector.tensor_scalar(e_sb[:, sl], e_sb[:, sl], EXP_CAP, None, ALU.min).then_inc(mish_dve, 1)
                dve.wait_ge(mish_dve, 3 * c + 1)
                nc.vector.scalar_tensor_tensor(out=n_sb[:, sl], in0=e_sb[:, sl], scalar=2.0, in1=e_sb[:, sl],
                                               op0=ALU.add, op1=ALU.mult).then_inc(mish_dve, 1)
                dve.wait_ge(mish_dve, 3 * c + 2)
                nc.vector.tensor_scalar(m_sb[:, sl], n_sb[:, sl], 2.0, None, ALU.add).then_inc(mish_dve, 1)
                dve.wait_ge(mish_dve, 3 * c + 3)

            def mish_end(c):
                sl = slice(c * BANK, (c + 1) * BANK)
                dve.wait_ge(gn_done, c + 1)
                nc.vector.tensor_tensor(gn_sb[:, sl], gn_sb[:, sl], r_sb[:, sl], ALU.mult).then_inc(gT_done, 1)
                dve.wait_ge(gT_done, 2 * c + 1)
                dve.wait_ge(inner_ps, c + 1)
                nc.vector.scalar_tensor_tensor(out=gT[:, sl], in0=ps[:, 2 * c + 1, :], scalar=b_noisy[:, 1:2],
                                               in1=gn_sb[:, sl], op0=ALU.add, op1=ALU.mult).then_inc(gT_done, 1)

            def embed(c):
                dve.wait_ge(h_ps, c + 1)
                nc.vector.tensor_tensor(h[:, CT * c:CT * (c + 1), :],
                                        ps[:, 4 + c, :].rearrange("p (t d) -> p t d", d=P),
                                        posb[:, :].unsqueeze(1).to_broadcast([P, CT, P]), ALU.add).then_inc(h_done, 1)
                dve.wait_ge(h_done, c + 1)
                stats(h, (bn1_done, ln_stats), c + 1)

            def copy_k(c):
                dve.wait_ge(k_ps, c + 1)
                nc.vector.tensor_copy(kT[:, 8 * c:8 * (c + 1), 0:PATCHES],
                                      ps[:, 4 + c, :].rearrange("p (i r) -> p i r", r=PATCHES)).then_inc(k_done, 1)

            GS = HP * GI

            def rows(g):
                return S[:, g, :, :, :].rearrange("p h i k -> p (h i) k")

            def centre(g):
                dve.wait_ge(scores_ps, g + 1)
                src = ps[:, 0:HP, 0:GI * KEYS].rearrange("p h (i k) -> p h i k", k=KEYS)
                nc.vector.tensor_tensor(
                    S[:, g, :, :, :], src,
                    bd("mask").unsqueeze(1).unsqueeze(1).to_broadcast([P, HP, GI, KEYS]), ALU.mult
                ).then_inc(S_masked, 1)
                dve.wait_ge(S_masked, g + 1)
                cols = slice(g * GS, (g + 1) * GS)
                nc.vector.tensor_reduce(ssum[:, cols], rows(g), AX.X, ALU.add).then_inc(S_sum, 1)
                dve.wait_ge(S_sum, g + 1)
                nc.vector.tensor_scalar(mu[:, cols], ssum[:, cols], bd("inv_n"), None, ALU.mult).then_inc(mu_done, 1)
                dve.wait_ge(mu_done, g + 1)
                nc.vector.tensor_tensor(rows(g), rows(g), mu[:, cols].unsqueeze(2).to_broadcast([P, GS, KEYS]),
                                        ALU.subtract).then_inc(S_centred, 1)

            def variance(g):
                cols = slice(g * GS, (g + 1) * GS)
                dve.wait_ge(squared, g + 1)
                nc.vector.tensor_reduce(qsum[:, cols], SQ[:, g, :].rearrange("p (n k) -> p n k", k=KEYS),
                                        AX.X, ALU.add).then_inc(sq_sum, 1)
                dve.wait_ge(sq_sum, g + 1)
                nc.vector.tensor_scalar(var[:, cols], qsum[:, cols], bd("inv_n"), ATT_EPS, ALU.mult, ALU.add
                                        ).then_inc(var_done, 1)

            def gain(g):
                cols = slice(g * GS, (g + 1) * GS)
                dve.wait_ge(sd_done, g + 1)
                nc.vector.reciprocal(rs[:, cols], sd[:, cols]).then_inc(rs_done, 1)
                dve.wait_ge(rs_done, g + 1)
                nc.vector.tensor_tensor(
                    rg[:, cols].rearrange("p (h i) -> p h i", h=HP), rs[:, cols].rearrange("p (h i) -> p h i", h=HP),
                    bd("g_tab").unsqueeze(2).to_broadcast([P, HP, GI]), ALU.mult).then_inc(rg_done, 1)

            def add_bias(g):
                dve.wait_ge(S_scaled, g + 1)
                dve.wait_ge(consts_set, 8)
                nc.vector.tensor_tensor(S[:, g, :, :, :], S[:, g, :, :, :],
                                        bmask[:, :, :].unsqueeze(2).to_broadcast([P, HP, GI, KEYS]), ALU.add
                                        ).then_inc(attn_done, 1)

            eye = bd("eye").rearrange("p (e n) -> p e n", n=EXPERTS)
            mish_start(0)
            normalise(xn, h, ln_rstd, xn_done, 0)
            recip_of(0)
            mish_end(0)
            dve.wait_ge(proj_ps, 1)
            nc.vector.tensor_tensor(acc[0:1, CLS, :], ps[0:1, 7, P:2 * P], hb[0:1, CLS, :], ALU.add).then_inc(acc_done, 1)
            dve.wait_ge(acc_done, 1)
            stats(acc, (bn2_done, ln2_stats), 0)
            mish_start(1)
            normalise(x2, acc, ln2_rstd, x2_done, 0)
            nc.vector.tensor_tensor(posb[:, :], bd("pos"), bd("b3"), ALU.add).then_inc(consts_set, 1)
            dve.wait_ge(consts_set, 5)
            embed(0)
            dve.wait_ge(x2T_cls_done, 1)
            nc.vector.tensor_scalar(x2T_each[:, :, :], eye, x2T_cls[:, 0:1], None, ALU.mult).then_inc(x2T_each_done, 1)
            recip_of(1)
            normalise(xn, h, ln_rstd, xn_done, 1)
            mish_end(1)
            nc.vector.tensor_tensor(bmask[:, :, :], bd("b_tab").unsqueeze(2).to_broadcast([P, HP, KEYS]),
                                    bd("mask").unsqueeze(1).to_broadcast([P, HP, KEYS]), ALU.mult
                                    ).then_inc(consts_set, 1)
            for a in range(2):
                nc.vector.tensor_scalar(wout_par[:, a, :], bd("wout"), bd("par")[:, a:a + 1], None, ALU.mult
                                        ).then_inc(consts_set, 1)
            copy_k(0)
            embed(1)
            normalise(xn, h, ln_rstd, xn_done, 2)
            centre(0)
            centre(1)
            variance(0)
            gain(0)
            for g in range(2, GROUPS + 2):
                if g < GROUPS:
                    centre(g)
                if g == 3:
                    dve.wait_ge(cls_hid_ps, 1)
                    nc.vector.tensor_scalar(cls_hid[:, :, :], ps[:, 7, 0:FT * EXPERTS].rearrange("p (f e) -> p f e", f=FT),
                                            0.0, None, ALU.max).then_inc(cls_hid_done, 1)
                if g == GROUPS:
                    variance(g - 1)
                add_bias(g - 2)
                if g < GROUPS:
                    variance(g - 1)
                if g <= GROUPS:
                    gain(g - 1)
                if g == 2:
                    dve.wait_ge(cls_units_ps, 1)
                    dve.wait_ge(b1_in, 16)
                    nc.vector.tensor_tensor(cls_units_sb[:, :], ps[0:EXPERTS, 7, :], b1_sb[:, :], ALU.add
                                            ).then_inc(cls_units_done, 1)
                if g == 3:
                    dve.wait_ge(cls_hid_done, 1)
                    for f in range(FT):
                        last = nc.vector.tensor_tensor(
                            cls_hid_each[:, f, :, :], cls_hid[:, f, :].unsqueeze(2).to_broadcast([P, EXPERTS, EXPERTS]),
                            eye, ALU.mult)
                    last.then_inc(cls_hid_each_done, 1)

            def cls_norm():
                dve.wait_ge(cls_y_ps, 1)
                nc.vector.tensor_tensor(cls_rows[E0:E1, :], ps[E0:E1, 7, 0:P], body_rows("b2_rows"), ALU.add
                                        ).then_inc(cls_row_done, 1)
                dve.wait_ge(cls_row_done, 1)
                nc.vector.bn_stats(cls_st[E0:E1, :], cls_rows[E0:E1, :]).then_inc(cls_row_done, 1)
                dve.wait_ge(cls_row_done, 2)
                nc.vector.bn_aggr(cls_mv[E0:E1, :], cls_st[E0:E1, :]).then_inc(cls_row_done, 1)
                dve.wait_ge(cls_row_done, 3)
                nc.vector.tensor_scalar(cls_ve[E0:E1, :], cls_mv[E0:E1, 1:2], MOE_EPS, None, ALU.add
                                        ).then_inc(cls_ve_done, 1)

            def cls_affine():
                dve.wait_ge(cls_rs_done, 1)
                nc.vector.tensor_scalar(cls_rows[E0:E1, :], cls_rows[E0:E1, :], cls_mv[E0:E1, 0:1], cls_rs[E0:E1, 0:1],
                                        ALU.subtract, ALU.mult).then_inc(cls_row_done, 1)
                dve.wait_ge(cls_row_done, 4)
                nc.vector.tensor_tensor(cls_rows[E0:E1, :], cls_rows[E0:E1, :], body_rows("gamma_rows"), ALU.mult
                                        ).then_inc(cls_row_done, 1)
                dve.wait_ge(cls_row_done, 5)
                nc.vector.tensor_tensor(cls_rows[E0:E1, :], cls_rows[E0:E1, :], body_rows("beta_rep"), ALU.add
                                        ).then_inc(cls_row_done, 1)

            def body_rows(name):
                return bd(name)[E0:E1, :]

            dve.wait_ge(hb_done, 1)
            dve.wait_ge(xn_done, TILES + 1)
            for c in range(CHUNKS):
                dve.wait_ge(proj_ps, c + 2)
                nc.vector.tensor_tensor(acc[:, CT * c:CT * (c + 1), :],
                                        ps[:, c, :].rearrange("p (t d) -> p t d", d=P),
                                        hb[:, CT * c:CT * (c + 1), :], ALU.add).then_inc(acc_done, 1)
                dve.wait_ge(acc_done, c + 2)
                stats(acc, (bn2_done, ln2_stats), c + 1)
                normalise(x2, acc, ln2_rstd, x2_done, c + 1)

            dve.wait_ge(logits_ps, 1)
            nc.vector.tensor_copy(lg[:, 0:TILES, :], ps[:, 6, 0:TILES * EXPERTS].rearrange("p (t e) -> p t e", e=EXPERTS)
                                  ).then_inc(routing, 1)
            nc.vector.tensor_copy(lg[:, CLS, :], bd("iota")).then_inc(routing, 1)
            dve.wait_ge(routing, 2)
            nc.vector.tensor_copy(lg[0:1, CLS, :], ps[0:1, 6, TILES * EXPERTS:(TILES + 1) * EXPERTS]
                                  ).then_inc(routing, 1)
            dve.wait_ge(routing, 3)
            for t in range(TILES + 1):
                nc.vector.max(top[:, t, :], lg[:, t, :]).then_inc(topped, 1)
            dve.wait_ge(topped, TILES + 1)
            nc.vector.tensor_tensor(dlt[:, :], top[:, :, 1], top[:, :, 0], ALU.subtract).then_inc(routing, 1)
            for t in range(TILES + 1):
                nc.vector.max_index(top_at[:, t, :], top[:, t, :], lg[:, t, :]).then_inc(topped, 1)
            dve.wait_ge(topped, 2 * (TILES + 1))
            nc.vector.tensor_copy(top_atf[:, :, :], top_at[:, :, 0:2]).then_inc(topped, 1)
            dve.wait_ge(exp_gate, 1)
            nc.vector.tensor_scalar(den[:, :], ex[:, :], 1.0, None, ALU.add).then_inc(topped, 1)
            dve.wait_ge(topped, 2 * (TILES + 1) + 2)
            nc.vector.reciprocal(g1[:, :], den[:, :]).then_inc(topped, 1)
            dve.wait_ge(topped, 2 * (TILES + 1) + 3)
            nc.vector.tensor_tensor(g2[:, :], ex[:, :], g1[:, :], ALU.mult).then_inc(topped, 1)
            iota = bd("iota").unsqueeze(1).to_broadcast([P, TILES + 1, EXPERTS])
            for k in range(2):
                nc.vector.tensor_tensor(sel[:, k, :, :], iota,
                                        top_atf[:, :, k:k + 1].to_broadcast([P, TILES + 1, EXPERTS]), ALU.is_equal
                                        ).then_inc(topped, 1)
            dve.wait_ge(topped, 2 * (TILES + 1) + 6)
            for k, gk in ((0, g1), (1, g2)):
                nc.vector.tensor_tensor(sel[:, k, :, :], sel[:, k, :, :],
                                        gk[:, :].unsqueeze(2).to_broadcast([P, TILES + 1, EXPERTS]), ALU.mult
                                        ).then_inc(topped, 1)
            dve.wait_ge(topped, 2 * (TILES + 1) + 8)
            nc.vector.tensor_tensor(gate[:, :, :], sel[:, 0, :, :], sel[:, 1, :, :], ALU.add).then_inc(gates_done, 1)

            def expert(it, b, last_expert=False):
                e = 2 * it + b
                dve.wait_ge(gb2_loaded[b], 16 * (it + 1))
                for c in range(CHUNKS):
                    n = 2 * e + c + 1
                    dve.wait_ge(y_ps, n)
                    dve.wait_ge(x2b_done, n)
                    nc.vector.tensor_tensor(y[c], ps[:, 4 + c, :].rearrange("p (t d) -> p t d", d=P), x2b[c], ALU.add
                                            ).then_inc(y_read, 1)
                    dve.wait_ge(y_read, n)
                    for t in range(CT):
                        last = nc.vector.bn_stats(yst[c][:, t, :], y[c][:, t, :])
                    last.then_inc(y_stats, 1)
                    dve.wait_ge(y_stats, n)
                    nc.vector.tensor_tensor(ymv[c][:, :, :], yst[c][:, :, 1:3], yst[c][:, :, 4:6], ALU.add
                                            ).then_inc(y_parts, 1)
                    nc.vector.tensor_tensor(yd[c][:, :], yst[c][:, :, 1], yst[c][:, :, 4], ALU.subtract
                                            ).then_inc(y_parts, 1)
                    dve.wait_ge(y_parts, 4 * n - 2)
                    nc.vector.tensor_scalar(ymean[c][:, :], ymv[c][:, :, 0], 0.5, None, ALU.mult
                                            ).then_inc(y_parts, 1)
                    nc.vector.scalar_tensor_tensor(out=yd[c][:, :], in0=yd[c][:, :], scalar=P / 4.0,
                                                   in1=yd[c][:, :], op0=ALU.mult, op1=ALU.mult
                                                   ).then_inc(y_parts, 1)
                    dve.wait_ge(y_parts, 4 * n)
                    nc.vector.tensor_tensor(yd[c][:, :], yd[c][:, :], ymv[c][:, :, 1], ALU.add
                                            ).then_inc(y_var, 1)
                    dve.wait_ge(y_var, n)
                    nc.vector.tensor_scalar(yve[c][:, :], yd[c][:, :], 1.0 / P, MOE_EPS, ALU.mult, ALU.add
                                            ).then_inc(y_ve, 1)
                    for t in range(CT):
                        last = nc.vector.scalar_tensor_tensor(
                            out=u[c][:, t, :], in0=y[c][:, t, :], scalar=ymean[c][:, t:t + 1],
                            in1=gb2_in[b][:, 0, :], op0=ALU.subtract, op1=ALU.mult)
                    last.then_inc(u_done, 1)
                    if last_expert and c == 0:
                        continue
                    dve.wait_ge(u_done, n)
                    dve.wait_ge(y_a, n)
                    for t in range(CT):
                        at = acc[:, CT * c + t, :]
                        last = nc.vector.scalar_tensor_tensor(out=at, in0=u[c][:, t, :], scalar=ya[c][:, t:t + 1],
                                                              in1=at, op0=ALU.mult, op1=ALU.add)
                    last.then_inc(moe_acc, 1)

            cls_norm()
            expert(0, 0)
            cls_affine()
            dve.wait_ge(moe_acc, 2)
            for c in range(CHUNKS):
                dve.wait_ge(beta_ps, c + 1)
                nc.vector.tensor_tensor(acc[:, CT * c:CT * (c + 1), :], acc[:, CT * c:CT * (c + 1), :],
                                        ps[:, [7, 6][c], :].rearrange("p (t d) -> p t d", d=P), ALU.add
                                        ).then_inc(final_done, 1)
            dve.wait_ge(final_done, CHUNKS)
            expert(0, 1)
            dve.wait_ge(beta_ps, CHUNKS + 1)
            nc.vector.tensor_tensor(acc[0:1, CLS, :], acc[0:1, CLS, :], ps[0:1, 7, 0:P], ALU.add
                                    ).then_inc(final_done, 1)
            with dve.Fori(1, EXPERTS // 2 - 1) as it:
                for b in range(2):
                    expert(it, b)
            expert(EXPERTS // 2 - 1, 0)
            expert(EXPERTS // 2 - 1, 1, last_expert=True)

        @block.tensor
        def _(pe):
            mm = nc.tensor.matmul

            def project(c, k, done):
                for half in range(HALVES):
                    last = mm(ps[:, 2 * c + k, :], w_noisy[:, 2 * k + half, :], xT[:, c, half, :],
                              start=(half == 0), stop=(half == HALVES - 1))
                last.then_inc(done, 1)

            pe.wait_ge(zeros_set, 2)
            for n in range(WARM):
                mm(ps[:, 6, 0:P], zeros[:, :], zeros[:, :], start=True, stop=True)
            pe.wait_ge(w_done, 2)
            pe.wait_ge(patches_in[0], 16)
            project(0, 0, gate_ps)
            pe.wait_ge(w_done, 4)
            project(0, 1, inner_ps)
            pe.wait_ge(patches_in[1], 16)
            project(1, 0, gate_ps)
            pe.wait_ge(body_in, 16)
            pe.wait_ge(xn_done, 1)
            nc.tensor.transpose(ps[:, 7, 0:1], xn[0:1, CLS, :], ident[0:1, 0:1]).then_inc(xnT_ps, 1)
            pe.wait_ge(xnT_done, 1)
            mm(ps[:, 7, 1:2], bd("wk"), xnT_cls, start=True, stop=True)
            mm(ps[:, 7, 2:3], bd("wv"), xnT_cls, start=True, stop=True).then_inc(cls_ps, 1)
            project(1, 1, inner_ps)
            pe.wait_ge(cls_done, 2)
            mm(ps[0:1, 7, P:2 * P], v_cls_b[:, 0:1], bd("wout"), start=True, stop=True).then_inc(proj_ps, 1)

            def embed(c):
                pe.wait_ge(gT_done, 2 * (c + 1))
                for t in range(CT * c, CT * (c + 1)):
                    last = mm(ps[:, 4 + c, (t % CT) * P:(t % CT + 1) * P], gT[:, t * P:(t + 1) * P], bd("w3T"),
                              start=True, stop=True)
                last.then_inc(h_ps, 1)

            def cls_column():
                pe.wait_ge(x2_done, 1)
                nc.tensor.transpose(ps[:, 7, 3:4], x2[0:1, CLS, :], ident[0:1, 0:1]).then_inc(x2T_ps, 1)

            def cls_units(e0, e1):
                pe.wait_ge(x2T_each_done, 1)
                pe.wait_ge(w1_loaded, 16)
                for e in range(e0, e1):
                    last = mm(ps[0:EXPERTS, 7, :], x2T_each[:, e, :], w1_all[:, e, 0:HIDDEN],
                              start=(e == 0), stop=(e == EXPERTS - 1))
                if e1 == EXPERTS:
                    last.then_inc(cls_units_ps, 1)

            def cls_turn_units():
                pe.wait_ge(cls_units_done, 1)
                for f in range(FT):
                    last = nc.tensor.transpose(ps[:, 7, f * EXPERTS:(f + 1) * EXPERTS],
                                               cls_units_sb[:, f * P:(f + 1) * P], ident[0:EXPERTS, 0:EXPERTS])
                last.then_inc(cls_hid_ps, 1)

            def cls_outputs(e0, e1):
                pe.wait_ge(cls_hid_each_done, 1)
                pe.wait_ge(w2_loaded, 16)
                for e in range(e0, e1):
                    for f in range(FT):
                        mm(ps[E0:E1, 7, 0:P], cls_hid_each[:, f, e, :], w2_all[:, e, f, :],
                           start=(e == 0 and f == 0), stop=False)
                if e1 == EXPERTS:
                    mm(ps[E0:E1, 7, 0:P], ones_row[:, :], x2[0:1, CLS, :], start=False, stop=True
                       ).then_inc(cls_y_ps, 1)

            def turn_norm(c):
                for t in range(CT * c, CT * (c + 1)):
                    pe.wait_ge(xn_done, t + 2)
                    last = nc.tensor.transpose(ps[:, 6, (t % CT) * P:(t % CT + 1) * P], xn[:, t, :], ident)
                last.then_inc(xnT_ps, 1)

            def q_and_k(c):
                pe.wait_ge(xnT_done, c + 2)
                pe.wait_ge(gate_read, 2)
                pe.wait_ge(h_done, c + 1)
                cols = xnT[:, 8 * c:8 * (c + 1), 0:PATCHES]
                mm(ps[:, [2, 6][c], :], bd("wq"), cols, start=True, stop=True).then_inc(q_ps, 1)
                mm(ps[:, 4 + c, :], bd("wk"), cols, start=True, stop=True).then_inc(k_ps, 1)

            def scores(g):
                pe.wait_ge(q_done, 2 * (g // 2 + 1))
                pe.wait_ge(k_done, g // 2 + 1)
                if g > 0:
                    pe.wait_ge(S_masked, g)
                for i in range(GI):
                    n = GI * g + i
                    for h_ in range(HP):
                        rows = slice(32 * h_, 32 * (h_ + 1))
                        last = mm(ps[:, h_, i * KEYS:(i + 1) * KEYS], qTm[rows, n, :, :], kT[rows, n, :],
                                  start=True, stop=True)
                last.then_inc(scores_ps, 1)

            def values(g):
                pe.wait_ge(*[(k_done, 1), (k_done, 2), (q_done, 4), (v_done, 1)][g])
                for i in range(GI):
                    last = mm(ps[0:KEYS, V_BANK[g], i * P:(i + 1) * P], xnT[:, GI * g + i, :], bd("wv"),
                              start=True, stop=True)
                last.then_inc(v_ps, 1)

            def turn(n):
                g, i = n // GI, n % GI
                if i == 0:
                    pe.wait_ge(attn_done, g + 1)
                if n >= 2:
                    pe.wait_ge(attnT_done, n - 1)
                for h_ in range(HP):
                    last = nc.tensor.transpose(ps[0:KEYS, 4 + n % 2, h_ * P:(h_ + 1) * P], S[:, g, h_, i, :], ident)
                last.then_inc(attnT_ps, 1)

            def weigh(n):
                g, i = n // GI, n % GI
                pe.wait_ge(attnT_done, n + 1)
                if i == 0 and g >= 2:
                    pe.wait_ge(o_done, g - 1)
                for h_ in range(HP):
                    last = mm(ps[32 * h_:32 * (h_ + 1), 6 + g % 2, i * P:(i + 1) * P],
                              v[:, n, 32 * h_:32 * (h_ + 1)], attnT[0:KEYS, n % 8, h_ * P:(h_ + 1) * P],
                              start=True, stop=True)
                if i == GI - 1:
                    last.then_inc(o_ps, 1)

            def weigh_group(g):
                for n in range(GI * g, GI * (g + 1)):
                    turn(n)
                    if n >= 1:
                        weigh(n - 1)

            embed(0)
            cls_column()
            cls_units(0, 2)
            turn_norm(0)
            q_and_k(0)
            embed(1)
            scores(0)
            cls_units(2, 3)
            turn_norm(1)
            q_and_k(1)
            scores(1)
            values(0)
            values(1)
            scores(2)
            values(2)
            values(3)
            cls_units(3, 8)
            pe.wait_ge(v_done, GROUPS)
            scores(3)
            weigh_group(0)
            cls_turn_units()
            pe.wait_ge(cls_hid_done, 1)
            weigh_group(1)
            weigh_group(2)

            def output(c):
                pe.wait_ge(o_done, 2 * (c + 1))
                pe.wait_ge(S_masked, GROUPS)
                for t in range(CT * c, CT * (c + 1)):
                    for a in range(2):
                        last = mm(ps[:, c, (t % CT) * P:(t % CT + 1) * P],
                                  oT[:, a, 2 * t:2 * t + 2, :].rearrange("p i r -> p (i r)"),
                                  wout_par[:, a, :], start=(a == 0), stop=(a == 1))
                last.then_inc(proj_ps, 1)

            def turn_norm2(c):
                for t in range(CT * c, CT * (c + 1)):
                    pe.wait_ge(x2_done, t + 2)
                    last = nc.tensor.transpose(ps[:, [2, 5][c], (t % CT) * P:(t % CT + 1) * P], x2[:, t, :], ident)
                last.then_inc(x2T_ps, 1)

            def route(c):
                pe.wait_ge(x2T_done, c + 1)
                for t in range(CT * c, CT * (c + 1)):
                    mm(ps[:, 6, t * EXPERTS:(t + 1) * EXPERTS], x2T[:, t * P:(t + 1) * P], bd("router"),
                       start=True, stop=True)

            output(0)
            weigh_group(3)
            weigh(IMAGES - 1)

            def first_product(it, b, c, early=False):
                e = 2 * it + b
                cols = slice(c * BANK, (c + 1) * BANK)
                for f in range(FT):
                    w = slice(f * P, (f + 1) * P)
                    if c > 0 or early:
                        pe.wait_ge(hid_done, (2 * e + c - 1) * FT + f + 1)
                    mm(ps[:, f, :], w1_hi[b][:, w], x2T_lo[:, cols], start=True, stop=False)
                    mm(ps[:, f, :], w1_lo[b][:, w], x2T_hi[:, cols], start=False, stop=False)
                    mm(ps[:, f, :], w1_hi[b][:, w], x2T_hi[:, cols], start=False, stop=True).then_inc(hid_ps, 1)

            def second_product(it, b, c, first=False, tiles=range(CT)):
                e = 2 * it + b
                pe.wait_ge(hid_done, (2 * e + c + 1) * FT)
                if not first:
                    pe.wait_ge(y_read, 2 * e + c - 1)
                for t in tiles:
                    for f in range(FT):
                        last = mm(ps[:, 4 + c, t * P:(t + 1) * P], hid[c][:, f, t * P:(t + 1) * P],
                                  w2_all[:, bass.ds(e, 1), f, :].rearrange("p a n -> p (a n)"),
                                  start=(f == 0), stop=(f == FT - 1))
                if tiles[-1] == CT - 1:
                    last.then_inc(y_ps, 1)

            def expert(it, b):
                pe.wait_ge(w1_lo_done, 2 * it + b + 1)
                for c in range(CHUNKS):
                    first_product(it, b, c)
                for c in range(CHUNKS):
                    second_product(it, b, c)

            turn_norm2(0)
            output(1)
            route(0)
            cls_outputs(0, EXPERTS)
            pe.wait_ge(w1_lo_done, 1)
            pe.wait_ge(x2T_lo_done, 1)
            pe.wait_ge(acc_done, CHUNKS + 1)
            first_product(0, 0, 0)
            turn_norm2(1)
            second_product(0, 0, 0, first=True, tiles=range(0, 2))
            route(1)
            mm(ps[0:1, 6, TILES * EXPERTS:(TILES + 1) * EXPERTS], x2T_cls[:, :], bd("router"),
               start=True, stop=True).then_inc(logits_ps, 1)

            def turn_gates():
                pe.wait_ge(gates_done, 1)
                nc.tensor.transpose(ps[0:E1, 6, 0:P], gate[:, :, :].rearrange("p t e -> p (t e)"), ident
                                    ).then_inc(gateT_ps, 1)

            second_product(0, 0, 0, first=True, tiles=range(2, CT))
            pe.wait_ge(x2T_lo_done, 2)
            first_product(0, 0, 1)
            turn_gates()
            pe.wait_ge(w1_lo_done, 2)
            first_product(0, 1, 0, early=True)
            pe.wait_ge(x2T_done, 2)
            second_product(0, 0, 1, first=True)
            pe.wait_ge(gateT_done, 1)
            pe.wait_ge(beta_sel_done, 1)
            pe.wait_ge(cls_row_done, 1)
            for c in range(CHUNKS):
                mm(ps[:, [7, 6][c], :], gateT[0:E0, :], beta_sel[0:E0, CT * c:CT * (c + 1), :].rearrange("p t d -> p (t d)"),
                   start=True, stop=True).then_inc(beta_ps, 1)
            first_product(0, 1, 1)
            for c in range(CHUNKS):
                second_product(0, 1, c)
            pe.wait_ge(final_done, 1)
            pe.wait_ge(cls_row_done, 6)
            mm(ps[0:1, 7, 0:P], gateT[E0:E1, 0:1], cls_rows[E0:E1, :], start=True, stop=True).then_inc(beta_ps, 1)
            with pe.Fori(1, EXPERTS // 2) as it:
                for b in range(2):
                    expert(it, b)


def constants():
    pos = np.arange(PATCHES, dtype=np.float32)[:, None]
    div = np.exp(np.arange(0, P, 2, dtype=np.float32) * np.float32(-np.log(10000.0) / P))
    ang = pos * div
    pe = np.stack([np.sin(ang), np.cos(ang)], axis=-1).reshape(PATCHES, P).astype(np.float32)
    row = np.arange(P) % PATCHES
    mask = np.concatenate([np.arange(PATCHES)[None, :] <= row[:, None], np.ones((P, 1), bool)], 1)
    par = (np.arange(P)[:, None] // HD % 2) == np.arange(2)[None, :]
    sel = (np.arange(P)[:, None] // EXPERTS) == np.arange(TILES + 1)[None, :]
    f = np.float32
    return {"sel": sel.astype(f), "eye": np.tile(np.eye(EXPERTS, dtype=f).reshape(1, -1), (P, 1)), "pos": np.tile(pe, (2, 1)), "ident": np.eye(P, dtype=f), "mask": mask.astype(f),
            "inv_n": (1.0 / (row + 2.0))[:, None].astype(f), "par_scaled": (par * float(P) ** -0.5).astype(f),
            "par": par.astype(f), "iota": np.tile(np.arange(EXPERTS, dtype=f), (P, 1))}


def pack(spec, parts):
    cols = []
    for name, width in spec:
        a = parts[name]
        assert a.shape[1] == width and a.dtype == np.float32, name
        cols.append(np.concatenate([a, np.zeros((P - a.shape[0], width), np.float32)], 0))
    return np.ascontiguousarray(np.concatenate(cols, 1))


def kernel(**inputs):
    import concourse.bacc as bacc
    from concourse.bass_utils import run_bass_kernel_spmd

    a = {k: np.asarray(v) for k, v in inputs.items()}

    def rows(vec):
        return np.broadcast_to(vec.reshape(1, -1), (P, vec.size))

    def by_feature(m):
        return m.T.reshape(HALVES, P, P).transpose(1, 0, 2).reshape(P, HALVES * P)

    t = {k[7:]: v for k, v in a.items() if k.startswith("L0_tok_")}
    noise = pack(NOISE_COLS, {
        "w": np.concatenate([by_feature(t["W1_w"]), by_feature(t["W2_w"])], 1),
        "sw": np.concatenate([by_feature(t["W1_sw"]), by_feature(t["W2_sw"])], 1),
        "ei": np.concatenate([t["eps_in1"].reshape(HALVES, P).T, t["eps_in2"].reshape(HALVES, P).T], 1),
        "eo_row": np.concatenate([rows(t["eps_out1"]), rows(t["eps_out2"])], 1),
        "eo_col": np.stack([t["eps_out1"], t["eps_out2"]], 1),
        "b": np.stack([t["W1_b"], t["W2_b"]], 1),
        "sb": np.stack([t["W1_sb"], t["W2_sb"]], 1)})
    norm_g, norm_b = a["L0_attn_norm_g"].reshape(HEADS), a["L0_attn_norm_b"].reshape(HEADS)

    def head_table(vec):
        return np.repeat(vec.reshape(HP, 2).T, PATCHES, axis=0)

    body = pack(BODY_COLS, dict(
        constants(), w3T=t["W3_w"].T, b3=rows(t["W3_b"]), cls=a["cls_tok"].reshape(1, P),
        wq=a["L0_attn_w_qkv"][:, 0:P], wk=a["L0_attn_w_qkv"][:, P:2 * P], wv=a["L0_attn_w_qkv"][:, 2 * P:3 * P],
        wout=a["L0_attn_w_out"], bout=rows(a["L0_attn_b_out"]), 
        beta_rep=np.tile(a["L0_ffn_beta"], (TILES + 1, 1)), gamma_rows=np.tile(a["L0_ffn_gamma"], (TILES + 1, 1)),
        b2_rows=np.tile(a["L0_ffn_b2"], (TILES + 1, 1)),
        router=a["L0_ffn_router_w"], g_tab=head_table(norm_g), b_tab=head_table(norm_b),
        b_col=np.repeat(norm_b, HD)[:, None]))
    px = a["x"].reshape(IMAGES, GRID, HALVES, PATCH // HALVES, GRID, PATCH)
    px = px.transpose(3, 5, 2, 0, 1, 4).reshape(P, HALVES, CHUNKS, BANK).transpose(0, 2, 1, 3)
    w1b1 = np.concatenate([a["L0_ffn_w1"], a["L0_ffn_b1"].reshape(EXPERTS, FT, P).transpose(0, 2, 1)], 2)
    w1b1 = w1b1.transpose(1, 0, 2)
    arrays = {
        "patches": px, "noise": noise, "body": body, "b1": a["L0_ffn_b1"], "w1b1": w1b1,
        "w2": a["L0_ffn_w2"].reshape(EXPERTS, FT, P, P).transpose(2, 0, 1, 3),
        "gb2": np.stack([a["L0_ffn_gamma"], a["L0_ffn_b2"]], 1)}
    arrays = {k: np.ascontiguousarray(v) for k, v in arrays.items()}

    nc = bacc.Bacc("TRN2", target_bir_lowering=False, num_devices=1)
    args = [nc.dram_tensor(k, v.shape, mybir.dt.from_np(v.dtype), kind="ExternalInput").ap()
            for k, v in arrays.items()]
    out = nc.dram_tensor("out", (IMAGES, KEYS, P), F32, kind="ExternalOutput").ap()
    vit_tower(nc, *args, out)
    r = run_bass_kernel_spmd(nc, [arrays], core_ids=[0])
    return r.results[0]["out"]
```
